# Optimizing a Trainium2 kernel written in Bass

```python
import numpy as np
import jax
import jax.numpy as jnp

def _softmax(x, axis=-1):
    return jax.nn.softmax(x, axis=axis)

def _gelu(x):
    return jax.nn.gelu(x, approximate=True)

def _silu(x):
    return jax.nn.silu(x)

def _sigmoid(x):
    return jax.nn.sigmoid(x)

def _layernorm(x, axis=-1, eps=1e-05):
    m = jnp.mean(x, axis=axis, keepdims=True)
    v = jnp.var(x, axis=axis, keepdims=True)
    return (x - m) / jnp.sqrt(v + eps)

def _scatter_add(tgt, idx, src, axis=0):
    return tgt.at[idx].add(src)

def _segment_sum(src, seg, n):
    return jax.ops.segment_sum(src, seg, n)
kernel_name = 'mk_decoder_postln_d2_seqx_r4_4b9cbd'

def setup_inputs(seed: int=0):
    np.random.seed(seed)
    _w = jnp.asarray

    def _rec_inputs():
        import jax
        import jax.numpy as jnp
        _rk = jax.random.key(seed)
        x = 7.22e-05 + 1 * jax.random.normal(jax.random.fold_in(_rk, 1), (8, 256, 256), jnp.float32)
        _lenS = 256 - jax.random.randint(jax.random.fold_in(_rk, 7), (8,), 0, max(1, 256 // 4) + 1, jnp.int32)
        _lenS2 = 77 - jax.random.randint(jax.random.fold_in(_rk, 8), (8,), 0, max(1, 77 // 4) + 1, jnp.int32)
        _ctx_768P = jax.random.normal(jax.random.fold_in(_rk, 11), (8, 16, 192), jnp.float32)
        _ctx_768c = jax.random.dirichlet(jax.random.fold_in(_rk, 511), 0.3 * jnp.ones((16,), jnp.float32), (8, 77))
        _ctx_768t = jnp.einsum('bsk,bkd->bsd', _ctx_768c, _ctx_768P)
        _ctx_768t = _ctx_768t * jax.lax.rsqrt(jnp.mean(jnp.square(_ctx_768t)) + 1e-12) * 0.953939
        ctx_768 = -0.000191848 + 0.999787 * (_ctx_768t + 0.3 * jax.random.normal(jax.random.fold_in(_rk, 611), (8, 77, 192), jnp.float32))
        return (x, ctx_768)
    x, ctx_768 = _rec_inputs()

    def _L0_attn_setup():
        import jax, jax.numpy as jnp
        import numpy as np
        D_MODEL = 256
        N_HEADS = 4
        KEY_DIM = 256
        VALUE_DIM = 512
        DK = KEY_DIM // N_HEADS
        DV = VALUE_DIM // N_HEADS
        LOW_RANK = 16
        GATE_NORM = 16.0
        EPS = 1e-05

        def _gla_scan(q, k, v, gk):
            B, H, L, dk = q.shape
            dv = v.shape[-1]
            qs = jnp.moveaxis(q, 2, 0)
            ks_ = jnp.moveaxis(k, 2, 0)
            vs = jnp.moveaxis(v, 2, 0)
            gs = jnp.moveaxis(gk, 2, 0)

            def step(S, inp):
                q_t, k_t, v_t, g_t = inp
                S = S * jnp.exp(g_t)[..., None] + k_t[..., None] * v_t[..., None, :]
                o_t = jnp.einsum('bhk,bhkv->bhv', q_t, S)
                return (S, o_t)
            S0 = jnp.zeros((B, H, dk, dv), q.dtype)
            _, os = jax.lax.scan(step, S0, (qs, ks_, vs, gs))
            return jnp.moveaxis(os, 0, 2)
        key = jax.random.key(seed)
        ks = jax.random.split(key, 10)
        B, L = (2, 512)
        gain = 2.0 ** (-2.5)

        def xavier(k, shape, g=gain):
            fan_in, fan_out = (shape[0], shape[1])
            a = g * np.sqrt(6.0 / (fan_in + fan_out))
            return jax.random.uniform(k, shape, jnp.float32, -a, a)
        return {'x': jax.random.normal(ks[0], (B, L, D_MODEL), jnp.float32), 'Wq': xavier(ks[1], (D_MODEL, KEY_DIM)), 'Wk': xavier(ks[2], (D_MODEL, KEY_DIM)), 'Wv': xavier(ks[3], (D_MODEL, VALUE_DIM)), 'Wg': xavier(ks[4], (D_MODEL, VALUE_DIM)), 'gk_w1': xavier(ks[5], (D_MODEL, LOW_RANK)), 'gk_w2': xavier(ks[6], (LOW_RANK, KEY_DIM)), 'gk_b2': jnp.zeros((KEY_DIM,), jnp.float32), 'g_norm_w': jnp.ones((DV,), jnp.float32), 'Wo': xavier(ks[7], (VALUE_DIM, D_MODEL))}
    _L0_attn_all = _L0_attn_setup()
    _L0_attn_in = {k: v for k, v in _L0_attn_all.items() if k in ('Wq', 'Wk', 'Wv', 'Wg', 'gk_w1', 'gk_w2', 'gk_b2', 'g_norm_w', 'Wo')}
    del _L0_attn_all

    def _L0_xattn_setup():
        import jax, jax.numpy as jnp
        import numpy as np
        N_HEADS = 16
        key = jax.random.key(seed)
        ks = jax.random.split(key, 8)
        b, l, m = (8, 256, 256)
        d_embed, d_cross = (256, 192)
        s_q = 1.0 / np.sqrt(d_embed)
        s_kv = 1.0 / np.sqrt(d_cross)
        return {'x': jax.random.normal(ks[0], (b, l, d_embed), jnp.float32), 'y': jax.random.normal(ks[1], (b, m, d_cross), jnp.float32), 'Wq': jax.random.normal(ks[2], (d_embed, d_embed), jnp.float32) * s_q, 'bq': jax.random.normal(ks[3], (d_embed,), jnp.float32) * 0.01, 'Wkv': jax.random.normal(ks[4], (2 * d_embed, d_cross), jnp.float32) * s_kv, 'bkv': jax.random.normal(ks[5], (2 * d_embed,), jnp.float32) * 0.01, 'Wo': jax.random.normal(ks[6], (d_embed, d_embed), jnp.float32) * s_q, 'bo': jax.random.normal(ks[7], (d_embed,), jnp.float32) * 0.01}
    _L0_xattn_all = _L0_xattn_setup()
    _L0_xattn_in = {k: v for k, v in _L0_xattn_all.items() if k in ('Wq', 'bq', 'Wkv', 'bkv', 'Wo', 'bo')}
    del _L0_xattn_all

    def _L0_ffn_setup():
        import jax, jax.numpy as jnp
        import numpy as np
        E = 8
        TOP_K = 2
        D = 256
        H = 2 * D
        key = jax.random.key(seed)
        k0, k1, k2, k3, k4 = jax.random.split(key, 5)
        scale = 0.02
        x = jax.random.normal(k0, (4, 512, D), dtype=jnp.float32)
        Wg = jax.random.normal(k1, (D, E), dtype=jnp.float32) * scale
        W1 = jax.random.normal(k2, (E, D, H), dtype=jnp.float32) * scale
        W2 = jax.random.normal(k3, (E, D, H), dtype=jnp.float32) * scale
        W3 = jax.random.normal(k4, (E, H, D), dtype=jnp.float32) * scale
        return {'x': x, 'Wg': Wg, 'W1': W1, 'W2': W2, 'W3': W3}
    _L0_ffn_all = _L0_ffn_setup()
    _L0_ffn_in = {k: v for k, v in _L0_ffn_all.items() if k in ('Wg', 'W1', 'W2', 'W3')}
    del _L0_ffn_all

    def _L1_attn_setup():
        import jax, jax.numpy as jnp
        import numpy as np
        EMBED_DIM = 256
        NUM_HEADS = 16
        HEAD_DIM = EMBED_DIM // NUM_HEADS
        WINDOW = 128
        key = jax.random.key(seed)
        ks = jax.random.split(key, 9)
        B, S, E = (4, 1024, EMBED_DIM)
        s = 1.0 / np.sqrt(E)
        return {'x': jax.random.normal(ks[0], (B, S, E), jnp.float32), 'Wq': jax.random.normal(ks[1], (E, E), jnp.float32) * s, 'bq': jnp.zeros((E,), jnp.float32), 'Wk': jax.random.normal(ks[2], (E, E), jnp.float32) * s, 'bk': jnp.zeros((E,), jnp.float32), 'Wv': jax.random.normal(ks[3], (E, E), jnp.float32) * s, 'bv': jnp.zeros((E,), jnp.float32), 'Wo': jax.random.normal(ks[4], (E, E), jnp.float32) * s, 'bo': jnp.zeros((E,), jnp.float32)}
    _L1_attn_all = _L1_attn_setup()
    _L1_attn_in = {k: v for k, v in _L1_attn_all.items() if k in ('Wq', 'bq', 'Wk', 'bk', 'Wv', 'bv', 'Wo', 'bo')}
    del _L1_attn_all

    def _L1_xattn_setup():
        import jax, jax.numpy as jnp
        import numpy as np
        NUM_HEADS = 16
        CLAMP = 10000.0
        key = jax.random.key(seed)
        ks = jax.random.split(key, 8)
        B, Nq, Nkv, Cq, Ckv = (4, 512, 512, 256, 192)
        s_q = 1.0 / np.sqrt(Cq)
        s_kv = 1.0 / np.sqrt(Ckv)
        return {'query': jax.random.normal(ks[0], (B, Nq, Cq), jnp.float32), 'key_value': jax.random.normal(ks[1], (B, Nkv, Ckv), jnp.float32), 'Wq': jax.random.normal(ks[2], (Cq, Cq), jnp.float32) * s_q, 'bq': jnp.zeros((Cq,), jnp.float32), 'Wk': jax.random.normal(ks[3], (Ckv, Cq), jnp.float32) * s_kv, 'bk': jnp.zeros((Cq,), jnp.float32), 'Wv': jax.random.normal(ks[4], (Ckv, Cq), jnp.float32) * s_kv, 'bv': jnp.zeros((Cq,), jnp.float32), 'Wo': jax.random.normal(ks[5], (Cq, Cq), jnp.float32) * s_q, 'bo': jnp.zeros((Cq,), jnp.float32)}
    _L1_xattn_all = _L1_xattn_setup()
    _L1_xattn_in = {k: v for k, v in _L1_xattn_all.items() if k in ('Wq', 'bq', 'Wk', 'bk', 'Wv', 'bv', 'Wo', 'bo')}
    del _L1_xattn_all

    def _L1_ffn_setup():
        import jax, jax.numpy as jnp
        import numpy as np
        CAPACITY_FACTOR = 1.25
        key = jax.random.key(seed)
        ks = jax.random.split(key, 6)
        B, S, H, E = (4, 1024, 256, 8)
        scale = 1.0 / np.sqrt(H)
        return {'tokens': jax.random.normal(ks[0], (B, S, H), dtype=jnp.float32), 'gate_w': jax.random.normal(ks[1], (E, H), dtype=jnp.float32) * scale, 'w1': jax.random.normal(ks[2], (E, H, H), dtype=jnp.float32) * scale, 'b1': jax.random.normal(ks[3], (E, H), dtype=jnp.float32) * 0.01, 'w2': jax.random.normal(ks[4], (E, H, H), dtype=jnp.float32) * scale, 'b2': jax.random.normal(ks[5], (E, H), dtype=jnp.float32) * 0.01}
    _L1_ffn_all = _L1_ffn_setup()
    _L1_ffn_in = {k: v for k, v in _L1_ffn_all.items() if k in ('gate_w', 'w1', 'b1', 'w2', 'b2')}
    del _L1_ffn_all
    return {'x': x, 'ctx_768': ctx_768, 'L0_attn_Wq': _L0_attn_in['Wq'], 'L0_attn_Wk': _L0_attn_in['Wk'], 'L0_attn_Wv': _L0_attn_in['Wv'], 'L0_attn_Wg': _L0_attn_in['Wg'], 'L0_attn_gk_w1': _L0_attn_in['gk_w1'], 'L0_attn_gk_w2': _L0_attn_in['gk_w2'], 'L0_attn_gk_b2': _L0_attn_in['gk_b2'], 'L0_attn_g_norm_w': _L0_attn_in['g_norm_w'], 'L0_attn_Wo': _L0_attn_in['Wo'], 'L0_xattn_Wq': _L0_xattn_in['Wq'], 'L0_xattn_bq': _L0_xattn_in['bq'], 'L0_xattn_Wkv': _L0_xattn_in['Wkv'], 'L0_xattn_bkv': _L0_xattn_in['bkv'], 'L0_xattn_Wo': _L0_xattn_in['Wo'], 'L0_xattn_bo': _L0_xattn_in['bo'], 'L0_ffn_Wg': _L0_ffn_in['Wg'], 'L0_ffn_W1': _L0_ffn_in['W1'], 'L0_ffn_W2': _L0_ffn_in['W2'], 'L0_ffn_W3': _L0_ffn_in['W3'], 'L1_attn_Wq': _L1_attn_in['Wq'], 'L1_attn_bq': _L1_attn_in['bq'], 'L1_attn_Wk': _L1_attn_in['Wk'], 'L1_attn_bk': _L1_attn_in['bk'], 'L1_attn_Wv': _L1_attn_in['Wv'], 'L1_attn_bv': _L1_attn_in['bv'], 'L1_attn_Wo': _L1_attn_in['Wo'], 'L1_attn_bo': _L1_attn_in['bo'], 'L1_xattn_Wq': _L1_xattn_in['Wq'], 'L1_xattn_bq': _L1_xattn_in['bq'], 'L1_xattn_Wk': _L1_xattn_in['Wk'], 'L1_xattn_bk': _L1_xattn_in['bk'], 'L1_xattn_Wv': _L1_xattn_in['Wv'], 'L1_xattn_bv': _L1_xattn_in['bv'], 'L1_xattn_Wo': _L1_xattn_in['Wo'], 'L1_xattn_bo': _L1_xattn_in['bo'], 'L1_ffn_gate_w': _L1_ffn_in['gate_w'], 'L1_ffn_w1': _L1_ffn_in['w1'], 'L1_ffn_b1': _L1_ffn_in['b1'], 'L1_ffn_w2': _L1_ffn_in['w2'], 'L1_ffn_b2': _L1_ffn_in['b2']}

def reference(x, ctx_768, L0_attn_Wq, L0_attn_Wk, L0_attn_Wv, L0_attn_Wg, L0_attn_gk_w1, L0_attn_gk_w2, L0_attn_gk_b2, L0_attn_g_norm_w, L0_attn_Wo, L0_xattn_Wq, L0_xattn_bq, L0_xattn_Wkv, L0_xattn_bkv, L0_xattn_Wo, L0_xattn_bo, L0_ffn_Wg, L0_ffn_W1, L0_ffn_W2, L0_ffn_W3, L1_attn_Wq, L1_attn_bq, L1_attn_Wk, L1_attn_bk, L1_attn_Wv, L1_attn_bv, L1_attn_Wo, L1_attn_bo, L1_xattn_Wq, L1_xattn_bq, L1_xattn_Wk, L1_xattn_bk, L1_xattn_Wv, L1_xattn_bv, L1_xattn_Wo, L1_xattn_bo, L1_ffn_gate_w, L1_ffn_w1, L1_ffn_b1, L1_ffn_w2, L1_ffn_b2):
    import jax
    import jax.numpy as jnp

    def _L0_attn_ref(x, Wq, Wk, Wv, Wg, gk_w1, gk_w2, gk_b2, g_norm_w, Wo):
        import jax, jax.numpy as jnp
        import numpy as np
        D_MODEL = 256
        N_HEADS = 4
        KEY_DIM = 256
        VALUE_DIM = 512
        DK = KEY_DIM // N_HEADS
        DV = VALUE_DIM // N_HEADS
        LOW_RANK = 16
        GATE_NORM = 16.0
        EPS = 1e-05

        def _gla_scan(q, k, v, gk):
            B, H, L, dk = q.shape
            dv = v.shape[-1]
            qs = jnp.moveaxis(q, 2, 0)
            ks_ = jnp.moveaxis(k, 2, 0)
            vs = jnp.moveaxis(v, 2, 0)
            gs = jnp.moveaxis(gk, 2, 0)

            def step(S, inp):
                q_t, k_t, v_t, g_t = inp
                S = S * jnp.exp(g_t)[..., None] + k_t[..., None] * v_t[..., None, :]
                o_t = jnp.einsum('bhk,bhkv->bhv', q_t, S)
                return (S, o_t)
            S0 = jnp.zeros((B, H, dk, dv), q.dtype)
            _, os = jax.lax.scan(step, S0, (qs, ks_, vs, gs))
            return jnp.moveaxis(os, 0, 2)
        B, L, _ = x.shape
        scale = DK ** (-0.5)

        def heads(t, d):
            return t.reshape(B, L, N_HEADS, d).transpose(0, 2, 1, 3)
        q = heads(x @ Wq, DK) * scale
        k = heads(x @ Wk, DK)
        v = heads(x @ Wv, DV)
        gk = heads(jax.nn.log_sigmoid(x @ gk_w1 @ gk_w2 + gk_b2) / GATE_NORM, DK)
        o = _gla_scan(q, k, v, gk)
        o = o.transpose(0, 2, 1, 3)
        g = (x @ Wg).reshape(B, L, N_HEADS, DV)
        rms = o * jax.lax.rsqrt(jnp.mean(o * o, axis=-1, keepdims=True) + EPS)
        o = rms * g_norm_w * (g * jax.nn.sigmoid(g))
        o = o.reshape(B, L, VALUE_DIM)
        return o @ Wo

    def _L0_xattn_ref(x, y, Wq, bq, Wkv, bkv, Wo, bo):
        import jax, jax.numpy as jnp
        import numpy as np
        N_HEADS = 16
        b, l, d = x.shape
        m = y.shape[1]
        h = N_HEADS
        dh = d // h
        q = (jnp.einsum('bld,ed->ble', x, Wq) + bq).reshape(b, l, h, dh)
        kv = (jnp.einsum('bmc,ec->bme', y, Wkv) + bkv).reshape(b, m, h, 2 * dh)
        k, v = (kv[..., :dh], kv[..., dh:])
        scale = 1.0 / jnp.sqrt(jnp.asarray(dh, x.dtype))
        att = jax.nn.softmax(jnp.einsum('blhd,bmhd->blmh', q, k) * scale, axis=2)
        out = jnp.einsum('blmh,bmhd->blhd', att, v).reshape(b, l, d)
        return jnp.einsum('bld,ed->ble', out, Wo) + bo

    def _L0_ffn_ref(x, Wg, W1, W2, W3):
        import jax, jax.numpy as jnp
        import numpy as np
        E = 8
        TOP_K = 2
        D = 256
        H = 2 * D
        logits = jnp.einsum('bsd,de->bse', x, Wg)
        top_vals, top_idx = jax.lax.top_k(logits, TOP_K)
        probs = jax.nn.softmax(top_vals, axis=-1)
        onehot = jax.nn.one_hot(top_idx, E, dtype=x.dtype)
        weights = jnp.einsum('bsk,bske->bse', probs, onehot)
        out = jnp.zeros_like(x)
        for e in range(E):
            u = jnp.einsum('bsd,dh->bsh', x, W1[e])
            v = jnp.einsum('bsd,dh->bsh', x, W2[e])
            h = u * jax.nn.sigmoid(u) * v
            y = jnp.einsum('bsh,hd->bsd', h, W3[e])
            out = out + y * weights[..., e][..., None]
        return out

    def _L1_attn_ref(x, Wq, bq, Wk, bk, Wv, bv, Wo, bo):
        import jax, jax.numpy as jnp
        import numpy as np
        EMBED_DIM = 256
        NUM_HEADS = 16
        HEAD_DIM = EMBED_DIM // NUM_HEADS
        WINDOW = 128
        B, S, E = x.shape
        H, D, W = (NUM_HEADS, HEAD_DIM, WINDOW)
        scale = jnp.sqrt(jnp.asarray(D, x.dtype))

        def heads(t):
            return t.reshape(B, S, H, D).transpose(0, 2, 1, 3)
        q = heads(x @ Wq + bq)
        k = heads(x @ Wk + bk)
        v = heads(x @ Wv + bv)
        offs = jnp.arange(-W, W + 1)
        idx = jnp.arange(S)[:, None] + offs[None, :]
        valid = (idx >= 0) & (idx < S)
        idxc = jnp.clip(idx, 0, S - 1)
        k_win = k[:, :, idxc, :]
        v_win = v[:, :, idxc, :]
        scores = jnp.einsum('bhsd,bhswd->bhsw', q, k_win) / scale
        scores = jnp.where(valid[None, None], scores, jnp.asarray(-jnp.inf, scores.dtype))
        attn = jax.nn.softmax(scores, axis=-1)
        out = jnp.einsum('bhsw,bhswd->bhsd', attn, v_win)
        out = out.transpose(0, 2, 1, 3).reshape(B, S, E)
        return out @ Wo + bo

    def _L1_xattn_ref(query, key_value, Wq, bq, Wk, bk, Wv, bv, Wo, bo):
        import jax, jax.numpy as jnp
        import numpy as np
        NUM_HEADS = 16
        CLAMP = 10000.0
        B, Nq, Cq = query.shape
        Nkv = key_value.shape[1]
        H = NUM_HEADS
        D = Cq // H
        scale = D ** (-0.5)
        q = (query @ Wq + bq).reshape(B, Nq, H, D).transpose(0, 2, 1, 3)
        k = (key_value @ Wk + bk).reshape(B, Nkv, H, D).transpose(0, 2, 1, 3)
        v = (key_value @ Wv + bv).reshape(B, Nkv, H, D).transpose(0, 2, 1, 3)
        attn = jnp.einsum('bhqd,bhkd->bhqk', q, k) * scale
        attn = jnp.clip(attn, -CLAMP, CLAMP)
        attn = jax.nn.softmax(attn, axis=-1)
        attn = jnp.where(jnp.any(jnp.isnan(attn)), jnp.asarray(1.0 / Nkv, attn.dtype), attn)
        x = jnp.einsum('bhqk,bhkd->bqhd', attn, v).reshape(B, Nq, Cq)
        return x @ Wo + bo

    def _L1_ffn_ref(tokens, gate_w, w1, b1, w2, b2):
        import jax, jax.numpy as jnp
        import numpy as np
        CAPACITY_FACTOR = 1.25
        B, S, H = tokens.shape
        E = gate_w.shape[0]
        N = B * S
        cap = int(CAPACITY_FACTOR * N / E)
        x = tokens.reshape(N, H)
        probs = jax.nn.softmax(x @ gate_w.T, axis=-1)
        top2_w, top2_idx = jax.lax.top_k(probs, 2)
        a_e = top2_idx.reshape(-1)
        a_w = top2_w.reshape(-1)
        tok_id = jnp.arange(2 * N) // 2
        counts = jnp.bincount(a_e, length=E)
        keep = counts <= cap
        valid = keep[a_e]
        onehot = jax.nn.one_hot(a_e, E, dtype=jnp.int32)
        pos = jnp.take_along_axis(jnp.cumsum(onehot, axis=0) - 1, a_e[:, None], axis=1)[:, 0]
        p = jnp.where(valid, jnp.minimum(pos, cap - 1), cap)
        x_a = x[tok_id]
        buf = jnp.zeros((E, cap + 1, H), dtype=x.dtype).at[a_e, p].set(x_a)
        h = jax.nn.silu(jnp.einsum('ech,efh->ecf', buf, w1) + b1[:, None, :])
        y = jnp.einsum('ecf,egf->ecg', h, w2) + b2[:, None, :]
        contrib = y[a_e, p] * (a_w * valid.astype(x.dtype))[:, None]
        out = contrib.reshape(N, 2, H).sum(axis=1)
        return out.reshape(B, S, H)
    x = _layernorm(x + _L0_attn_ref(x, L0_attn_Wq, L0_attn_Wk, L0_attn_Wv, L0_attn_Wg, L0_attn_gk_w1, L0_attn_gk_w2, L0_attn_gk_b2, L0_attn_g_norm_w, L0_attn_Wo), axis=-1)
    x = _layernorm(x + _L0_xattn_ref(x, ctx_768, L0_xattn_Wq, L0_xattn_bq, L0_xattn_Wkv, L0_xattn_bkv, L0_xattn_Wo, L0_xattn_bo), axis=-1)
    x = _layernorm(x + _L0_ffn_ref(x, L0_ffn_Wg, L0_ffn_W1, L0_ffn_W2, L0_ffn_W3), axis=-1)
    x = _layernorm(x + _L1_attn_ref(x, L1_attn_Wq, L1_attn_bq, L1_attn_Wk, L1_attn_bk, L1_attn_Wv, L1_attn_bv, L1_attn_Wo, L1_attn_bo), axis=-1)
    x = _layernorm(x + _L1_xattn_ref(x, ctx_768, L1_xattn_Wq, L1_xattn_bq, L1_xattn_Wk, L1_xattn_bk, L1_xattn_Wv, L1_xattn_bv, L1_xattn_Wo, L1_xattn_bo), axis=-1)
    x = _layernorm(x + _L1_ffn_ref(x, L1_ffn_gate_w, L1_ffn_w1, L1_ffn_b1, L1_ffn_w2, L1_ffn_b2), axis=-1)
    return x

_drawn_inputs = setup_inputs


def setup_inputs(seed=0):
    import zlib

    import numpy as np

    out = dict(_drawn_inputs(seed))
    spreads = {'L0_attn_gk_b2': (0.0, 0.8),
     'L0_attn_g_norm_w': (1.0, 0.6),
     'L1_attn_bq': (0.0, 0.8),
     'L1_attn_bk': (0.0, 2.0),
     'L1_attn_bv': (0.0, 0.1),
     'L1_attn_bo': (0.0, 0.1),
     'L1_xattn_bq': (0.0, 0.344),
     'L1_xattn_bk': (0.0, 2.0),
     'L1_xattn_bv': (0.0, 0.1),
     'L1_xattn_bo': (0.0, 0.1)}
    factors = {'L0_attn_Wq': 4.703,
     'L0_attn_Wk': 4.535,
     'L0_attn_Wv': 4.617,
     'L0_attn_Wg': 4.83,
     'L0_attn_gk_w1': 8.0,
     'L0_attn_gk_w2': 8.0,
     'L0_attn_Wo': 4.704,
     'L0_xattn_bq': 8.0,
     'L0_xattn_bkv': 5.553,
     'L0_xattn_bo': 5.208,
     'L0_ffn_Wg': 4.383,
     'L0_ffn_W1': 3.794,
     'L0_ffn_W2': 3.761,
     'L0_ffn_W3': 3.812,
     'L1_ffn_b1': 64.0,
     'L1_ffn_b2': 64.0}
    for name, (base, spread) in spreads.items():
        noise = np.random.default_rng([zlib.crc32(name.encode()), seed]).standard_normal(out[name].shape)
        drawn = base * np.exp(spread * noise) if base else spread * noise
        out[name] = jnp.asarray(drawn.astype(out[name].dtype))
    for name, factor in factors.items():
        out[name] = (out[name] * factor).astype(out[name].dtype)
    return out
```

```python
from contextlib import ExitStack

import numpy as np

import concourse.bass as bass
from concourse import mybir

F32 = mybir.dt.float32
BF16 = mybir.dt.bfloat16
ALU = mybir.AluOpType
ACT = mybir.ActivationFunctionType
AX = mybir.AxisListType

P = 128
B, L, D = 8, 256, 256
NT = L // P
KC = D // P
TILES = B * NT
PAIRS = B // 2
M, DC = 77, 192
GH, GDK, GDV = 4, 64, 128
VD = GH * GDV
VC = VD // P
LOWRANK = 16
GATE_NORM = 16.0
H, DH = 16, 16
HC = P // DH
QSCALE = DH ** -0.5
E, FH = 8, 512
MC = FH // P
BLK = 512
NBLK = B * L // BLK
TB = BLK // P
CAP = int(1.25 * B * L / E)
CLAMP = 10000.0
EPS = 1e-5
BIG = 1e30


class Attn:

    def __init__(self, name, prefix, before, selfattn, clip):
        self.name, self.selfattn, self.clip = name, selfattn, clip
        self.prefix, self.pairs_before = prefix, before
        self.keys = P if selfattn else M
        self.key_tiles = NT if selfattn else 1
        self.nk = self.keys * self.key_tiles
        self.bank_heads = 2 if selfattn else 4
        self.rounds = NT * H // (2 * self.bank_heads)
        self.unit_heads = 1 if selfattn else 2
        self.units = H // self.unit_heads


X0 = Attn("x0", "x", 0, False, False)
S1 = Attn("s1", "s", 0, True, False)
X1 = Attn("x1", "x", PAIRS, False, True)


def build_program(nc, dram, out):
    with ExitStack() as ctx:
        def sb(name, shape, dt=F32):
            return ctx.enter_context(nc.sbuf_tensor("sb_" + name, shape, dt))

        sems = {}

        def S(name):
            if name not in sems:
                sems[name] = ctx.enter_context(nc.semaphore(name))
            return sems[name]

        ident = sb("ident", [P, P])
        causal = sb("causal", [P, 3, P])
        rowmask = sb("rowmask", [P, HC])
        headrow = sb("headrow", [3 * H, H, P], BF16)
        identb = sb("identb", [P, P], BF16)
        winmask = sb("winmask", [P, 2, P], BF16)
        tiebreak = sb("tiebreak", [P, TILES, E])
        onemat = sb("onemat", [P, P])
        ones = sb("ones", [P, L])
        neghalf = sb("neghalf", [P, 8])
        eps = sb("eps", [P, 8])
        tick = sb("tick", [P, 1])
        r0, r1 = sb("r0", [P, KC, E]), sb("r1", [P, KC, E])
        f_b2 = sb("f_b2", [E, D])
        always = {"ident": ident, "causal": causal, "rowmask": rowmask, "headrow": headrow, "identb": identb,
                  "winmask": winmask, "tiebreak": tiebreak, "r0": r0, "r1": r1, "f_b2": f_b2}
        always = {n: t[:] for n, t in always.items()}

        xres = sb("xres", [P, TILES, D])
        xTres = sb("xTres", [P, KC, B * L])
        logits = sb("logits", [P, TILES, E])
        wts = sb("wts", [P, TILES, E])
        hot = sb("hot", [P, 2, TILES, E])
        rt = sb("rt", [P, TILES, E])
        top = sb("top", [P, 8, TILES])
        cnt = sb("cnt", [P, 2, E])
        wcol = sb("wcol", [P, 2, TILES])

        WREG = 7168
        wreg = sb("wreg", [P, WREG])

        def view(t, off, dims, rows=P):
            v = t[0:rows, off:off + int(np.prod(dims))]
            if len(dims) == 2:
                v = v.rearrange("p (a b) -> p a b", a=dims[0])
            if len(dims) == 3:
                v = v.rearrange("p (a b c) -> p a b c", a=dims[0], b=dims[1])
            return v

        def place(t, off, end, items):
            got = {}
            for name, dims in items:
                got[name] = view(t, off, dims)
                off += int(np.prod(dims))
            assert off <= end, (off, end)
            return got

        def attn_items(n):
            return [(f"{n}_{w}", (KC, D)) for w in ("wq", "wk", "wv", "wo")] + \
                   [(f"{n}_{w}", (KC,)) for w in ("bq", "bk")] + [(f"{n}_{w}", (D,)) for w in ("bv", "bo")]

        w0 = place(wreg, 0, WREG, [("a_wq", (KC, D)), ("a_wk", (KC, D)), ("a_wv", (KC, VD)), ("a_wg", (KC, VD)),
                                   ("a_w1", (KC, LOWRANK)), ("a_w2", (D,)), ("a_b2", (KC,)), ("a_gn", (GDV,)),
                                   ("a_wo", (VC, D))] + attn_items("x0"))
        w1 = place(wreg, 0, WREG, attn_items("s1") + attn_items("x1"))
        W = w0 | w1
        W["a_w2"] = W["a_w2"][0:LOWRANK, :]

        COMMON, REGION = 5248, 11520
        arena = sb("arena", [P, 2 * (COMMON + REGION)])
        bufs = []
        for p in range(2):
            o = p * (COMMON + REGION)
            b = place(arena, o, o + COMMON, [
                ("xT", (KC, L)), ("xtok", (NT, D)), ("ctxT", (2, M + 1)), ("xA", (NT, D)), ("xB", (NT, D)),
                ("xinT", (KC, L)), ("xb", (NT, D)), ("res", (NT, D)), ("xo", (NT, D)), ("xoT", (KC, L)),
                ("f", (KC,)), ("fx", (KC,)), ("ms", (8,)), ("rms", (8,)), ("st0", (6,)), ("st1", (6,)),
                ("mv", (NT, 2)), ("var", (NT,)), ("rstd", (NT,)), ("nm", (NT, H)), ("rec", (NT, H)),
                ("nmb", (NT * 3 * H // 2,)), ("nmr", (2 * NT * H,)), ("nmTf", (L // 2,))])
            o += COMMON
            b |= place(arena, o, o + REGION, [
                ("v", (NT, VD)), ("gw", (NT, VD)), ("th", (NT, VD)), ("zb", (KC, L)), ("la", (KC, L)),
                ("gl", (KC, L)), ("G", (KC, L)), ("qd", (KC, L)), ("kd", (KC, L)), ("qx", (KC, P)), ("g1", (L,)),
                ("AT", (GH * 3, P))])
            b |= place(arena, o + 3072, o + REGION, [("Eq", (KC, L)), ("Ek", (KC, L)), ("Dd", (KC, L))])
            b |= place(arena, o + 2048, o + REGION, [("sq", (NT, VD)), ("y", (NT, VD)), ("yT", (NT, VD))])
            b |= place(arena, o, o + REGION, [
                ("qs", (KC, L)), ("kT", (KC, L)), ("KB", (KC, HC, L)), ("va", (NT, H, 2 * DH)), ("PT", (4, BLK)),
                ("OT", (4, L)), ("on", (NT, D)), ("onT", (KC, L))])
            b["KBm"] = view(arena, o + 1024, (KC, HC, M))
            b["g1"] = b["g1"][0:LOWRANK, :]
            b["nmb"] = b["nmb"].bitcast(BF16).rearrange("p (t a h) -> p t a h", t=NT, a=3)
            b["nmr"] = b["nmr"].rearrange("p (a t h) -> p a t h", a=2, t=NT)
            b["nmT"] = b["nmTf"].bitcast(BF16)[0:3 * H, :]
            bufs.append(type("Bufs", (), b))
        stream0, stream1, hid, sil = [], [], [], []
        for p in range(2):
            o = p * 3072
            stream0.append(place(arena, o, o + 3072, [("w1", (KC, FH)), ("w2", (KC, FH)), ("w3", (MC, D))]))
            stream1.append(place(arena, o, o + 3072, [("w1", (KC, D)), ("w2", (KC, D)), ("b1", (KC,))]))
            hid.append(view(arena, 6144 + 2048 * p, (MC, BLK)))
            sil.append(view(arena, 10240 + 512 * p, (BLK,)))
        wT = view(arena, 11264, (TILES, P), E)
        bias_y = view(arena, 13312, (2, D))

        ps = ctx.enter_context(nc.psum_tensor("ps", [P, 8, 512], F32))

        def bank(p, n, k=1):
            return ps[:, 4 * p + n, :] if k == 1 else ps[:, 4 * p + n:4 * p + n + k, :]

        def halves(ap):
            return ap.rearrange("p (a b) -> p a b", a=2)

        def chunks128(ap):
            return ap.rearrange("p (a b) -> p a b", b=P)

        block = ctx.enter_context(nc.Block())

        def load_weight(eng, n, signal):
            src = dram[n]
            dst = W.get(n, always.get(n))
            if n[-2:] in ("bv", "bo") or n == "a_gn":
                src = src.broadcast_to([P, src.shape[1]])
            if n in ("x0_wk", "x0_wv", "x1_wk", "x1_wv"):
                eng.dma_start(dst[:, 0, :], src[0:P, :]).then_inc(S(signal), 16)
                eng.dma_start(dst[0:DC - P, 1, :], src[P:DC, :]).then_inc(S(signal), 16)
            else:
                eng.dma_start(dst, src).then_inc(S(signal), 16)

        x0_names = [n for n, _ in attn_items("x0")]
        x0_loads = 16 * (len(x0_names) + 2)
        c_loads = 16 * (2 * len(x0_names) + 2)

        @block.sync
        def _(sp):
            def loads(b1, p, first):
                bf = bufs[p]
                if first:
                    sp.dma_start(bf.xT, dram["xT"][b1, :, :, :].rearrange("a k p t -> (a p) k t")).then_inc(S(f"a_in{p}"), 16)
                    sp.dma_start(bf.xtok, dram["x"][b1, :, :, :].rearrange("a t p d -> (a p) t d")).then_inc(S(f"a_in{p}"), 16)
                name = f"a_in{p}" if first else f"c_in{p}"
                sp.dma_start(bf.ctxT[:, 0, 0:M], dram["ctxT"][b1, 0:P, :].rearrange("a c m -> (a c) m")).then_inc(S(name), 16)
                sp.dma_start(bf.ctxT[0:DC - P, 1, 0:M], dram["ctxT"][b1, P:DC, :].rearrange("a c m -> (a c) m")).then_inc(S(name), 16)

            for p in range(2):
                loads(bass.ds(p, 1), p, True)
            for n in ("a_wv", "a_wg", "a_wq", "a_wk", "a_w1"):
                sp.dma_start(W[n], dram[n]).then_inc(S("a_weights"), 16)
            with sp.Fori(1, PAIRS) as i:
                for p in range(2):
                    sp.wait_ge(S("x_out"), 2 * i + p - 1)
                    loads(bass.ds(2 * i + p, 1), p, True)
            sp.wait_ge(S("logits"), 2 + B)
            sp.wait_ge(S("store"), B)

            def experts0(e, p):
                for n in ("w1", "w2", "w3"):
                    sp.dma_start(stream0[p][n], dram["m0_" + n][e, :, :, :].rearrange("a k p h -> (a p) k h")).then_inc(S(f"b_w{p}"), 16)

            for p in range(2):
                experts0(bass.ds(p, 1), p)
            for n in [n for n, _ in attn_items("s1") + attn_items("x1")]:
                load_weight(sp, n, "c_weights")
            with sp.Fori(1, E // 2) as i:
                for p in range(2):
                    sp.wait_ge(S("b_y"), NBLK * (2 * i + p - 1))
                    experts0(bass.ds(2 * i + p, 1), p)
            sp.wait_ge(S("b_acc"), 2 + NBLK * E)
            for p in range(2):
                loads(bass.ds(p, 1), p, False)
            with sp.Fori(1, PAIRS) as i:
                for p in range(2):
                    sp.wait_ge(S("x_out"), B + 2 * i + p - 1)
                    loads(bass.ds(2 * i + p, 1), p, False)
            sp.wait_ge(S("logits"), 2 + 2 * B)
            sp.wait_ge(S("store"), 2 * B)

            def experts1(e, p):
                for n in ("w1", "w2", "b1"):
                    sp.dma_start(stream1[p][n], (dram["m1_" + n][e, :, :, :].rearrange("a k p h -> (a p) k h") if n != "b1"
                                 else dram["m1_b1"][e, :, :].rearrange("a p k -> (a p) k"))).then_inc(S(f"d_w{p}"), 16)

            for p in range(2):
                experts1(bass.ds(p, 1), p)
            with sp.Fori(1, E // 2) as i:
                for p in range(2):
                    sp.wait_ge(S("d_y"), NBLK * (2 * i + p - 1))
                    experts1(bass.ds(2 * i + p, 1), p)
            with sp.Fori(0, PAIRS) as i:
                for p in range(2):
                    sp.wait_ge(S("a_out"), 2 * B + 2 * i + p + 1)
                    sp.dma_start(out[bass.ds(2 * i + p, 1), :, :, :].rearrange("a t p d -> (a p) t d"),
                                 bufs[p].xo).then_inc(S(f"stored{p}"), 16)
            for p in range(2):
                sp.wait_ge(S(f"stored{p}"), 16 * PAIRS)

        @block.scalar
        def _(act):
            for n in always:
                load_weight(act, n, "const_in")
            for n in ("a_w2", "a_b2", "a_gn", "a_wo"):
                load_weight(act, n, "a_weights")
            for n in x0_names:
                load_weight(act, n, "x0_weights")
            nc.scalar.preload_act_table_set("natural_log_exp_and_others")

            def attn_stages(c, i):
                n, wn, i = c.prefix, c.name, i + c.pairs_before

                def xinT(p):
                    act.wait_ge(S(f"{n}_xT_done"), 2 * i + p + 1)
                    nc.scalar.activation(bufs[p].xinT, halves(bank(p, 1)), ACT.Copy).then_inc(S(f"{n}_xinT"), 1)

                def q(p):
                    act.wait_ge(S(f"{n}_q"), 2 * i + p + 1)
                    for k in range(KC):
                        ins = nc.scalar.activation(bufs[p].qs[:, k, :], bank(p, 2)[:, k * L:(k + 1) * L], ACT.Identity,
                                                   bias=W[f"{wn}_bq"][:, k:k + 1], scale=QSCALE)
                    ins.then_inc(S(f"{n}_qs"), 1)

                def shift(p):
                    act.wait_ge(S(f"{n}_nmT_done"), 2 * i + p + 1)
                    nc.scalar.activation(bufs[p].nmT, bank(p, 0)[0:3 * H, 0:L], ACT.Copy).then_inc(S(f"{n}_nmT"), 1)

                def probs(p):
                    for u in range(c.units):
                        act.wait_ge(S(f"{n}_ST"), c.units * (2 * i + p) + u + 1)
                        nc.scalar.activation(bufs[p].PT[0:c.keys, u % 4, :], bank(p, u % 2)[0:c.keys, :],
                                             ACT.Exp).then_inc(S(f"{n}_PT"), 1)

                def heads(p):
                    act.wait_ge(S(f"{n}_OT_done"), 2 * i + p + 1)
                    nc.scalar.activation(bufs[p].OT, bank(p, 2, 2), ACT.Copy).then_inc(S(f"{n}_OT"), 1)

                def onT(p):
                    act.wait_ge(S(f"{n}_onT_done"), 2 * i + p + 1)
                    nc.scalar.activation(bufs[p].onT, halves(bank(p, 2)), ACT.Copy).then_inc(S(f"{n}_onT"), 1)

                return [xinT, q, shift, probs, heads, onT]

            def outT(i):
                def stage(p):
                    act.wait_ge(S("xoT_done"), 2 * i + p + 1)
                    nc.scalar.activation(bufs[p].xoT, halves(bank(p, 2)), ACT.Copy).then_inc(S("xoT"), 1)
                return [stage]

            def gla_stages(i):
                def v(p):
                    act.wait_ge(S("a_v"), 2 * i + p + 1)
                    nc.scalar.activation(bufs[p].v, bank(p, 0, 2), ACT.Copy).then_inc(S("a_vs"), 1)

                def gate(p):
                    act.wait_ge(S("a_g"), 2 * i + p + 1)
                    nc.scalar.activation(bufs[p].th, bank(p, 2, 2), ACT.Tanh, scale=0.5).then_inc(S("a_th"), 1)

                def lowrank(p):
                    act.wait_ge(S("a_g1_done"), 2 * i + p + 1)
                    nc.scalar.activation(bufs[p].g1, bank(p, 2)[0:LOWRANK, 0:L], ACT.Copy).then_inc(S("a_g1"), 1)

                def softplus(p):
                    b = bufs[p]
                    act.wait_ge(S("a_zb"), 2 * i + p + 1)
                    nc.scalar.activation(b.la, b.zb, ACT.Abs).then_inc(S("a_log"), 1)
                    act.wait_ge(S("a_log"), 3 * (2 * i + p) + 1)
                    nc.scalar.activation(b.la, b.la, ACT.Exp, scale=-1.0).then_inc(S("a_log"), 1)
                    act.wait_ge(S("a_log"), 3 * (2 * i + p) + 2)
                    nc.scalar.activation(b.la, b.la, ACT.Ln, bias=ones[:, 0:1]).then_inc(S("a_log"), 1)

                def decay(p):
                    b = bufs[p]
                    act.wait_ge(S("a_Dd"), 2 * i + p + 1)
                    nc.scalar.activation(b.Eq, b.Dd, ACT.Exp, scale=1.0 / GATE_NORM)
                    nc.scalar.activation(b.Ek, b.Dd, ACT.Exp, scale=-1.0 / GATE_NORM)
                    nc.scalar.activation(b.fx, b.f, ACT.Exp, scale=1.0 / GATE_NORM).then_inc(S("a_decay"), 1)

                def square(p):
                    act.wait_ge(S("a_o"), 2 * i + p + 1)
                    nc.scalar.activation(bufs[p].sq, bank(p, 0, 2), ACT.Square, scale=GDV ** -0.5).then_inc(S("a_sq"), 1)

                def yT(p):
                    act.wait_ge(S("a_yT_done"), 2 * i + p + 1)
                    nc.scalar.activation(bufs[p].yT, bank(p, 2, 2), ACT.Copy).then_inc(S("a_yT"), 1)

                return [v, gate, lowrank, softplus, decay, square, yT]

            act.wait_ge(S("memsets"), 4)
            act.wait_ge(S("bq_scaled0"), 1)
            with act.Fori(0, PAIRS) as i:
                for stage in gla_stages(i) + attn_stages(X0, i) + outT(i):
                    for p in range(2):
                        stage(p)

            def router(nth):
                act.wait_ge(S("top2"), nth)
                nc.scalar.activation(top[:, 5, :], top[:, 4, :], ACT.Exp)
                nc.scalar.activation(rt[:, :, :], rt[:, :, :], ACT.Exp).then_inc(S("exp2"), 1)

            router(1)
            with act.Fori(0, E // 2) as i:
                for p in range(2):
                    for blk in range(NBLK):
                        for m in range(MC):
                            s = (p * NBLK + blk) * MC + m
                            act.wait_ge(S("b_uv"), 2 * NBLK * MC * i + s + 1)
                            nc.scalar.activation(sil[s % 2], ps[:, 2 * (s % 2), :], ACT.Silu).then_inc(S("b_sil"), 1)
            act.wait_ge(S("bq_scaled1"), 1)
            with act.Fori(0, PAIRS) as i:
                for stage in attn_stages(S1, i) + attn_stages(X1, i) + outT(i + PAIRS):
                    for p in range(2):
                        stage(p)
            router(2)
            for g in range(TILES // TB):
                act.wait_ge(S("d_wT_done"), g + 1)
                nc.scalar.activation(wT[:, g * TB:(g + 1) * TB, :], chunks128(ps[0:E, g % 2, :]), ACT.Copy).then_inc(S("d_wT"), 1)
            with act.Fori(0, E // 2) as i:
                for p in range(2):
                    for blk in range(NBLK):
                        for m in range(KC):
                            s = (p * NBLK + blk) * KC + m
                            if s % (NBLK * KC) == 0:
                                act.wait_ge(S(f"d_w{p}"), 48 * (i + 1))
                            act.wait_ge(S("d_u"), 2 * NBLK * KC * i + s + 1)
                            nc.scalar.activation(hid[blk % 2][:, m, :], ps[:, s % 4, :], ACT.Silu,
                                                 bias=stream1[p]["b1"][:, m:m + 1]).then_inc(S("d_h"), 1)

        @block.vector
        def _(dve):
            v = nc.vector
            v.memset(onemat[:, :], 1.0).then_inc(S("memsets"), 1)
            v.memset(neghalf[:, :], -0.5).then_inc(S("memsets"), 1)
            v.memset(eps[:, :], EPS).then_inc(S("memsets"), 1)
            v.memset(ones[:, :], 1.0).then_inc(S("memsets"), 1)
            v.memset(cnt[:, 0, 0:1], 0.0).then_inc(S("b_h"), 2)
            v.memset(cnt[:, 0, 1:2], 0.0).then_inc(S("b_acc"), 2)
            v.memset(cnt[:, 0, 2:3], 0.0).then_inc(S("d_acc"), 2)
            v.memset(cnt[:, 0, 3:4], 0.0).then_inc(S("logits"), 2)

            def scale_bias(names, signal):
                for k, n in enumerate(names):
                    ins = v.tensor_scalar(W[n], W[n], QSCALE, None, ALU.mult)
                ins.then_inc(S(signal), 1)

            dve.wait_ge(S("x0_weights"), x0_loads)
            scale_bias(["x0_bq"], "bq_scaled0")
            dve.wait_ge(S("a_weights"), 16 * 9)
            v.tensor_scalar(W["a_gn"], W["a_gn"], 0.5, None, ALU.mult).then_inc(S("gn_halved"), 1)
            dve.wait_ge(S("const_in"), 16 * len(always))

            def layernorm(n, p, i, src, dst):
                b = bufs[p]
                w = 2 * i + p + 1
                dve.wait_ge(S(f"{n}_res"), w)
                v.bn_stats(b.st0, src[:, 0, :])
                v.bn_stats(b.st1, src[:, 1, :]).then_inc(S(f"{n}_stats"), 1)
                dve.wait_ge(S(f"{n}_stats"), w)
                v.memset(tick[:, :], 0.0)
                v.bn_aggr(b.mv[:, 0, :], b.st0)
                v.bn_aggr(b.mv[:, 1, :], b.st1).then_inc(S(f"{n}_mv"), 1)

            def normalise(n, p, i, src, dst):
                b = bufs[p]
                dve.wait_ge(S(f"{n}_rstd"), 2 * i + p + 1)
                for t in range(NT):
                    ins = v.tensor_scalar(dst[:, t, :], src[:, t, :], b.mv[:, t, 0:1], b.rstd[:, t:t + 1],
                                          ALU.subtract, ALU.mult)
                ins.then_inc(S(f"{n}_out"), 1)

            def attn_stages(c, loop, xout):
                n, wn, i = c.prefix, c.name, loop + c.pairs_before

                def kv(p):
                    b, w = bufs[p], 2 * i + p + 1
                    dve.wait_ge(S(f"{n}_kv"), w)
                    kp = halves(bank(p, 3)) if c.selfattn else bank(p, 3)[:, 0:KC * M].rearrange("p (a b) -> p a b", a=KC)
                    for k in range(KC):
                        ins = v.tensor_scalar(b.kT[:, k, 0:c.nk], kp[:, k, :], W[f"{wn}_bk"][:, k:k + 1], None, ALU.add)
                    ins.then_inc(S(f"{n}_kT"), 1)
                    bv = W[f"{wn}_bv"].rearrange("p (h d) -> p h d", h=H)
                    for t in range(c.key_tiles):
                        vp = halves(bank(p, 0))[:, t, :] if c.selfattn else bank(p, 3)[:, D:2 * D]
                        v.tensor_tensor(b.va[0:c.keys, t, :, 0:DH], vp.rearrange("p (h d) -> p h d", h=H)[0:c.keys],
                                        bv[0:c.keys], ALU.add)
                        v.memset(b.va[0:c.keys, t, :, DH:DH + 1], 1.0)
                        ins = v.memset(b.va[0:c.keys, t, :, DH + 1:2 * DH], 0.0)
                    ins.then_inc(S(f"{n}_va"), 1)

                def maxima(p):
                    b, w = bufs[p], 2 * i + p + 1
                    per = c.rounds // NT
                    hr = 2 * c.bank_heads
                    for r in range(c.rounds):
                        t, g = r // per, r % per
                        dve.wait_ge(S(f"{n}_S"), c.rounds * (2 * i + p) + r + 1)
                        src = bank(p, 2 * (r % 2), 2)[:, :, 0:c.bank_heads * c.nk].rearrange("p a (h k) -> p a h k", k=c.nk)
                        v.tensor_reduce(b.nm[:, t, g * hr:(g + 1) * hr].rearrange("p (a h) -> p a h", a=2), src,
                                        axis=AX.X, op=ALU.max, negate=True).then_inc(S(f"{n}_Smax"), 1)
                    dve.wait_ge(S(f"{n}_Smax"), c.rounds * w)
                    steps = 4 * (2 * i + p)
                    if c.clip:
                        ins = v.tensor_scalar(b.nmr[:, 0], b.nm, CLAMP, -CLAMP, ALU.min, ALU.max)
                    else:
                        ins = v.tensor_copy(b.nmr[:, 0], b.nm)
                    ins.then_inc(S(f"{n}_nm"), 1)
                    dve.wait_ge(S(f"{n}_nm"), steps + 1)
                    v.tensor_copy(b.nmb[:, :, 0, :], b.nmr[:, 0]).then_inc(S(f"{n}_nm"), 1)
                    dve.wait_ge(S(f"{n}_nm"), steps + 2)
                    v.tensor_tensor(b.nmr[:, 1], b.nmr[:, 0], b.nmb[:, :, 0, :], ALU.subtract).then_inc(S(f"{n}_nm"), 1)
                    dve.wait_ge(S(f"{n}_nm"), steps + 3)
                    v.tensor_copy(b.nmb[:, :, 1, :], b.nmr[:, 1]).then_inc(S(f"{n}_nm"), 1)
                    dve.wait_ge(S(f"{n}_nm"), steps + 4)
                    v.tensor_tensor(b.nmb[:, :, 2, :], b.nmr[:, 1], b.nmb[:, :, 1, :], ALU.subtract).then_inc(S(f"{n}_nmb"), 1)

                def clip(p):
                    for u in range(c.units):
                        dve.wait_ge(S(f"{n}_ST0"), c.units * (2 * loop + p) + u + 1)
                        sc = bank(p, u % 2)[0:c.keys, :]
                        v.tensor_scalar(sc, sc, CLAMP, -CLAMP, ALU.min, ALU.max).then_inc(S(f"{n}_clip"), 1)

                def norm(p):
                    b, w = bufs[p], 2 * i + p + 1
                    dve.wait_ge(S(f"{n}_O"), w)
                    o = bank(p, 0, 2).rearrange("p t (h x) -> p t h x", x=2 * DH)
                    v.reciprocal(b.rec, o[:, :, :, DH]).then_inc(S(f"{n}_rec"), 1)
                    dve.wait_ge(S(f"{n}_rec"), w)
                    v.tensor_tensor(b.on.rearrange("p t (h x) -> p t h x", h=H), o[:, :, :, 0:DH],
                                    b.rec.unsqueeze(3).broadcast_to([P, NT, H, DH]), ALU.mult).then_inc(S(f"{n}_on"), 1)

                def residual(p):
                    b, w = bufs[p], 2 * i + p + 1
                    dve.wait_ge(S(f"{n}_wo"), w)
                    dve.wait_ge(S(f"{n}_xb"), w)
                    v.tensor_tensor(b.res, halves(bank(p, 3)), b.xb, ALU.add).then_inc(S(f"{n}_res"), 1)
                    layernorm(n, p, i, b.res, None)

                def final(p):
                    normalise(n, p, i, bufs[p].res, xout(bufs[p]))

                return [kv, maxima] + [clip] * c.clip + [norm, residual, final]

            def outlogits(i, tile):
                def stage(p):
                    dve.wait_ge(S("logits_done"), 2 * i + p + 1)
                    v.tensor_copy(logits[:, bass.ds(tile + 2 * p, NT), :],
                                  bank(p, 3)[:, 0:NT * E].rearrange("p (t e) -> p t e", t=NT)).then_inc(S("logits"), 1)
                return [stage]

            def gla_stages(i):
                def gate(p):
                    b, w = bufs[p], 2 * i + p + 1
                    dve.wait_ge(S("a_th"), w)
                    v.scalar_tensor_tensor(out=b.gw, in0=b.th, scalar=1.0, in1=bank(p, 2, 2), op0=ALU.add,
                                           op1=ALU.mult).then_inc(S("a_gate"), 1)

                def zbias(p):
                    b, w = bufs[p], 2 * i + p + 1
                    dve.wait_ge(S("a_z"), w)
                    for k in range(KC):
                        ins = v.tensor_scalar(b.zb[:, k, :], bank(p, 3)[:, k * L:(k + 1) * L], W["a_b2"][:, k:k + 1], None, ALU.add)
                    ins.then_inc(S("a_zb"), 1)

                def sums(p):
                    b, w = bufs[p], 2 * i + p + 1
                    dve.wait_ge(S("a_log"), 3 * w)
                    v.scalar_tensor_tensor(out=b.gl, in0=b.zb, scalar=0.0, in1=b.la, op0=ALU.min,
                                           op1=ALU.subtract).then_inc(S("a_gl"), 1)
                    dve.wait_ge(S("a_gl"), w)
                    for k in range(KC):
                        ins = v.tensor_tensor_scan(b.G[:, k, :], ones[:, :], b.gl[:, k, :], 0.0, ALU.mult, ALU.add)
                    ins.then_inc(S("a_G"), 1)
                    dve.wait_ge(S("a_G"), w)
                    g4 = b.G.rearrange("p k (t s) -> p (k t) s", t=NT)
                    mid = P // 2 - 1
                    v.tensor_tensor(b.f, b.G[:, :, P + mid], b.G[:, :, mid], ALU.subtract)
                    v.tensor_tensor(b.Dd.rearrange("p k (t s) -> p (k t) s", t=NT), g4,
                                    g4[:, :, mid:mid + 1].broadcast_to([P, KC * NT, P]), ALU.subtract).then_inc(S("a_Dd"), 1)

                def scaled(p):
                    b, w = bufs[p], 2 * i + p + 1
                    dve.wait_ge(S("a_decay"), w)
                    dve.wait_ge(S("a_qk"), w)
                    v.scalar_tensor_tensor(out=b.qd, in0=halves(bank(p, 0)), scalar=GDK ** -0.5, in1=b.Eq,
                                           op0=ALU.mult, op1=ALU.mult).then_inc(S("a_qd"), 1)
                    v.tensor_tensor(b.kd, halves(bank(p, 1)), b.Ek, ALU.mult)
                    dve.wait_ge(S("a_qd"), w)
                    for k in range(KC):
                        ins = v.tensor_scalar(b.qx[:, k, :], b.qd[:, k, P:L], b.fx[:, k:k + 1], None, ALU.mult)
                    ins.then_inc(S("a_scaled"), 1)

                def mask(p):
                    b, w = bufs[p], 2 * i + p + 1
                    dve.wait_ge(S("a_A"), w)
                    v.tensor_tensor(b.AT.rearrange("p (h a) s -> p h (a s)", h=GH), bank(p, 0, 4)[:, :, 0:3 * P],
                                    causal[:, :, :].rearrange("p a s -> p (a s)").unsqueeze(1).broadcast_to([P, GH, 3 * P]),
                                    ALU.mult).then_inc(S("a_AT"), 1)

                def gated(p):
                    b, w = bufs[p], 2 * i + p + 1
                    dve.wait_ge(S("a_sq"), w)
                    v.tensor_reduce(b.ms, b.sq.rearrange("p t (h d) -> p (t h) d", h=GH), axis=AX.X, op=ALU.add).then_inc(S("a_ms"), 1)
                    dve.wait_ge(S("a_gatew"), w)
                    v.tensor_tensor(b.y, bank(p, 0, 2), b.gw, ALU.mult).then_inc(S("a_y"), 1)

                def residual(p):
                    b, w = bufs[p], 2 * i + p + 1
                    dve.wait_ge(S("a_wo"), w)
                    v.tensor_tensor(b.res, halves(bank(p, 0)), b.xtok, ALU.add).then_inc(S("a_res"), 1)
                    layernorm("a", p, i, b.res, None)

                def final(p):
                    normalise("a", p, i, bufs[p].res, bufs[p].xA)

                return [gate, zbias, sums, scaled, mask, gated, residual, final]

            with dve.Fori(0, PAIRS) as i:
                for stage in gla_stages(i) + attn_stages(X0, i, lambda b: b.xo) + outlogits(i, 4 * i):
                    for p in range(2):
                        stage(p)

            chain = [0]

            def link(ins):
                chain[0] += 1
                ins.then_inc(S("router_chain"), 1)
                dve.wait_ge(S("router_chain"), chain[0])

            def wide(col):
                return top[:, col, :].unsqueeze(2).broadcast_to([P, TILES, E])

            def router(nth, over_all):
                dve.wait_ge(S("logits"), 2 + B * nth)
                src = logits[:, :, :]
                for k in range(2):
                    link(v.tensor_reduce(top[:, 2 * k, :], src, axis=AX.X, op=ALU.max))
                    link(v.tensor_tensor(rt[:, :, :], src, wide(2 * k), ALU.is_equal))
                    link(v.tensor_tensor(rt[:, :, :], rt[:, :, :], tiebreak[:, :, :], ALU.mult))
                    link(v.tensor_reduce(top[:, 1, :], rt[:, :, :], axis=AX.X, op=ALU.max))
                    link(v.tensor_tensor(hot[:, k], rt[:, :, :], wide(1), ALU.is_equal))
                    if k == 0:
                        link(v.scalar_tensor_tensor(out=wts[:, :, :], in0=hot[:, 0], scalar=-BIG, in1=logits[:, :, :],
                                                    op0=ALU.mult, op1=ALU.add))
                        src = wts[:, :, :]
                v.tensor_tensor(top[:, 4, :], top[:, 2, :], top[:, 0, :], ALU.subtract)
                v.tensor_tensor(rt[:, :, :], logits[:, :, :], wide(0), ALU.subtract).then_inc(S("top2"), 1)
                dve.wait_ge(S("exp2"), nth)
                if over_all:
                    link(v.tensor_reduce(top[:, 6, :], rt[:, :, :], axis=AX.X, op=ALU.add))
                else:
                    link(v.tensor_scalar(top[:, 6, :], top[:, 5, :], 1.0, None, ALU.add))
                link(v.reciprocal(top[:, 6, :], top[:, 6, :]))
                link(v.tensor_tensor(top[:, 7, :], top[:, 5, :], top[:, 6, :], ALU.mult))
                link(v.tensor_tensor(wts[:, :, :], hot[:, 0], wide(6), ALU.mult))
                link(v.tensor_tensor(rt[:, :, :], hot[:, 1], wide(7), ALU.mult))
                link(v.tensor_tensor(wts[:, :, :], wts[:, :, :], rt[:, :, :], ALU.add))

            router(1, False)
            with dve.Fori(0, E // 2) as i:
                for p in range(2):
                    v.tensor_copy(wcol[:, p, :], wts[:, :, bass.ds(2 * i + p, 1)].rearrange("p t a -> p (t a)")).then_inc(S("b_wcol"), 1)
                    dve.wait_ge(S("b_wcol"), 2 * i + p + 1)

                    def accumulate(blk):
                        dve.wait_ge(S("b_y"), NBLK * (2 * i + p) + blk + 1)
                        for j in range(TB):
                            t = blk * TB + j
                            ins = v.scalar_tensor_tensor(
                                out=xres[:, t, :], in0=ps[:, 4 + 2 * (blk % 2) + j // 2, (j % 2) * D:(j % 2 + 1) * D],
                                scalar=wcol[:, p, t:t + 1], in1=xres[:, t, :], op0=ALU.mult, op1=ALU.add)
                        ins.then_inc(S("b_acc"), 1)

                    for blk in range(NBLK):
                        for m in range(MC):
                            s = (p * NBLK + blk) * MC + m
                            dve.wait_ge(S("b_sil"), 2 * NBLK * MC * i + s + 1)
                            v.tensor_tensor(hid[blk % 2][:, m, :], ps[:, 2 * (s % 2) + 1, :], sil[s % 2], ALU.mult).then_inc(S("b_h"), 1)
                        if blk:
                            accumulate(blk - 1)
                    accumulate(NBLK - 1)

            dve.wait_ge(S("c_weights"), c_loads)
            scale_bias(["s1_bq", "x1_bq"], "bq_scaled1")
            dve.wait_ge(S("b_acc"), 2 + NBLK * E)

            def incoming(i):
                def stats(p):
                    b, w = bufs[p], 2 * i + p + 1
                    v.tensor_copy(b.res, xres[:, bass.ds(4 * i + 2 * p, NT), :]).then_inc(S("a_res"), 1)
                    layernorm("a", p, i + PAIRS, b.res, None)

                def final(p):
                    normalise("a", p, i + PAIRS, bufs[p].res, bufs[p].xA)
                return [stats, final]

            with dve.Fori(0, PAIRS) as i:
                for stage in incoming(i) + attn_stages(S1, i, lambda b: b.xB) + attn_stages(X1, i, lambda b: b.xo) \
                        + outlogits(i + PAIRS, 4 * i):
                    for p in range(2):
                        stage(p)
            router(2, True)
            link(v.tensor_tensor(rt[:, :, :], hot[:, 0], hot[:, 1], ALU.add))
            v.tensor_reduce(cnt[:, 0, :], rt[:, :, :].rearrange("p t e -> p e t"), axis=AX.X, op=ALU.add).then_inc(S("d_cnt"), 1)
            dve.wait_ge(S("d_cnt_all"), 1)
            link(v.tensor_scalar(cnt[:, 1, :], ps[:, 4, 0:E], float(CAP), None, ALU.is_le))
            v.tensor_tensor(wts[:, :, :], wts[:, :, :], cnt[:, 1, :].unsqueeze(1).broadcast_to([P, TILES, E]), ALU.mult).then_inc(S("d_wts"), 1)
            dve.wait_ge(S("store"), 2 * B)
            for g in range(TILES // 2):
                dve.wait_ge(S("d_by"), g + 1)
                ins = v.tensor_tensor(xres[:, 2 * g:2 * g + 2, :], halves(ps[:, 2 + g % 2, :]), xres[:, 2 * g:2 * g + 2, :], ALU.add)
                ins.then_inc(S("d_biased"), 1)
            dve.wait_ge(S("d_wts"), 1)
            dve.wait_ge(S("d_biased"), TILES // 2)
            with dve.Fori(0, E // 2) as i:
                for p in range(2):
                    v.tensor_copy(wcol[:, p, :], wts[:, :, bass.ds(2 * i + p, 1)].rearrange("p t a -> p (t a)")).then_inc(S("d_wcol"), 1)
                    dve.wait_ge(S("d_wcol"), 2 * i + p + 1)
                    for blk in range(NBLK):
                        dve.wait_ge(S("d_y"), NBLK * (2 * i + p) + blk + 1)
                        for j in range(TB):
                            t = blk * TB + j
                            ins = v.scalar_tensor_tensor(
                                out=xres[:, t, :], in0=ps[:, 4 + 2 * (blk % 2) + j // 2, (j % 2) * D:(j % 2 + 1) * D],
                                scalar=wcol[:, p, t:t + 1], in1=xres[:, t, :], op0=ALU.mult, op1=ALU.add)
                        ins.then_inc(S("d_acc"), 1)
            dve.wait_ge(S("d_acc"), 2 + NBLK * E)

            def outgoing(i, first):
                def stats(p):
                    b = bufs[p]
                    dve.wait_ge(S("a_out"), 2 * B + 2 * i + p - 1)
                    v.tensor_copy(b.res, xres[:, bass.ds(4 * i + 2 * p, NT), :]).then_inc(S("a_res"), 1)
                    layernorm("a", p, i + 2 * PAIRS, b.res, None)

                def final(p):
                    if not first:
                        dve.wait_ge(S(f"stored{p}"), 16 * i)
                    normalise("a", p, i + 2 * PAIRS, bufs[p].res, bufs[p].xo)
                return [stats, final]

            for stage in outgoing(0, True):
                for p in range(2):
                    stage(p)
            with dve.Fori(1, PAIRS) as i:
                for stage in outgoing(i, False):
                    for p in range(2):
                        stage(p)

        @block.gpsimd
        def _(pool):
            g = nc.gpsimd
            pool.wait_ge(S("memsets"), 4)
            pool.wait_ge(S("gn_halved"), 1)
            pool.wait_ge(S("const_in"), 16 * len(always))
            pool.wait_ge(S("x0_weights"), x0_loads)

            def rstd(n, p, i):
                b, w = bufs[p], 2 * i + p + 1
                pool.wait_ge(S(f"{n}_mv"), w)
                g.tensor_tensor(b.var, b.mv[:, :, 1], eps[:, 0:NT], ALU.add).then_inc(S(f"{n}_var"), 1)
                pool.wait_ge(S(f"{n}_var"), w)
                g.tensor_tensor(b.rstd, b.var, neghalf[:, 0:NT], ALU.pow).then_inc(S(f"{n}_rstd"), 1)

            def attn_stages(c, loop, before, xin):
                n, wn, i = c.prefix, c.name, loop + c.pairs_before

                def xb(p):
                    b = bufs[p]
                    pool.wait_ge(S(f"{before[0]}_out"), before[1] + 2 * loop + p + 1)
                    g.tensor_tensor(b.xb, xin(b), W[f"{wn}_bo"].unsqueeze(1).broadcast_to([P, NT, D]), ALU.add).then_inc(S(f"{n}_xb"), 1)

                def headkeys(p):
                    b, w = bufs[p], 2 * i + p + 1
                    pool.wait_ge(S(f"{n}_kT"), w)
                    kb = b.KB if c.selfattn else b.KBm
                    for k in range(KC):
                        ins = g.tensor_tensor(kb[:, k], b.kT[:, k, 0:c.nk].unsqueeze(1).broadcast_to([P, HC, c.nk]),
                                              rowmask[:, :].unsqueeze(2).broadcast_to([P, HC, c.nk]), ALU.mult)
                    ins.then_inc(S(f"{n}_KB"), 1)

                return [xb, headkeys, lambda p: rstd(n, p, i)]

            def store(first, i):
                def stage(p):
                    w = 2 * i + p + 1
                    pool.wait_ge(S("x_out"), first + w)
                    g.tensor_copy(xres[:, bass.ds(4 * i + 2 * p, NT), :], bufs[p].xo)
                    pool.wait_ge(S("xoT"), first + w)
                    g.tensor_copy(xTres[:, :, bass.ds(512 * i + 256 * p, L)], bufs[p].xoT).then_inc(S("store"), 1)
                return [stage]

            def gla_stages(i):
                def gate(p):
                    b, w = bufs[p], 2 * i + p + 1
                    pool.wait_ge(S("a_gate"), w)
                    gw = b.gw.rearrange("p t (h d) -> p (t h) d", h=GH)
                    g.tensor_tensor(gw, gw, W["a_gn"].unsqueeze(1).broadcast_to([P, NT * GH, GDV]), ALU.mult).then_inc(S("a_gatew"), 1)

                def rms(p):
                    b, w = bufs[p], 2 * i + p + 1
                    pool.wait_ge(S("a_ms"), w)
                    g.tensor_tensor(b.ms, b.ms, eps[:, :], ALU.add).then_inc(S("a_msv"), 1)
                    pool.wait_ge(S("a_msv"), w)
                    g.tensor_tensor(b.rms, b.ms, neghalf[:, :], ALU.pow).then_inc(S("a_rms"), 1)
                    pool.wait_ge(S("a_rms"), w)
                    pool.wait_ge(S("a_y"), w)
                    y = b.y.rearrange("p t (h d) -> p (t h) d", h=GH)
                    g.tensor_tensor(y, y, b.rms.unsqueeze(2).broadcast_to([P, NT * GH, GDV]), ALU.mult).then_inc(S("a_yn"), 1)

                return [gate, rms, lambda p: rstd("a", p, i)]

            with pool.Fori(0, PAIRS) as i:
                for stage in gla_stages(i) + attn_stages(X0, i, ("a", 0), lambda b: b.xA) + store(0, i):
                    for p in range(2):
                        stage(p)
            pool.wait_ge(S("c_weights"), c_loads)
            with pool.Fori(0, PAIRS) as i:
                for stage in [lambda p: rstd("a", p, i + PAIRS)] + attn_stages(S1, i, ("a", B), lambda b: b.xA) \
                        + attn_stages(X1, i, ("s", 0), lambda b: b.xB) + store(B, i):
                    for p in range(2):
                        stage(p)
            with pool.Fori(0, PAIRS) as i:
                for p in range(2):
                    rstd("a", p, i + 2 * PAIRS)

        @block.tensor
        def _(pe):
            mm, tr = nc.tensor.matmul, nc.tensor.transpose

            def attn_stages(c, loop, before, xin, inputs):
                n, wn, i = c.prefix, c.name, loop + c.pairs_before

                def turn(p):
                    b = bufs[p]
                    pe.wait_ge(S(f"{before[0]}_out"), before[1] + 2 * loop + p + 1)
                    for k in range(KC):
                        for t in range(NT):
                            ins = tr(bank(p, 1)[:, k * L + t * P:k * L + (t + 1) * P], xin(b)[:, t, k * P:(k + 1) * P], ident[:, :])
                    ins.then_inc(S(f"{n}_xT_done"), 1)

                def project(p):
                    b, w = bufs[p], 2 * i + p + 1
                    pe.wait_ge(S(f"{n}_xinT"), w)

                    def feat(dst, wt, src, rows, cols):
                        for m in range(KC):
                            for k in range(KC):
                                ins = mm(dst[:, m * cols:(m + 1) * cols], wt[0:rows[k], k, m * P:(m + 1) * P],
                                         src[0:rows[k], k, 0:cols], start=(k == 0), stop=(k == KC - 1))
                        return ins

                    def toks(dst, wt, src, rows, lo, cnt_):
                        for k in range(KC):
                            ins = mm(dst, src[0:rows[k], k, lo:lo + cnt_], wt[0:rows[k], k, :], start=(k == 0), stop=(k == KC - 1))
                        return ins

                    full, part = (P, P), (P, DC - P)
                    feat(bank(p, 2), W[f"{wn}_wq"], b.xinT, full, L).then_inc(S(f"{n}_q"), 1)
                    if c.selfattn:
                        feat(bank(p, 3), W[f"{wn}_wk"], b.xinT, full, L)
                        for t in range(NT):
                            ins = toks(bank(p, 0)[:, t * D:(t + 1) * D], W[f"{wn}_wv"], b.xinT, full, t * P, P)
                    else:
                        pe.wait_ge(S(f"{inputs}{p}"), (64 if inputs == "a_in" else 32) * (loop + 1))
                        feat(bank(p, 3), W[f"{wn}_wk"], b.ctxT, part, M)
                        ins = toks(bank(p, 3)[0:M, D:2 * D], W[f"{wn}_wv"], b.ctxT, part, 0, M)
                    ins.then_inc(S(f"{n}_kv"), 1)

                def scores(p):
                    b, w = bufs[p], 2 * i + p + 1
                    kb = b.KB if c.selfattn else b.KBm
                    pe.wait_ge(S(f"{n}_qs"), w)
                    pe.wait_ge(S(f"{n}_va"), w)
                    pe.wait_ge(S(f"{n}_KB"), w)
                    per = c.rounds // NT
                    for r in range(c.rounds):
                        t, g = r // per, r % per
                        if r >= 2:
                            pe.wait_ge(S(f"{n}_Smax"), c.rounds * (2 * i + p) + r - 1)
                        for j in range(2):
                            h = (2 * g + j) * c.bank_heads
                            k, hh = h // HC, h % HC
                            dst = bank(p, 2 * (r % 2) + j)
                            ins = mm(dst[:, 0:c.bank_heads * c.nk], b.qs[:, k, t * P:(t + 1) * P],
                                     kb[:, k, hh:hh + c.bank_heads, :].rearrange("p h k -> p (h k)"),
                                     start=True, stop=not c.selfattn)
                            if c.selfattn:
                                for a in range(c.bank_heads):
                                    ins = mm(dst[:, a * L + (1 - t) * P:a * L + (2 - t) * P], identb[:, :], winmask[:, t, :],
                                             start=False, stop=(a == c.bank_heads - 1))
                        ins.then_inc(S(f"{n}_S"), 1)

                def shift(p):
                    b = bufs[p]
                    pe.wait_ge(S(f"{n}_nmb"), 2 * i + p + 1)
                    for t in range(NT):
                        ins = mm(bank(p, 0)[0:3 * H, t * P:(t + 1) * P], b.nmb[:, t].rearrange("p a h -> p (a h)"), identb[:, :],
                                 start=True, stop=True)
                    ins.then_inc(S(f"{n}_nmT_done"), 1)

                def attend(p):
                    b, w = bufs[p], 2 * i + p + 1
                    kb = b.KB if c.selfattn else b.KBm
                    pe.wait_ge(S(f"{n}_nmT"), w)

                    def scoresT(u):
                        if u >= 2:
                            pe.wait_ge(S(f"{n}_PT"), c.units * (2 * i + p) + u - 1)
                        dst = bank(p, u % 2)
                        for a in range(2):
                            h = u if c.selfattn else 2 * u + a
                            kt = a if c.selfattn else 0
                            k, hh = h // HC, h % HC
                            cols = dst[0:c.keys, a * L:(a + 1) * L]
                            ins = mm(cols, kb[:, k, hh, kt * P:kt * P + c.keys], b.qs[:, k, :],
                                     start=(a == 0 or not c.clip), stop=c.clip, skip_group_check=c.clip)
                            if c.selfattn:
                                mm(cols[:, (1 - kt) * P:(2 - kt) * P], identb[:, :], winmask[:, kt, :], start=False, stop=False)
                            if not c.clip:
                                ins = mm(cols, headrow[:, h, 0:c.keys], b.nmT, start=False, stop=True)
                        ins.then_inc(S(f"{n}_ST0" if c.clip else f"{n}_ST"), 1)

                    def shifted(u):
                        pe.wait_ge(S(f"{n}_clip"), c.units * (2 * loop + p) + u + 1)
                        for a in range(2):
                            ins = mm(bank(p, u % 2)[0:c.keys, a * L:(a + 1) * L], headrow[:, 2 * u + a, 0:c.keys], b.nmT,
                                     start=False, stop=True, skip_group_check=True)
                        ins.then_inc(S(f"{n}_ST"), 1)

                    def values(u):
                        pe.wait_ge(S(f"{n}_PT"), c.units * (2 * i + p) + u + 1)
                        for a in range(c.unit_heads):
                            h = u * c.unit_heads + a
                            j, gg = h % 4, h // 4
                            for kt in range(c.key_tiles):
                                half = kt if c.selfattn else a
                                ins = mm(bank(p, 2 + gg // 2)[32 * j:32 * j + 32, (gg % 2) * L:(gg % 2 + 1) * L],
                                         b.va[0:c.keys, kt, h, :], b.PT[0:c.keys, u % 4, half * L:(half + 1) * L],
                                         start=(kt == 0), stop=(kt == c.key_tiles - 1))
                        return ins

                    for u in range(c.units):
                        scoresT(u)
                        if c.clip:
                            shifted(u)
                        if u:
                            values(u - 1)
                    values(c.units - 1).then_inc(S(f"{n}_OT_done"), 1)

                def untranspose(p):
                    b, w = bufs[p], 2 * i + p + 1
                    pe.wait_ge(S(f"{n}_OT"), w)
                    for t in range(NT):
                        for gg in range(4):
                            ins = tr(bank(p, t)[:, gg * P:(gg + 1) * P], b.OT[:, gg, t * P:(t + 1) * P], ident[:, :])
                    ins.then_inc(S(f"{n}_O"), 1)

                def turn_out(p):
                    b, w = bufs[p], 2 * i + p + 1
                    pe.wait_ge(S(f"{n}_on"), w)
                    for k in range(KC):
                        for t in range(NT):
                            ins = tr(bank(p, 2)[:, k * L + t * P:k * L + (t + 1) * P], b.on[:, t, k * P:(k + 1) * P], ident[:, :])
                    ins.then_inc(S(f"{n}_onT_done"), 1)

                def project_out(p):
                    b, w = bufs[p], 2 * i + p + 1
                    pe.wait_ge(S(f"{n}_onT"), w)
                    for t in range(NT):
                        for k in range(KC):
                            ins = mm(bank(p, 3)[:, t * D:(t + 1) * D], b.onT[:, k, t * P:(t + 1) * P], W[f"{wn}_wo"][:, k, :],
                                     start=(k == 0), stop=(k == KC - 1))
                    ins.then_inc(S(f"{n}_wo"), 1)

                return [turn, project, scores, shift, attend, untranspose, turn_out, project_out]

            def out_stages(first, r, i):
                def turn(p):
                    b, w = bufs[p], 2 * i + p + 1
                    pe.wait_ge(S("x_out"), first + w)
                    for k in range(KC):
                        for t in range(NT):
                            ins = tr(bank(p, 2)[:, k * L + t * P:k * L + (t + 1) * P], b.xo[:, t, k * P:(k + 1) * P], ident[:, :])
                    ins.then_inc(S("xoT_done"), 1)

                def route(p):
                    b, w = bufs[p], 2 * i + p + 1
                    pe.wait_ge(S("xoT"), first + w)
                    for t in range(NT):
                        for k in range(KC):
                            ins = mm(bank(p, 3)[:, t * E:(t + 1) * E], b.xoT[:, k, t * P:(t + 1) * P], r[:, k, :],
                                     start=(k == 0), stop=(k == KC - 1))
                    ins.then_inc(S("logits_done"), 1)

                return [turn, route]

            def gla_stages(i):
                def values(p):
                    b, w = bufs[p], 2 * i + p + 1
                    pe.wait_ge(S(f"a_in{p}"), 64 * (i + 1))
                    pe.wait_ge(S("logits"), w)
                    for wt, first, signal in (("a_wv", 0, "a_v"), ("a_wg", 2, "a_g")):
                        for t in range(NT):
                            for k in range(KC):
                                ins = mm(bank(p, first + t), b.xT[:, k, t * P:(t + 1) * P], W[wt][:, k, :],
                                         start=(k == 0), stop=(k == KC - 1))
                        ins.then_inc(S(signal), 1)

                def keys(p):
                    b, w = bufs[p], 2 * i + p + 1
                    pe.wait_ge(S("a_vs"), w)
                    for n, wt in enumerate(("a_wq", "a_wk")):
                        for m in range(KC):
                            for k in range(KC):
                                ins = mm(bank(p, n)[:, m * L:(m + 1) * L], W[wt][:, k, m * P:(m + 1) * P], b.xT[:, k, :],
                                         start=(k == 0), stop=(k == KC - 1))
                    ins.then_inc(S("a_qk"), 1)
                    pe.wait_ge(S("a_gate"), w)
                    for k in range(KC):
                        ins = mm(bank(p, 2)[0:LOWRANK, 0:L], W["a_w1"][:, k, :], b.xT[:, k, :], start=(k == 0), stop=(k == KC - 1))
                    ins.then_inc(S("a_g1_done"), 1)

                def decay(p):
                    b, w = bufs[p], 2 * i + p + 1
                    pe.wait_ge(S("a_g1"), w)
                    for m in range(KC):
                        ins = mm(bank(p, 3)[:, m * L:(m + 1) * L], W["a_w2"][:, m * P:(m + 1) * P], b.g1, start=True, stop=True)
                    ins.then_inc(S("a_z"), 1)

                def scores(p):
                    b, w = bufs[p], 2 * i + p + 1
                    pe.wait_ge(S("a_scaled"), w)
                    for h in range(GH):
                        k, r = h // 2, slice(GDK * (h % 2), GDK * (h % 2) + GDK)
                        for a, (key, qry) in enumerate(((b.kd[r, k, 0:P], b.qd[r, k, 0:P]), (b.kd[r, k, P:L], b.qd[r, k, P:L]),
                                                        (b.kd[r, k, 0:P], b.qx[r, k, :]))):
                            ins = mm(bank(p, h)[:, a * P:(a + 1) * P], key, qry, start=True, stop=True)
                    ins.then_inc(S("a_A"), 1)

                def mix(p):
                    b, w = bufs[p], 2 * i + p + 1
                    pe.wait_ge(S("a_AT"), w)
                    for h in range(GH):
                        c = slice(h * GDV, (h + 1) * GDV)
                        mm(bank(p, 0)[:, c], b.AT[:, 3 * h, :], b.v[:, 0, c], start=True, stop=True)
                        mm(bank(p, 1)[:, c], b.AT[:, 3 * h + 2, :], b.v[:, 0, c], start=True, stop=False)
                        ins = mm(bank(p, 1)[:, c], b.AT[:, 3 * h + 1, :], b.v[:, 1, c], start=False, stop=True)
                    ins.then_inc(S("a_o"), 1)

                def turn(p):
                    b, w = bufs[p], 2 * i + p + 1
                    pe.wait_ge(S("a_yn"), w)
                    for t in range(NT):
                        for k in range(VC):
                            ins = tr(bank(p, 2 + t)[:, k * P:(k + 1) * P], b.y[:, t, k * P:(k + 1) * P], ident[:, :])
                    ins.then_inc(S("a_yT_done"), 1)

                def project_out(p):
                    b, w = bufs[p], 2 * i + p + 1
                    pe.wait_ge(S("a_yT"), w)
                    for t in range(NT):
                        for k in range(VC):
                            ins = mm(bank(p, 0)[:, t * D:(t + 1) * D], b.yT[:, t, k * P:(k + 1) * P], W["a_wo"][:, k, :],
                                     start=(k == 0), stop=(k == VC - 1))
                    ins.then_inc(S("a_wo"), 1)

                return [values, keys, decay, scores, mix, turn, project_out]

            pe.wait_ge(S("a_weights"), 16 * 9)
            pe.wait_ge(S("const_in"), 16 * len(always))
            pe.wait_ge(S("x0_weights"), x0_loads)
            with pe.Fori(0, PAIRS) as i:
                for stage in gla_stages(i) + attn_stages(X0, i, ("a", 0), lambda b: b.xA, "a_in") + out_stages(0, r0, i):
                    for p in range(2):
                        stage(p)

            with pe.Fori(0, E // 2) as i:
                def hidden(p, blk):
                    for m in range(MC):
                        s = (p * NBLK + blk) * MC + m
                        pe.wait_ge(S("b_h"), 2 * NBLK * MC * i + s + 1)
                        for a, wt in enumerate(("w1", "w2")):
                            for k in range(KC):
                                ins = mm(ps[:, 2 * (s % 2) + a, :], stream0[p][wt][:, k, m * P:(m + 1) * P],
                                         xTres[:, k, blk * BLK:(blk + 1) * BLK], start=(k == 0), stop=(k == KC - 1))
                        ins.then_inc(S("b_uv"), 1)

                def outputs(p, blk):
                    pe.wait_ge(S("b_acc"), NBLK * (2 * i + p) + blk + 1)
                    pe.wait_ge(S("b_h"), 2 + 2 * NBLK * MC * i + (p * NBLK + blk) * MC + MC)
                    for j in range(TB):
                        dst = ps[:, 4 + 2 * (blk % 2) + j // 2, (j % 2) * D:(j % 2 + 1) * D]
                        for m in range(MC):
                            ins = mm(dst, hid[blk % 2][:, m, j * P:(j + 1) * P], stream0[p]["w3"][:, m, :],
                                     start=(m == 0), stop=(m == MC - 1))
                    ins.then_inc(S("b_y"), 1)

                for p in range(2):
                    pe.wait_ge(S(f"b_w{p}"), 48 * (i + 1))
                    for blk in range(NBLK):
                        hidden(p, blk)
                        if blk:
                            outputs(p, blk - 1)
                    outputs(p, NBLK - 1)

            pe.wait_ge(S("c_weights"), c_loads)
            with pe.Fori(0, PAIRS) as i:
                for stage in attn_stages(S1, i, ("a", B), lambda b: b.xA, "") + attn_stages(X1, i, ("s", 0), lambda b: b.xB, "c_in") \
                        + out_stages(B, r1, i):
                    for p in range(2):
                        stage(p)

            pe.wait_ge(S("d_cnt"), 1)
            mm(ps[:, 4, 0:E], onemat[:, :], cnt[:, 0, :], start=True, stop=True).then_inc(S("d_cnt_all"), 1)
            pe.wait_ge(S("d_wts"), 1)
            pe.wait_ge(S("store"), 2 * B)
            for q in range(TILES // TB):
                if q >= 2:
                    pe.wait_ge(S("d_wT"), q - 1)
                for j in range(TB):
                    ins = tr(ps[0:E, q % 2, j * P:(j + 1) * P], wts[:, q * TB + j, :], ident[:, :])
                ins.then_inc(S("d_wT_done"), 1)
            for q in range(TILES // 2):
                pe.wait_ge(S("d_wT"), q // 2 + 1)
                if q >= 2:
                    pe.wait_ge(S("d_biased"), q - 1)
                for j in range(2):
                    ins = mm(ps[:, 2 + q % 2, j * D:(j + 1) * D], wT[:, 2 * q + j, :], f_b2[:, :], start=True, stop=True)
                ins.then_inc(S("d_by"), 1)

            pe.wait_ge(S("d_biased"), TILES // 2)
            with pe.Fori(0, E // 2) as i:
                def hidden1(p, blk):
                    for m in range(KC):
                        s = (p * NBLK + blk) * KC + m
                        for k in range(KC):
                            ins = mm(ps[:, s % 4, :], stream1[p]["w1"][:, k, m * P:(m + 1) * P],
                                     xTres[:, k, blk * BLK:(blk + 1) * BLK], start=(k == 0), stop=(k == KC - 1))
                        ins.then_inc(S("d_u"), 1)

                def outputs1(p, blk):
                    pe.wait_ge(S("d_acc"), NBLK * (2 * i + p) + blk + 1)
                    pe.wait_ge(S("d_h"), 2 * NBLK * KC * i + (p * NBLK + blk) * KC + KC)
                    for j in range(TB):
                        dst = ps[:, 4 + 2 * (blk % 2) + j // 2, (j % 2) * D:(j % 2 + 1) * D]
                        for m in range(KC):
                            ins = mm(dst, hid[blk % 2][:, m, j * P:(j + 1) * P], stream1[p]["w2"][:, m, :],
                                     start=(m == 0), stop=(m == KC - 1))
                    ins.then_inc(S("d_y"), 1)

                for p in range(2):
                    pe.wait_ge(S(f"d_w{p}"), 48 * (i + 1))
                    for blk in range(NBLK):
                        hidden1(p, blk)
                        if blk:
                            outputs1(p, blk - 1)
                    outputs1(p, NBLK - 1)


def kernel(**inputs):
    import concourse.bacc as bacc
    from concourse.bass_utils import run_bass_kernel_spmd
    import ml_dtypes

    a = {k: np.asarray(v) for k, v in inputs.items()}
    bf = ml_dtypes.bfloat16

    def chunk(w):
        return w.reshape(-1, P, w.shape[-1]).transpose(1, 0, 2)

    def cols(v):
        return v.reshape(-1, P).T

    d = {"x": a["x"].reshape(B, NT, P, D), "xT": a["x"].transpose(0, 2, 1).reshape(B, KC, P, L),
         "ctxT": a["ctx_768"].transpose(0, 2, 1)}
    for n, k in (("wq", "Wq"), ("wk", "Wk"), ("wv", "Wv"), ("wg", "Wg"), ("w1", "gk_w1"), ("wo", "Wo")):
        d["a_" + n] = chunk(a["L0_attn_" + k])
    d["a_w2"] = a["L0_attn_gk_w2"]
    d["a_b2"] = cols(a["L0_attn_gk_b2"])
    d["a_gn"] = a["L0_attn_g_norm_w"][None]
    wkv = a["L0_xattn_Wkv"].reshape(H, 2, DH, DC)
    bkv = a["L0_xattn_bkv"].reshape(H, 2, DH)
    layers = {
        "x0": {"wq": a["L0_xattn_Wq"].T, "wk": wkv[:, 0].reshape(D, DC).T, "wv": wkv[:, 1].reshape(D, DC).T,
               "wo": a["L0_xattn_Wo"].T, "bq": a["L0_xattn_bq"], "bk": bkv[:, 0].reshape(D), "bv": bkv[:, 1].reshape(D),
               "bo": a["L0_xattn_bo"]},
        "s1": {n.lower(): a["L1_attn_" + n] for n in ("Wq", "Wk", "Wv", "Wo", "bq", "bk", "bv", "bo")},
        "x1": {n.lower(): a["L1_xattn_" + n] for n in ("Wq", "Wk", "Wv", "Wo", "bq", "bk", "bv", "bo")},
    }
    for x, w in layers.items():
        for n, t in w.items():
            if n[0] == "w":
                d[f"{x}_{n}"] = chunk(t) if t.shape[0] % P == 0 else t
            else:
                d[f"{x}_{n}"] = cols(t) if n in ("bq", "bk") else t[None]
    d["r0"] = chunk(a["L0_ffn_Wg"])
    d["r1"] = chunk(a["L1_ffn_gate_w"].T)
    d["m1_b1"] = a["L1_ffn_b1"].reshape(E, KC, P).transpose(0, 2, 1)
    d["f_b2"] = a["L1_ffn_b2"]
    d["m0_w1"] = a["L0_ffn_W1"].reshape(E, KC, P, FH)
    d["m0_w2"] = a["L0_ffn_W2"].reshape(E, KC, P, FH)
    d["m0_w3"] = a["L0_ffn_W3"].reshape(E, MC, P, D)
    d["m1_w1"] = a["L1_ffn_w1"].transpose(0, 2, 1).reshape(E, KC, P, D)
    d["m1_w2"] = a["L1_ffn_w2"].transpose(0, 2, 1).reshape(E, KC, P, D)
    r = np.arange(P)
    upper = (r[None, :] >= r[:, None]).astype(np.float32)
    d["ident"] = np.eye(P, dtype=np.float32)
    d["identb"] = np.eye(P, dtype=bf)
    d["causal"] = np.stack([upper, upper, np.ones((P, P), np.float32)], 1)
    d["rowmask"] = (r[:, None] // DH == np.arange(HC)[None]).astype(np.float32)
    d["headrow"] = np.broadcast_to((np.arange(3 * H)[:, None] % H == np.arange(H)[None])[:, :, None], (3 * H, H, P)).astype(bf)
    d["winmask"] = np.stack([np.where(r[None, :] > r[:, None], -BIG, 0), np.where(r[None, :] < r[:, None], -BIG, 0)], 1).astype(bf)
    d["tiebreak"] = np.broadcast_to(E - np.arange(E, dtype=np.float32), (P, TILES, E))

    nc = bacc.Bacc("TRN2", target_bir_lowering=False, num_devices=1)
    arrays, dram = {}, {}
    for n, t in d.items():
        t = np.ascontiguousarray(t)
        arrays["in_" + n] = t
        dram[n] = nc.dram_tensor("in_" + n, t.shape, mybir.dt.from_np(t.dtype), kind="ExternalInput").ap()
    out = nc.dram_tensor("out_x", (B, NT, P, D), F32, kind="ExternalOutput").ap()
    build_program(nc, dram, out)
    r = run_bass_kernel_spmd(nc, [arrays], core_ids=[0])
    return r.results[0]["out_x"].reshape(B, L, D)
```

```python
from contextlib import ExitStack

import numpy as np

import concourse.bass as bass
from concourse import mybir

F32 = mybir.dt.float32
F32R = mybir.dt.float32r
I32 = mybir.dt.int32
BF16 = mybir.dt.bfloat16
ALU = mybir.AluOpType
ACT = mybir.ActivationFunctionType
AX = mybir.AxisListType

P = 128
B, L, D = 8, 256, 256
NT = L // P
KC = D // P
TILES = B * NT
PAIRS = B // 2
M, DC = 77, 192
GH, GDK, GDV = 4, 64, 128
VD = GH * GDV
VC = VD // P
LOWRANK = 16
GATE_NORM = 16.0
H, DH = 16, 16
HC = P // (2 * DH)
QC = H // HC
QSCALE = DH ** -0.5
E, FH = 8, 512
MC = FH // P
TILES0 = 2 * TILES + E
SLOTS1 = 384
ST1 = SLOTS1 // P
CAP = int(1.25 * B * L / E)
assert CAP <= SLOTS1
TRASH = E * SLOTS1
ROWS = max(TILES0 * P, TRASH + 2 * B * L)
assert TRASH <= TILES0 * P
CLAMP = 10000.0
EPS = 1e-5
BIG = 1e30


class Attn:

    def __init__(self, name, prefix, before, selfattn, clip):
        self.name, self.selfattn, self.clip = name, selfattn, clip
        self.prefix, self.pairs_before = prefix, before
        self.keys = P if selfattn else M
        self.key_tiles = NT if selfattn else 1
        self.nk = self.keys * self.key_tiles
        self.bank_heads = 2 if selfattn else 4
        self.turn_bank = 1 if selfattn else 2
        self.rounds = NT * H // (2 * self.bank_heads)
        self.unit_heads = 1 if selfattn else 2
        self.units = H // self.unit_heads
        self.units_at_once = 4 // self.unit_heads
        self.PT_units = 2 * self.units_at_once


class Both:

    def __init__(self, steps):
        self.steps = steps


def in_turn(stages):
    for stage in stages:
        if isinstance(stage, Both):
            stage.steps()
        else:
            for p in range(2):
                stage(p)


X0 = Attn("x0", "x", 0, False, False)
S1 = Attn("s1", "s", 0, True, False)
X1 = Attn("x1", "x", PAIRS, False, True)


def build_program(nc, dram, out, rows_in, rows_out):
    with ExitStack() as ctx:
        def sb(name, shape, dt=F32):
            return ctx.enter_context(nc.sbuf_tensor("sb_" + name, shape, dt))

        sems = {}

        def S(name):
            if name not in sems:
                sems[name] = ctx.enter_context(nc.semaphore(name))
            return sems[name]

        ident = sb("ident", [P, P])
        causal = sb("causal", [P, 3, P])
        rowmask = sb("rowmask", [P, HC])
        lowrow = sb("lowrow", [P, 2])
        headrow = sb("headrow", [3 * H, H, P], BF16)
        identb = sb("identb", [P, P], BF16)
        winmask = sb("winmask", [P, 2, P], BF16)
        tiebreak = sb("tiebreak", [P, TILES, E])
        onemat = sb("onemat", [P, P])
        ones = sb("ones", [P, L])
        neghalf = sb("neghalf", [P, 8])
        eps = sb("eps", [P, 8])
        ptick = sb("ptick", [P, 1])
        tick = sb("tick", [P, 1])
        r0, r1 = sb("r0", [P, KC, E]), sb("r1", [P, KC, E])
        zeros = sb("zeros", [P, D])
        scan_reset = sb("scan_reset", [P, E * TILES])
        tile_start = sb("tile_start", [P, TILES])
        tile_no = sb("tile_no", [P, TILES0])
        base1 = sb("base1", [P, E])
        trash = sb("trash", [P, 2, TILES])
        always = {"ident": ident, "causal": causal, "rowmask": rowmask, "lowrow": lowrow, "headrow": headrow, "identb": identb,
                  "winmask": winmask, "tiebreak": tiebreak, "r0": r0, "r1": r1, "scan_reset": scan_reset, "tile_start": tile_start, "tile_no": tile_no, "base1": base1, "trash": trash}
        always = {n: t[:] for n, t in always.items()}

        xres = sb("xres", [P, TILES, D])
        logits = sb("logits", [P, TILES, E])
        wts = sb("wts", [P, 2, TILES])
        hot = sb("hot", [P, 2, TILES, E])
        rt = sb("rt", [P, TILES, E])
        masked = sb("masked", [P, TILES, E])
        rank = sb("rank", [P, E, TILES])
        part = sb("part", [P, E, TILES])
        top = sb("top", [P, 8, TILES])
        cnt = sb("cnt", [P, 4, E])
        slot = sb("slot", [P, 2, TILES])
        keep = sb("keep", [P, 2, TILES])
        scat = sb("scat", [P, 2, TILES], I32)
        gath = sb("gath", [P, 2, TILES], I32)
        gidx = sb("gidx", [P, 2, 2, NT], I32)
        owner = sb("owner", [1, TILES0])
        owner_i = sb("owner_i", [1, TILES0], I32)
        owned = sb("owned", [1, TILES0, E])

        WREG = 8192
        wreg = sb("wreg", [P, WREG])

        def view(t, off, dims, rows=P):
            v = t[0:rows, off:off + int(np.prod(dims))]
            if len(dims) == 2:
                v = v.rearrange("p (a b) -> p a b", a=dims[0])
            if len(dims) == 3:
                v = v.rearrange("p (a b c) -> p a b c", a=dims[0], b=dims[1])
            return v

        def place(t, off, end, items):
            got = {}
            for name, dims in items:
                got[name] = view(t, off, dims)
                off += int(np.prod(dims))
            assert off <= end, (off, end)
            return got

        def attn_items(n):
            return [(f"{n}_{w}", (KC, 2 * D)) for w in ("wq", "wk")] + [(f"{n}_{w}", (KC, D)) for w in ("wv", "wo")] + \
                   [(f"{n}_{w}", (QC,)) for w in ("bq", "bk")] + [(f"{n}_{w}", (D,)) for w in ("bv", "bo")]

        w0 = place(wreg, 0, WREG, [("a_wq", (KC, D)), ("a_wk", (KC, D)), ("a_wv", (KC, VD)), ("a_wg", (KC, VD)),
                                   ("a_w1", (KC, LOWRANK)), ("a_w2", (D,)), ("a_b2", (KC,)), ("a_gn", (GDV,)),
                                   ("a_wo", (VC, D))] + attn_items("x0"))
        w1 = place(wreg, 0, WREG, attn_items("s1") + attn_items("x1"))
        W = w0 | w1
        W["a_w2"] = W["a_w2"][0:LOWRANK, :]

        COMMON, REGION = 5248, 12288
        arena = sb("arena", [P, 2 * (COMMON + REGION)])
        arena_at = nc.sbuf_base - 4 * 2 * (COMMON + REGION)
        bufs = []
        for p in range(2):
            o = p * (COMMON + REGION)
            b = place(arena, o, o + COMMON, [
                ("xT", (KC, L)), ("xtok", (NT, D)), ("ctxT", (2, M + 1)), ("xA", (NT, D)), ("xB", (NT, D)),
                ("xinT", (KC, L)), ("xb", (NT, D)), ("res", (NT, D)), ("xo", (NT, D)), ("xoT", (KC, L)),
                ("f", (KC,)), ("fx", (KC,)), ("ms", (8,)), ("rms", (8,)), ("st0", (6,)), ("st1", (6,)),
                ("mv", (NT, 2)), ("var", (NT,)), ("rstd", (NT,)), ("nm", (NT, H)), ("rec", (NT, H)),
                ("nmb", (NT * 3 * H // 2,)), ("nmr", (2 * NT * H,)), ("nmTf", (L // 2,))])
            o += COMMON
            b |= place(arena, o, o + REGION, [
                ("v", (NT, VD)), ("gw", (NT, VD)), ("th", (NT, VD)), ("zb", (KC, L)), ("la", (KC, L)),
                ("gl", (KC, L)), ("G", (KC, L)), ("qd", (KC, L)), ("kd", (KC, L)), ("qx", (KC, P)), ("g1", (L,)),
                ("AT", (GH * 3, P))])
            b |= place(arena, o + 3072, o + REGION, [("Eq", (KC, L)), ("Ek", (KC, L)), ("Dd", (KC, L))])
            b |= place(arena, o + 2048, o + REGION, [("sq", (NT, VD)), ("y", (NT, VD)), ("yT", (NT, VD))])
            b |= place(arena, o, o + REGION, [
                ("parts", (3 * QC * 2 * L,)), ("va", (NT, H, 2 * DH)), ("PT", (8, 2 * L)), ("OT", (4, L))])
            parts = nc.alloc_sbuf_tensor_at(f"sb_parts{p}", [P, 3 * QC * 2 * L], F32R, offset=arena_at + 4 * o)
            b |= place(parts, 0, 3 * QC * 2 * L, [("qh", (QC, L)), ("ql", (QC, L)), ("KB", (QC, HC, L))])
            b["KBm"] = view(parts, 2 * QC * L, (QC, HC, M))
            b |= place(arena, o + 3 * QC * 2 * L + 1024, o + REGION, [("qf", (QC, L)), ("kl", (QC, L)), ("kh", (QC, L)), ("kp", (QC, L))])
            b |= place(arena, o, o + 1024, [("onT", (KC, L)), ("on", (NT, D))])
            b["g1"] = b["g1"][0:LOWRANK, :]
            b["yg"] = view(arena, p * (COMMON + REGION), (2, NT, D))
            b["nmb"] = b["nmb"].bitcast(BF16).rearrange("p (t a h) -> p t a h", t=NT, a=3)
            b["nmr"] = b["nmr"].rearrange("p (a t h) -> p a t h", a=2, t=NT)
            b["nmT"] = b["nmTf"].bitcast(BF16)[0:3 * H, :]
            bufs.append(type("Bufs", (), b))
        ew = arena[:, 0:E * 3072].rearrange("p (e a) -> p e a", e=E)
        slots0, experts1 = [], []
        for p in range(2):
            o = E * 3072 + 2304 * p
            slots0.append(type("Slots", (), place(arena, o, o + 2304, [
                ("x", (D,)), ("xT", (KC, P)), ("sil", (FH,)), ("h", (FH,)), ("hT", (MC, P)), ("y", (D,))])))
            o = 4608 * p
            experts1.append(type("Expert", (), place(arena, o, o + 4608, [
                ("w1", (KC, D)), ("w2", (KC, D)), ("b1", (KC,)), ("b2", (D,)), ("x", (ST1, D)), ("xT", (KC, SLOTS1)),
                ("hid", (KC, SLOTS1)), ("y", (ST1, D))])))

        ps = ctx.enter_context(nc.psum_tensor("ps", [P, 8, 512], F32))

        def bank(p, n, k=1):
            return ps[:, 4 * p + n, :] if k == 1 else ps[:, 4 * p + n:4 * p + n + k, :]

        def halves(ap):
            return ap.rearrange("p (a b) -> p a b", a=2)

        def chunks128(ap):
            return ap.rearrange("p (a b) -> p a b", b=P)

        block = ctx.enter_context(nc.Block())

        def load_weight(eng, n, signal):
            src = dram[n]
            dst = W.get(n, always.get(n))
            if n[-2:] in ("bv", "bo") or n == "a_gn":
                src = src.broadcast_to([P, src.shape[1]])
            if n in ("x0_wk", "x0_wv", "x1_wk", "x1_wv"):
                eng.dma_start(dst[:, 0, :], src[0:P, :]).then_inc(S(signal), 16)
                eng.dma_start(dst[0:DC - P, 1, :], src[P:DC, :]).then_inc(S(signal), 16)
            else:
                eng.dma_start(dst, src).then_inc(S(signal), 16)

        x0_names = [n for n, _ in attn_items("x0")]
        a_loads = 16 * (9 + len(always) + len(x0_names) + 2)
        c_loads = 16 * (2 * len(x0_names) + 2)

        @block.sync
        def _(sp):
            def loads(b1, p, first):
                bf = bufs[p]
                if first:
                    sp.dma_start(bf.xT, dram["xT"][b1, :, :, :].rearrange("a k p t -> (a p) k t")).then_inc(S(f"a_in{p}"), 16)
                    sp.dma_start(bf.xtok, dram["x"][b1, :, :, :].rearrange("a t p d -> (a p) t d")).then_inc(S(f"a_in{p}"), 16)
                name = f"a_in{p}" if first else f"c_in{p}"
                sp.dma_start(bf.ctxT[:, 0, 0:M], dram["ctxT"][b1, 0:P, :].rearrange("a c m -> (a c) m")).then_inc(S(name), 16)
                sp.dma_start(bf.ctxT[0:DC - P, 1, 0:M], dram["ctxT"][b1, P:DC, :].rearrange("a c m -> (a c) m")).then_inc(S(name), 16)

            for p in range(2):
                loads(bass.ds(p, 1), p, True)
            for n in ("a_wv", "a_wg", "a_wq", "a_wk", "a_w1"):
                sp.dma_start(W[n], dram[n]).then_inc(S("a_weights"), 16)
            sp.wait_ge(S("memsets"), 5)
            sp.dma_start(rows_in[0:TILES0 * P, :].rearrange("(t p) d -> p t d", p=P),
                         zeros[:, :].unsqueeze(1).broadcast_to([P, TILES0, D])).then_inc(S("cleared"), 16)
            with sp.Fori(1, PAIRS) as i:
                for p in range(2):
                    sp.wait_ge(S("x_out"), 2 * i + p - 1)
                    loads(bass.ds(2 * i + p, 1), p, True)
            sp.wait_ge(S("logits"), 2 + B)
            sp.wait_ge(S("store"), B)

            for e in range(E):
                for n, o, k in (("w1", 0, KC), ("w2", 1024, KC), ("w3", 2048, MC)):
                    sp.dma_start(ew[:, e, o:o + 1024].rearrange("p (k h) -> p k h", k=k),
                                 dram["m0_" + n][e:e + 1, :, :, :].rearrange("a k p h -> (a p) k h")).then_inc(S("t_w"), 16)
            for n in [n for n, _ in attn_items("s1") + attn_items("x1")]:
                load_weight(sp, n, "c_weights")

            def load_tile(j, p):
                sp.dma_start(slots0[p].x, rows_in[bass.ds(j * P, P), :]).then_inc(S(f"t_in{p}"), 16)

            def store_tile(j, p):
                sp.wait_ge(S("t_ys"), j + 1)
                sp.dma_start(rows_out[bass.ds(j * P, P), :], slots0[p].y).then_inc(S(f"t_out{p}"), 16)

            sp.wait_ge(S("scattered"), 16 * 2 * TILES)
            for p in range(2):
                load_tile(p, p)
            with sp.Fori(0, TILES0 // 2 - 1) as i:
                for p in range(2):
                    sp.wait_ge(S("t_X"), 2 * i + p + 1)
                    load_tile(2 * i + p + 2, p)
                    store_tile(2 * i + p, p)
            for p in range(2):
                store_tile(TILES0 - 2 + p, p)
            for p in range(2):
                sp.wait_ge(S(f"t_out{p}"), 16 * TILES0 // 2)
            for p in range(2):
                loads(bass.ds(p, 1), p, False)
            with sp.Fori(1, PAIRS) as i:
                for p in range(2):
                    sp.wait_ge(S("x_out"), B + 2 * i + p - 1)
                    loads(bass.ds(2 * i + p, 1), p, False)
            sp.wait_ge(S("logits"), 2 + 2 * B)
            sp.wait_ge(S("store"), 2 * B)

            def load_expert(e, p):
                b = experts1[p]
                for n in ("w1", "w2"):
                    sp.dma_start(b.w1 if n == "w1" else b.w2,
                                 dram["m1_" + n][e, :, :, :].rearrange("a k p h -> (a p) k h")).then_inc(S(f"e_w{p}"), 16)
                sp.dma_start(b.b1, dram["m1_b1"][e, :, :].rearrange("a p k -> (a p) k")).then_inc(S(f"e_w{p}"), 16)

            def load_bias(e, p):
                b = experts1[p]
                sp.dma_start(b.b2, dram["m1_b2"][e, :, :].rearrange("a b d -> (a b) d").broadcast_to([P, D])).then_inc(S(f"e_w{p}"), 16)

            def load_rows(e, p):
                sp.dma_start(experts1[p].x, rows_in[bass.ds(e * SLOTS1, SLOTS1), :].rearrange("(t p) d -> p t d", p=P)
                             ).then_inc(S(f"e_in{p}"), 16)

            def store_rows(e, p):
                sp.wait_ge(S("e_ys"), e + 1)
                sp.dma_start(rows_out[bass.ds(e * SLOTS1, SLOTS1), :].rearrange("(t p) d -> p t d", p=P),
                             experts1[p].y).then_inc(S(f"e_out{p}"), 16)

            for p in range(2):
                load_expert(bass.ds(p, 1), p)
                load_bias(bass.ds(p, 1), p)
            sp.wait_ge(S("scattered"), 2 * 16 * 2 * TILES)
            for p in range(2):
                load_rows(p, p)
            with sp.Fori(0, E // 2 - 1) as i:
                for p in range(2):
                    sp.wait_ge(S("e_X"), 2 * i + p + 1)
                    load_rows(2 * i + p + 2, p)
                    sp.wait_ge(S("e_y"), 2 * i + p + 1)
                    load_expert(bass.ds(2 * i + p + 2, 1), p)
                    store_rows(2 * i + p, p)
                    load_bias(bass.ds(2 * i + p + 2, 1), p)
            for p in range(2):
                store_rows(E - 2 + p, p)
            for p in range(2):
                sp.wait_ge(S(f"e_out{p}"), 16 * E // 2)
            with sp.Fori(0, PAIRS) as i:
                for p in range(2):
                    sp.wait_ge(S("a_out"), 2 * B + 2 * i + p + 1)
                    sp.dma_start(out[bass.ds(2 * i + p, 1), :, :, :].rearrange("a t p d -> (a p) t d"),
                                 bufs[p].xo).then_inc(S(f"stored{p}"), 16)
            for p in range(2):
                sp.wait_ge(S(f"stored{p}"), 16 * PAIRS)

        @block.scalar
        def _(act):
            for n in always:
                load_weight(act, n, "a_weights")
            for n in ("a_w2", "a_b2", "a_gn", "a_wo"):
                load_weight(act, n, "a_weights")
            for n in x0_names:
                load_weight(act, n, "a_weights")
            nc.scalar.preload_act_table_set("natural_log_exp_and_others")

            def attn_stages(c, i):
                n, wn, i = c.prefix, c.name, i + c.pairs_before

                def xinT(p):
                    act.wait_ge(S(f"{n}_xT_done"), 2 * i + p + 1)
                    nc.scalar.activation(bufs[p].xinT, halves(bank(p, c.turn_bank)), ACT.Copy).then_inc(S(f"{n}_xinT"), 1)

                def q(p):
                    act.wait_ge(S(f"{n}_q"), 2 * i + p + 1)
                    for dst in (bufs[p].qh, bufs[p].qf):
                        for k in range(QC):
                            ins = nc.scalar.activation(dst[:, k, :], bank(p, 2 + k // 2)[:, k % 2 * L:(k % 2 + 1) * L], ACT.Identity,
                                                       bias=W[f"{wn}_bq"][:, k:k + 1], scale=QSCALE)
                        ins.then_inc(S(f"{n}_qh"), 1)

                def shift(p):
                    act.wait_ge(S(f"{n}_nmT_done"), 2 * i + p + 1)
                    nc.scalar.activation(bufs[p].nmT, bank(p, 3)[0:3 * H, 0:L], ACT.Copy).then_inc(S(f"{n}_nmT"), 1)

                def probs():
                    for u in range(c.units):
                        for p in range(2):
                            act.wait_ge(S(f"{n}_ST"), 2 * c.units * i + 2 * u + p + 1)
                            nc.scalar.activation(bufs[p].PT[0:c.keys, u % c.PT_units, :], bank(p, u % 2)[0:c.keys, :],
                                                 ACT.Exp).then_inc(S(f"{n}_PT"), 1)

                def heads(p):
                    act.wait_ge(S(f"{n}_OT_done"), 2 * i + p + 1)
                    nc.scalar.activation(bufs[p].OT, bank(p, 2, 2), ACT.Copy).then_inc(S(f"{n}_OT"), 1)

                def onT(p):
                    act.wait_ge(S(f"{n}_onT_done"), 2 * i + p + 1)
                    nc.scalar.activation(bufs[p].onT, halves(bank(p, 2)), ACT.Copy).then_inc(S(f"{n}_onT"), 1)

                return [xinT, q, shift, Both(probs), heads, onT]

            def outT(i):
                def stage(p):
                    act.wait_ge(S("xoT_done"), 2 * i + p + 1)
                    nc.scalar.activation(bufs[p].xoT, halves(bank(p, 2)), ACT.Copy).then_inc(S("xoT"), 1)
                return [stage]

            def gla_stages(i):
                def v(p):
                    act.wait_ge(S("a_v"), 2 * i + p + 1)
                    nc.scalar.activation(bufs[p].v, bank(p, 2, 2), ACT.Copy).then_inc(S("a_vs"), 1)

                def gate(p):
                    act.wait_ge(S("a_g"), 2 * i + p + 1)
                    nc.scalar.activation(bufs[p].th, bank(p, 2, 2), ACT.Tanh, scale=0.5).then_inc(S("a_th"), 1)

                def lowrank(p):
                    act.wait_ge(S("a_g1_done"), 2 * i + p + 1)
                    nc.scalar.activation(bufs[p].g1, bank(p, 2)[0:LOWRANK, 0:L], ACT.Copy).then_inc(S("a_g1"), 1)

                def softplus(p):
                    b = bufs[p]
                    if p == 0:
                        nc.scalar.preload_act_table_set("natural_log_exp_and_others")
                    act.wait_ge(S("a_zb"), 2 * i + p + 1)
                    nc.scalar.activation(b.la, b.zb, ACT.Abs).then_inc(S("a_log"), 1)
                    act.wait_ge(S("a_log"), 3 * (2 * i + p) + 1)
                    nc.scalar.activation(b.la, b.la, ACT.Exp, scale=-1.0).then_inc(S("a_log"), 1)
                    act.wait_ge(S("a_log"), 3 * (2 * i + p) + 2)
                    nc.scalar.activation(b.la, b.la, ACT.Ln, bias=ones[:, 0:1]).then_inc(S("a_log"), 1)

                def decay(p):
                    b = bufs[p]
                    act.wait_ge(S("a_Dd"), 2 * i + p + 1)
                    nc.scalar.activation(b.Eq, b.Dd, ACT.Exp, scale=1.0 / GATE_NORM)
                    nc.scalar.activation(b.Ek, b.Dd, ACT.Exp, scale=-1.0 / GATE_NORM)
                    nc.scalar.activation(b.fx, b.f, ACT.Exp, scale=1.0 / GATE_NORM).then_inc(S("a_decay"), 1)

                def square(p):
                    act.wait_ge(S("a_o"), 2 * i + p + 1)
                    nc.scalar.activation(bufs[p].sq, bank(p, 0, 2), ACT.Square, scale=GDV ** -0.5).then_inc(S("a_sq"), 1)

                def yT(p):
                    act.wait_ge(S("a_yT_done"), 2 * i + p + 1)
                    nc.scalar.activation(bufs[p].yT, bank(p, 2, 2), ACT.Copy).then_inc(S("a_yT"), 1)

                return [lowrank, softplus, v, decay, gate, square, yT]

            act.wait_ge(S("memsets"), 5)
            act.wait_ge(S("rescaled"), 1)
            with act.Fori(0, PAIRS) as i:
                in_turn(gla_stages(i) + attn_stages(X0, i) + outT(i))

            def router(nth):
                act.wait_ge(S("top2"), nth)
                nc.scalar.activation(top[:, 5, :], top[:, 4, :], ACT.Exp)
                nc.scalar.activation(rt[:, :, :], rt[:, :, :], ACT.Exp).then_inc(S("exp2"), 1)

            router(1)

            def tile0(j, p):
                b = slots0[p]
                act.wait_ge(S("t_u"), j + 1)
                nc.scalar.activation(b.sil, bank(p, 0), ACT.Silu).then_inc(S("t_sil"), 1)
                act.wait_ge(S("t_H"), j + 1)
                nc.scalar.activation(b.hT, chunks128(bank(p, 2)), ACT.Copy).then_inc(S("t_hT"), 1)

            with act.Fori(0, TILES0 // 4) as i:
                for j in range(4):
                    tile0(4 * i + j, j % 2)
            act.wait_ge(S("rescaled"), 3)
            with act.Fori(0, PAIRS) as i:
                in_turn(attn_stages(S1, i) + attn_stages(X1, i) + outT(i + PAIRS))
            router(2)
            with act.Fori(0, E // 4) as i:
                for j in range(4):
                    p = j % 2
                    for m in range(KC):
                        if m == 0:
                            act.wait_ge(S(f"e_w{p}"), 64 * (2 * i + j // 2 + 1))
                        act.wait_ge(S("e_u"), KC * (4 * i + j) + m + 1)
                        nc.scalar.activation(experts1[p].hid[:, m, :], ps[:, 2 + m, 0:SLOTS1], ACT.Silu,
                                             bias=experts1[p].b1[:, m:m + 1]).then_inc(S("e_h"), 1)

        @block.vector
        def _(dve):
            v = nc.vector
            v.memset(onemat[:, :], 1.0).then_inc(S("memsets"), 1)
            v.memset(neghalf[:, :], -0.5).then_inc(S("memsets"), 1)
            v.memset(eps[:, :], EPS).then_inc(S("memsets"), 1)
            v.memset(ones[:, :], 1.0).then_inc(S("memsets"), 1)
            v.memset(zeros[:, :], 0.0).then_inc(S("memsets"), 1)
            v.memset(cnt[:, 0, 3:4], 0.0).then_inc(S("logits"), 2)

            def scale_bias(names, signal):
                for k, n in enumerate(names):
                    ins = v.tensor_scalar(W[n], W[n], QSCALE, None, ALU.mult)
                ins.then_inc(S(signal), 1)

            dve.wait_ge(S("a_weights"), a_loads)
            scale_bias(["x0_bq"], "rescaled")
            v.tensor_scalar(W["a_gn"], W["a_gn"], 0.5, None, ALU.mult).then_inc(S("rescaled"), 1)

            def layernorm(n, p, i, src, dst):
                b = bufs[p]
                w = 2 * i + p + 1
                dve.wait_ge(S(f"{n}_res"), w)
                v.bn_stats(b.st0, src[:, 0, :])
                v.bn_stats(b.st1, src[:, 1, :]).then_inc(S(f"{n}_stats"), 1)
                dve.wait_ge(S(f"{n}_stats"), w)
                v.memset(tick[:, :], 0.0)
                v.bn_aggr(b.mv[:, 0, :], b.st0)
                v.bn_aggr(b.mv[:, 1, :], b.st1).then_inc(S(f"{n}_mv"), 1)

            def normalise(n, p, i, src, dst):
                b = bufs[p]
                dve.wait_ge(S(f"{n}_rstd"), 2 * i + p + 1)
                for t in range(NT):
                    ins = v.tensor_scalar(dst[:, t, :], src[:, t, :], b.mv[:, t, 0:1], b.rstd[:, t:t + 1],
                                          ALU.subtract, ALU.mult)
                ins.then_inc(S(f"{n}_out"), 1)

            def attn_stages(c, loop, xout, between=()):
                n, wn, i = c.prefix, c.name, loop + c.pairs_before

                def keys(p):
                    b, w = bufs[p], 2 * i + p + 1
                    dve.wait_ge(S(f"{n}_kv"), 4 * i + p + 1)
                    kp = bank(p, 0, 2).rearrange("p a b -> p (a b)")[:, 0:QC * c.nk].rearrange("p (a b) -> p a b", a=QC)
                    kl, kh, parts = b.kl[:, :, 0:c.nk], b.kh[:, :, 0:c.nk], b.kp[:, :, 0:c.nk]
                    v.tensor_tensor(kh.bitcast(F32R), kp, W[f"{wn}_bk"].unsqueeze(2).broadcast_to([P, QC, c.nk]), ALU.add)
                    for k in range(QC):
                        ins = v.tensor_scalar(kl[:, k, :], kp[:, k, :], W[f"{wn}_bk"][:, k:k + 1], lowrow[:, 0:1], ALU.add, ALU.mult)
                    ins.then_inc(S(f"{n}_kT"), 1)
                    dve.wait_ge(S(f"{n}_kT"), 2 * w - 1)
                    v.scalar_tensor_tensor(out=parts.bitcast(F32R), in0=kh, scalar=lowrow[:, 1:2], in1=kl,
                                           op0=ALU.mult, op1=ALU.add).then_inc(S(f"{n}_kT"), 1)

                def values(p):
                    b, w = bufs[p], 2 * i + p + 1
                    dve.wait_ge(S(f"{n}_kv"), 4 * i + 2 + p + 1)
                    bv = W[f"{wn}_bv"].rearrange("p (h d) -> p h d", h=H)
                    for t in range(c.key_tiles):
                        vp = halves(bank(p, 2))[:, t, :] if c.selfattn else bank(p, 1)[:, 0:D]
                        v.tensor_tensor(b.va[0:c.keys, t, :, 0:DH], vp.rearrange("p (h d) -> p h d", h=H)[0:c.keys],
                                        bv[0:c.keys], ALU.add)
                        v.memset(b.va[0:c.keys, t, :, DH:DH + 1], 1.0)
                        ins = v.memset(b.va[0:c.keys, t, :, DH + 1:2 * DH], 0.0)
                    ins.then_inc(S(f"{n}_va"), 1)

                def maxima(p):
                    b, w = bufs[p], 2 * i + p + 1
                    per = c.rounds // NT
                    hr = 2 * c.bank_heads
                    for r in range(c.rounds):
                        t, g = r // per, r % per
                        dve.wait_ge(S(f"{n}_S"), c.rounds * (2 * i + p) + r + 1)
                        src = bank(p, 2 * (r % 2), 2)[:, :, 0:c.bank_heads * c.nk].rearrange("p a (h k) -> p a h k", k=c.nk)
                        v.tensor_reduce(b.nm[:, t, g * hr:(g + 1) * hr].rearrange("p (a h) -> p a h", a=2), src,
                                        axis=AX.X, op=ALU.max, negate=True).then_inc(S(f"{n}_Smax"), 1)

                def split():
                    def step(k, p):
                        return S(f"{n}_nm"), 8 * i + 2 * k + p + 1

                    for p in range(2):
                        b = bufs[p]
                        dve.wait_ge(S(f"{n}_Smax"), c.rounds * (2 * i + p + 1))
                        if c.clip:
                            ins = v.tensor_scalar(b.nmr[:, 0], b.nm, CLAMP, -CLAMP, ALU.min, ALU.max)
                        else:
                            ins = v.tensor_copy(b.nmr[:, 0], b.nm)
                        ins.then_inc(S(f"{n}_nm"), 1)
                    for p in range(2):
                        b = bufs[p]
                        dve.wait_ge(*step(0, p))
                        v.tensor_copy(b.nmb[:, :, 0, :], b.nmr[:, 0]).then_inc(S(f"{n}_nm"), 1)
                    for p in range(2):
                        b = bufs[p]
                        dve.wait_ge(*step(1, p))
                        v.tensor_tensor(b.nmr[:, 1], b.nmr[:, 0], b.nmb[:, :, 0, :], ALU.subtract).then_inc(S(f"{n}_nm"), 1)
                    for p in range(2):
                        b = bufs[p]
                        dve.wait_ge(*step(2, p))
                        v.tensor_copy(b.nmb[:, :, 1, :], b.nmr[:, 1]).then_inc(S(f"{n}_nm"), 1)
                    for p in range(2):
                        b = bufs[p]
                        dve.wait_ge(*step(3, p))
                        v.tensor_tensor(b.nmb[:, :, 2, :], b.nmr[:, 1], b.nmb[:, :, 1, :], ALU.subtract).then_inc(S(f"{n}_nmb"), 1)

                def clip():
                    for u in range(c.units):
                        for p in range(2):
                            dve.wait_ge(S(f"{n}_ST0"), 2 * c.units * loop + 2 * u + p + 1)
                            sc = bank(p, u % 2)[0:c.keys, :]
                            v.tensor_scalar(sc, sc, CLAMP, -CLAMP, ALU.min, ALU.max).then_inc(S(f"{n}_clip"), 1)

                def norm(p):
                    b, w = bufs[p], 2 * i + p + 1
                    dve.wait_ge(S(f"{n}_O"), w)
                    o = bank(p, 0, 2).rearrange("p t (h x) -> p t h x", x=2 * DH)
                    v.reciprocal(b.rec, o[:, :, :, DH]).then_inc(S(f"{n}_rec"), 1)
                    dve.wait_ge(S(f"{n}_rec"), w)
                    v.tensor_tensor(b.on.rearrange("p t (h x) -> p t h x", h=H), o[:, :, :, 0:DH],
                                    b.rec.unsqueeze(3).broadcast_to([P, NT, H, DH]), ALU.mult).then_inc(S(f"{n}_on"), 1)

                def residual(p):
                    b, w = bufs[p], 2 * i + p + 1
                    dve.wait_ge(S(f"{n}_wo"), w)
                    dve.wait_ge(S(f"{n}_xb"), w)
                    v.tensor_tensor(b.res, halves(bank(p, 3)), b.xb, ALU.add).then_inc(S(f"{n}_res"), 1)
                    layernorm(n, p, i, b.res, None)

                def final(p):
                    normalise(n, p, i, bufs[p].res, xout(bufs[p]))

                return [keys, values, maxima, Both(split), *between] + [Both(clip)] * c.clip + [norm, residual, final]

            def outlogits(i, tile):
                def stage(p):
                    dve.wait_ge(S("logits_done"), 2 * i + p + 1)
                    v.tensor_copy(logits[:, bass.ds(tile + 2 * p, NT), :],
                                  bank(p, 3)[:, 0:NT * E].rearrange("p (t e) -> p t e", t=NT)).then_inc(S("logits"), 1)
                return [stage]

            def gla_stages(i):
                def gate(p):
                    b, w = bufs[p], 2 * i + p + 1
                    dve.wait_ge(S("a_th"), w)
                    v.scalar_tensor_tensor(out=b.gw, in0=b.th, scalar=1.0, in1=bank(p, 2, 2), op0=ALU.add,
                                           op1=ALU.mult).then_inc(S("a_gate"), 1)

                def zbias(p):
                    b, w = bufs[p], 2 * i + p + 1
                    dve.wait_ge(S("a_z"), w)
                    for k in range(KC):
                        ins = v.tensor_scalar(b.zb[:, k, :], bank(p, 3)[:, k * L:(k + 1) * L], W["a_b2"][:, k:k + 1], None, ALU.add)
                    ins.then_inc(S("a_zb"), 1)

                def sums(p):
                    b, w = bufs[p], 2 * i + p + 1
                    dve.wait_ge(S("a_log"), 3 * w)
                    v.scalar_tensor_tensor(out=b.gl, in0=b.zb, scalar=0.0, in1=b.la, op0=ALU.min,
                                           op1=ALU.subtract).then_inc(S("a_gl"), 1)
                    dve.wait_ge(S("a_gl"), w)
                    for k in range(KC):
                        ins = v.tensor_tensor_scan(b.G[:, k, :], ones[:, :], b.gl[:, k, :], 0.0, ALU.mult, ALU.add)
                    ins.then_inc(S("a_G"), 1)
                    dve.wait_ge(S("a_G"), w)
                    g4 = b.G.rearrange("p k (t s) -> p (k t) s", t=NT)
                    mid = P // 2 - 1
                    v.tensor_tensor(b.f, b.G[:, :, P + mid], b.G[:, :, mid], ALU.subtract)
                    v.tensor_tensor(b.Dd.rearrange("p k (t s) -> p (k t) s", t=NT), g4,
                                    g4[:, :, mid:mid + 1].broadcast_to([P, KC * NT, P]), ALU.subtract).then_inc(S("a_Dd"), 1)

                def scaled(p):
                    b, w = bufs[p], 2 * i + p + 1
                    dve.wait_ge(S("a_decay"), w)
                    dve.wait_ge(S("a_qk"), w)
                    v.scalar_tensor_tensor(out=b.qd, in0=halves(bank(p, 0)), scalar=GDK ** -0.5, in1=b.Eq,
                                           op0=ALU.mult, op1=ALU.mult).then_inc(S("a_qd"), 1)
                    v.tensor_tensor(b.kd, halves(bank(p, 1)), b.Ek, ALU.mult)
                    dve.wait_ge(S("a_qd"), w)
                    for k in range(KC):
                        ins = v.tensor_scalar(b.qx[:, k, :], b.qd[:, k, P:L], b.fx[:, k:k + 1], None, ALU.mult)
                    ins.then_inc(S("a_scaled"), 1)

                def mask(p):
                    b, w = bufs[p], 2 * i + p + 1
                    dve.wait_ge(S("a_A"), w)
                    v.tensor_tensor(b.AT.rearrange("p (h a) s -> p h (a s)", h=GH), bank(p, 0, 4)[:, :, 0:3 * P],
                                    causal[:, :, :].rearrange("p a s -> p (a s)").unsqueeze(1).broadcast_to([P, GH, 3 * P]),
                                    ALU.mult).then_inc(S("a_AT"), 1)

                def gated(p):
                    b, w = bufs[p], 2 * i + p + 1
                    dve.wait_ge(S("a_sq"), w)
                    v.tensor_reduce(b.ms, b.sq.rearrange("p t (h d) -> p (t h) d", h=GH), axis=AX.X, op=ALU.add).then_inc(S("a_ms"), 1)
                    dve.wait_ge(S("a_gatew"), w)
                    v.tensor_tensor(b.y, bank(p, 0, 2), b.gw, ALU.mult).then_inc(S("a_y"), 1)

                def residual(p):
                    b, w = bufs[p], 2 * i + p + 1
                    dve.wait_ge(S("a_wo"), w)
                    v.tensor_tensor(b.res, halves(bank(p, 3)), b.xtok, ALU.add).then_inc(S("a_res"), 1)
                    layernorm("a", p, i, b.res, None)

                def final(p):
                    normalise("a", p, i, bufs[p].res, bufs[p].xA)

                return [zbias, sums, scaled, gate, mask, gated, residual, final]

            with dve.Fori(0, PAIRS) as i:
                in_turn(gla_stages(i) + attn_stages(X0, i, lambda b: b.xo) + outlogits(i, 4 * i))

            chain = [0]

            def link(ins):
                chain[0] += 1
                ins.then_inc(S("router_chain"), 1)
                dve.wait_ge(S("router_chain"), chain[0])

            def wide(col):
                return top[:, col, :].unsqueeze(2).broadcast_to([P, TILES, E])

            def router(nth, over_all):
                dve.wait_ge(S("logits"), 2 + B * nth)
                src = logits[:, :, :]
                for k in range(2):
                    link(v.tensor_reduce(top[:, 2 * k, :], src, axis=AX.X, op=ALU.max))
                    link(v.tensor_tensor(rt[:, :, :], src, wide(2 * k), ALU.is_equal))
                    link(v.tensor_tensor(rt[:, :, :], rt[:, :, :], tiebreak[:, :, :], ALU.mult))
                    link(v.tensor_reduce(top[:, 1, :], rt[:, :, :], axis=AX.X, op=ALU.max))
                    link(v.tensor_tensor(hot[:, k], rt[:, :, :], wide(1), ALU.is_equal))
                    if k == 0:
                        link(v.scalar_tensor_tensor(out=masked[:, :, :], in0=hot[:, 0], scalar=-BIG, in1=logits[:, :, :],
                                                    op0=ALU.mult, op1=ALU.add))
                        src = masked[:, :, :]
                v.tensor_tensor(top[:, 4, :], top[:, 2, :], top[:, 0, :], ALU.subtract)
                v.tensor_tensor(rt[:, :, :], logits[:, :, :], wide(0), ALU.subtract).then_inc(S("top2"), 1)
                link(v.tensor_tensor(masked[:, :, :], hot[:, 0], hot[:, 1], ALU.add))
                v.memset(tick[:, :], 0.0).then_inc(S("chosen"), 1)
                dve.wait_ge(S("exp2"), nth)
                if over_all:
                    link(v.tensor_reduce(top[:, 6, :], rt[:, :, :], axis=AX.X, op=ALU.add))
                else:
                    link(v.tensor_scalar(top[:, 6, :], top[:, 5, :], 1.0, None, ALU.add))
                link(v.reciprocal(wts[:, 0, :], top[:, 6, :]))
                link(v.tensor_tensor(wts[:, 1, :], top[:, 5, :], wts[:, 0, :], ALU.mult))

            def by_expert(ap):
                return ap.rearrange("p t e -> p e t")

            def over_tiles(ap):
                return ap.unsqueeze(2).broadcast_to([P, E, TILES])

            def choose(dst, values):
                for k in range(2):
                    link(v.tensor_tensor(part[:, :, :], by_expert(hot[:, k]), values, ALU.mult))
                    link(v.tensor_reduce(dst[:, k, :], part[:, :, :].rearrange("p e t -> p t e"), axis=AX.X, op=ALU.add))

            def ranks(nth):
                dve.wait_ge(S("counted"), nth)
                before, total = ps[:, 4, 0:P], ps[:, 4, P:2 * P]
                link(v.tensor_copy(rank[:, :, :], by_expert(total.rearrange("p (t e) -> p t e", e=E))))
                link(v.tensor_tensor_scan(part[:, :, :].rearrange("p e t -> p (e t)"), scan_reset[:, :],
                                          rank[:, :, :].rearrange("p e t -> p (e t)"), 0.0, ALU.mult, ALU.add))
                v.tensor_copy(cnt[:, 0, :], part[:, :, TILES - 1])
                link(v.tensor_tensor(rank[:, :, :], part[:, :, :], rank[:, :, :], ALU.subtract))
                link(v.tensor_tensor(rank[:, :, :], rank[:, :, :], by_expert(before.rearrange("p (t e) -> p t e", e=E)), ALU.add))
                link(v.tensor_tensor(rank[:, :, :], rank[:, :, :], by_expert(masked[:, :, :]), ALU.subtract))

            def dispatch0():
                link(v.tensor_tensor(part[:, :, :], over_tiles(cnt[:, 0, :]),
                                     tile_start[:, :].unsqueeze(1).broadcast_to([P, E, TILES]), ALU.is_gt))
                link(v.tensor_reduce(cnt[:, 1, :], part[:, :, :], axis=AX.X, op=ALU.add))
                link(v.tensor_tensor_scan(cnt[:, 2, :], ones[:, 0:E], cnt[:, 1, :], 0.0, ALU.mult, ALU.add))
                link(v.tensor_tensor(cnt[:, 3, :], cnt[:, 2, :], cnt[:, 1, :], ALU.subtract))
                link(v.tensor_scalar(cnt[:, 3, :], cnt[:, 3, :], float(P), None, ALU.mult))
                link(v.tensor_tensor(rank[:, :, :], rank[:, :, :], over_tiles(cnt[:, 3, :]), ALU.add))
                choose(slot, rank[:, :, :])
                v.tensor_copy(gath[:, :, :], slot[:, :, :])
                v.tensor_copy(scat[:, :, :], slot[:, :, :]).then_inc(S("dispatched"), 1)
                link(v.tensor_tensor(owned[:, :, :], cnt[0:1, 2, :].unsqueeze(1).broadcast_to([1, TILES0, E]),
                                     tile_no[0:1, :].unsqueeze(2).broadcast_to([1, TILES0, E]), ALU.is_le))
                link(v.tensor_reduce(owner[:, :], owned[:, :, :], axis=AX.X, op=ALU.add))
                link(v.tensor_scalar(owner[:, :], owner[:, :], float(E - 1), None, ALU.min))
                v.tensor_copy(owner_i[:, :], owner[:, :]).then_inc(S("dispatched"), 1)

            def dispatch1():
                link(v.tensor_scalar(cnt[:, 1, :], cnt[:, 0, :], float(CAP), None, ALU.is_le))
                link(v.tensor_tensor(rank[:, :, :], rank[:, :, :], over_tiles(base1[:, :]), ALU.add))
                choose(slot, rank[:, :, :])
                choose(keep, over_tiles(cnt[:, 1, :]))
                link(v.tensor_tensor(wts[:, :, :], wts[:, :, :], keep[:, :, :], ALU.mult))
                two = part[:, 0:2, :]
                link(v.tensor_tensor(two, slot[:, :, :], trash[:, :, :], ALU.subtract))
                link(v.tensor_tensor(two, two, keep[:, :, :], ALU.mult))
                link(v.tensor_tensor(two, two, trash[:, :, :], ALU.add))
                v.tensor_copy(scat[:, :, :], two).then_inc(S("dispatched"), 1)
                link(v.tensor_tensor(slot[:, :, :], slot[:, :, :], keep[:, :, :], ALU.mult))
                link(v.tensor_copy(gath[:, :, :], slot[:, :, :]))
                v.memset(tick[:, :], 0.0).then_inc(S("dispatched"), 1)

            router(1, False)
            ranks(1)
            dispatch0()

            def rows0(j, p):
                dve.wait_ge(S("t_X"), j + 1)
                v.tensor_copy(slots0[p].xT, bank(p, 2)[:, 0:D].rearrange("p (k t) -> p k t", k=KC)).then_inc(S("t_xT"), 1)

            def hidden0(j, p):
                b = slots0[p]
                dve.wait_ge(S("t_v"), j + 1)
                dve.wait_ge(S("t_sil"), j + 1)
                v.tensor_tensor(b.h, bank(p, 1), b.sil, ALU.mult).then_inc(S("t_h"), 1)

            def outputs0(j, p, h, first=False):
                dve.wait_ge(S("t_y"), j + 1)
                if not first:
                    dve.wait_ge(S(f"t_out{p}"), 16 * h)
                v.tensor_copy(slots0[p].y, bank(p, 3)[:, 0:D]).then_inc(S("t_ys"), 1)

            rows0(0, 0)
            rows0(1, 1)
            hidden0(0, 0)
            for j in (1, 2):
                hidden0(j, j % 2)
                rows0(j + 1, (j + 1) % 2)
                outputs0(j - 1, (j - 1) % 2, 0, True)
            with dve.Fori(1, TILES0 // 2 - 1) as i:
                for p in range(2):
                    j = 2 * i + 1 + p
                    hidden0(j, 1 - p)
                    rows0(j + 1, p)
                    outputs0(j - 1, p, i)
            hidden0(TILES0 - 1, 1)
            for p in range(2):
                outputs0(TILES0 - 2 + p, p, TILES0 // 2 - 1)

            dve.wait_ge(S("c_weights"), c_loads)
            scale_bias(["s1_bq", "x1_bq"], "rescaled")
            def mixed(i, ph, xout, first=False):
                def stats(p):
                    b = bufs[p]
                    if ph == 2:
                        dve.wait_ge(S("a_out"), 2 * B + 2 * i + p - 1)
                    dve.wait_ge(S(f"gathered{p}"), 64 * (PAIRS * (ph - 1) + i + 1))
                    for k in range(2):
                        for t in range(NT):
                            tile = 4 * i + 2 * p + t
                            before = xres[:, bass.ds(tile, 1), :].rearrange("p a d -> p (a d)") if k == 0 else b.res[:, t, :]
                            ins = v.scalar_tensor_tensor(out=b.res[:, t, :], in0=bufs[p].yg[:, k, t, :],
                                                         scalar=wts[:, k, bass.ds(tile, 1)], in1=before,
                                                         op0=ALU.mult, op1=ALU.add)
                        ins.then_inc(S("mixed" if k == 0 else "a_res"), 1)
                        if k == 0:
                            dve.wait_ge(S("mixed"), B * (ph - 1) + 2 * i + p + 1)
                    layernorm("a", p, i + ph * PAIRS, b.res, None)

                def final(p):
                    if ph == 2 and not first:
                        dve.wait_ge(S(f"stored{p}"), 16 * i)
                    normalise("a", p, i + ph * PAIRS, bufs[p].res, xout(bufs[p]))
                return [stats, final]

            def second(i, last=False):
                ahead = [] if last else mixed(i + 1, 1, lambda b: b.xA)
                in_turn(attn_stages(S1, i, lambda b: b.xB, ahead) + attn_stages(X1, i, lambda b: b.xo)
                        + outlogits(i + PAIRS, 4 * i))

            in_turn(mixed(0, 1, lambda b: b.xA))
            with dve.Fori(0, PAIRS - 1) as i:
                second(i)
            second(PAIRS - 1, True)
            router(2, True)
            ranks(2)
            dispatch1()

            def rows1(e, p):
                dve.wait_ge(S("e_X"), e + 1)
                v.tensor_copy(experts1[p].xT, ps[:, 0:2, 0:SLOTS1]).then_inc(S("e_xT"), 1)

            def outputs1(e, p, h, first=False):
                dve.wait_ge(S("e_y"), e + 1)
                if not first:
                    dve.wait_ge(S(f"e_out{p}"), 16 * h)
                b = experts1[p]
                v.tensor_tensor(b.y, ps[:, 4 + 2 * p:6 + 2 * p, :].rearrange("p a (t d) -> p (a t) d", d=D)[:, 0:ST1, :],
                                b.b2.unsqueeze(1).broadcast_to([P, ST1, D]), ALU.add).then_inc(S("e_ys"), 1)

            rows1(0, 0)
            for p in range(2):
                rows1(p + 1, 1 - p)
                outputs1(p, p, 0, True)
            with dve.Fori(1, E // 2 - 1) as i:
                for p in range(2):
                    rows1(2 * i + p + 1, 1 - p)
                    outputs1(2 * i + p, p, i)
            rows1(E - 1, 1)
            for p in range(2):
                outputs1(E - 2 + p, p, E // 2 - 1)
            in_turn(mixed(0, 2, lambda b: b.xo, True))
            with dve.Fori(1, PAIRS) as i:
                in_turn(mixed(i, 2, lambda b: b.xo))

        @block.gpsimd
        def _(pool):
            g = nc.gpsimd
            pool.wait_ge(S("memsets"), 5)
            pool.wait_ge(S("rescaled"), 2)
            pool.wait_ge(S("a_weights"), a_loads)

            def rstd(n, p, i):
                b, w = bufs[p], 2 * i + p + 1
                pool.wait_ge(S(f"{n}_mv"), w)
                g.tensor_tensor(b.var, b.mv[:, :, 1], eps[:, 0:NT], ALU.add).then_inc(S(f"{n}_var"), 1)
                pool.wait_ge(S(f"{n}_var"), w)
                g.tensor_tensor(b.rstd, b.var, neghalf[:, 0:NT], ALU.pow).then_inc(S(f"{n}_rstd"), 1)

            def attn_stages(c, loop, before, xin, between=()):
                n, wn, i = c.prefix, c.name, loop + c.pairs_before

                def xb(p):
                    b = bufs[p]
                    pool.wait_ge(S(f"{before[0]}_out"), before[1] + 2 * loop + p + 1)
                    g.tensor_tensor(b.xb, xin(b), W[f"{wn}_bo"].unsqueeze(1).broadcast_to([P, NT, D]), ALU.add).then_inc(S(f"{n}_xb"), 1)

                def headkeys(p):
                    b, w = bufs[p], 2 * i + p + 1
                    pool.wait_ge(S(f"{n}_kT"), 2 * w)
                    kb = b.KB if c.selfattn else b.KBm
                    for k in range(QC):
                        ins = g.tensor_tensor(kb[:, k], b.kp[:, k, 0:c.nk].unsqueeze(1).broadcast_to([P, HC, c.nk]),
                                              rowmask[:, :].unsqueeze(2).broadcast_to([P, HC, c.nk]), ALU.mult)
                        ins.then_inc(S(f"{n}_KB"), 1)

                def low(p):
                    b = bufs[p]
                    pool.wait_ge(S(f"{n}_qh"), 2 * (2 * i + p + 1))
                    g.tensor_tensor(b.ql, b.qf, b.qh, ALU.subtract).then_inc(S(f"{n}_qs"), 1)

                return [xb, headkeys, low, *between, lambda p: rstd(n, p, i)]

            def store(first, i):
                def stage(p):
                    pool.wait_ge(S("x_out"), first + 2 * i + p + 1)
                    g.tensor_copy(xres[:, bass.ds(4 * i + 2 * p, NT), :], bufs[p].xo).then_inc(S("store"), 1)
                return [stage]

            def scatter(nth):
                pool.wait_ge(S("dispatched"), 2 * nth - 1)
                pool.wait_ge(S("cleared"), 16)
                pool.wait_ge(S("store"), B * nth)
                for t in range(TILES):
                    for k in range(2):
                        g.indirect_dma_start(rows_in[:, :], bass.IndirectOffsetOnAxis(ap=scat[:, k, t:t + 1], axis=0),
                                             xres[:, t, :], None).then_inc(S("scattered"), 16)

            def gather(i, ph):
                def stage(p):
                    w = B * (ph - 1) + 2 * i + p + 1
                    if not (ph == 1 and type(i) is int and i == 0):
                        pool.wait_ge(S("a_res"), B * ph + 2 * i + p - 1)
                    g.tensor_copy(gidx[:, p, :, :], gath[:, :, bass.ds(4 * i + 2 * p, NT)]).then_inc(S("gidx"), 1)
                    pool.wait_ge(S("gidx"), w)
                    g.tensor_tensor(ptick[:, :], eps[:, 0:1], eps[:, 0:1], ALU.add)
                    for k in range(2):
                        for t in range(NT):
                            g.indirect_dma_start(bufs[p].yg[:, k, t, :], None, rows_out[0:TILES0 * P if ph == 1 else TRASH, :],
                                                 bass.IndirectOffsetOnAxis(ap=gidx[:, p, k, t:t + 1], axis=0)
                                                 ).then_inc(S(f"gathered{p}"), 16)
                return [stage]

            def gla_stages(i):
                def gate(p):
                    b, w = bufs[p], 2 * i + p + 1
                    pool.wait_ge(S("a_gate"), w)
                    gw = b.gw.rearrange("p t (h d) -> p (t h) d", h=GH)
                    g.tensor_tensor(gw, gw, W["a_gn"].unsqueeze(1).broadcast_to([P, NT * GH, GDV]), ALU.mult).then_inc(S("a_gatew"), 1)

                def rms(p):
                    b, w = bufs[p], 2 * i + p + 1
                    pool.wait_ge(S("a_ms"), w)
                    g.tensor_tensor(b.ms, b.ms, eps[:, :], ALU.add).then_inc(S("a_msv"), 1)
                    pool.wait_ge(S("a_msv"), w)
                    g.tensor_tensor(b.rms, b.ms, neghalf[:, :], ALU.pow).then_inc(S("a_rms"), 1)
                    pool.wait_ge(S("a_rms"), w)
                    pool.wait_ge(S("a_y"), w)
                    y = b.y.rearrange("p t (h d) -> p (t h) d", h=GH)
                    g.tensor_tensor(y, y, b.rms.unsqueeze(2).broadcast_to([P, NT * GH, GDV]), ALU.mult).then_inc(S("a_yn"), 1)

                return [gate, rms, lambda p: rstd("a", p, i)]

            with pool.Fori(0, PAIRS) as i:
                in_turn(gla_stages(i) + attn_stages(X0, i, ("a", 0), lambda b: b.xA) + store(0, i))
            scatter(1)
            pool.wait_ge(S("c_weights"), c_loads)
            for p in range(2):
                pool.wait_ge(S(f"t_out{p}"), 16 * TILES0 // 2)
            for p in range(2):
                gather(0, 1)[0](p)

            def second(i, last=False):
                ahead = [] if last else gather(i + 1, 1) + [lambda p: rstd("a", p, i + 1 + PAIRS)]
                in_turn(attn_stages(S1, i, ("a", B), lambda b: b.xA, ahead)
                        + attn_stages(X1, i, ("s", 0), lambda b: b.xB) + store(B, i))

            for p in range(2):
                rstd("a", p, PAIRS)
            with pool.Fori(0, PAIRS - 1) as i:
                second(i)
            second(PAIRS - 1, True)
            scatter(2)
            for p in range(2):
                pool.wait_ge(S(f"e_out{p}"), 16 * E // 2)
            pool.wait_ge(S("dispatched"), 4)
            for p in range(2):
                gather(0, 2)[0](p)
            with pool.Fori(0, PAIRS - 1) as i:
                in_turn(gather(i + 1, 2) + [lambda p: rstd("a", p, i + 2 * PAIRS)])
            for p in range(2):
                rstd("a", p, 3 * PAIRS - 1)

        @block.tensor
        def _(pe):
            mm, tr = nc.tensor.matmul, nc.tensor.transpose

            def attn_stages(c, loop, before, xin, inputs):
                n, wn, i = c.prefix, c.name, loop + c.pairs_before

                def turn(p):
                    b = bufs[p]
                    pe.wait_ge(S(f"{before[0]}_out"), before[1] + 2 * loop + p + 1)
                    for k in range(KC):
                        for t in range(NT):
                            ins = tr(bank(p, c.turn_bank)[:, k * L + t * P:k * L + (t + 1) * P], xin(b)[:, t, k * P:(k + 1) * P], ident[:, :])
                    ins.then_inc(S(f"{n}_xT_done"), 1)

                def feat(p, first, wt, src, rows, cols):
                    dst = bank(p, first, 2).rearrange("p a b -> p (a b)")
                    for m in range(QC):
                        for k in range(KC):
                            ins = mm(dst[:, m * cols:(m + 1) * cols], wt[0:rows[k], k, m * P:(m + 1) * P],
                                     src[0:rows[k], k, 0:cols], start=(k == 0), stop=(k == KC - 1))
                    return ins

                def project_k(p):
                    b = bufs[p]
                    if c.selfattn:
                        pe.wait_ge(S(f"{n}_xinT"), 2 * i + p + 1)
                        ins = feat(p, 0, W[f"{wn}_wk"], b.xinT, (P, P), L)
                    else:
                        pe.wait_ge(S(f"{inputs}{p}"), (64 if inputs == "a_in" else 32) * (loop + 1))
                        ins = feat(p, 0, W[f"{wn}_wk"], b.ctxT, (P, DC - P), M)
                    ins.then_inc(S(f"{n}_kv"), 1)

                def project_q(p):
                    pe.wait_ge(S(f"{n}_xinT"), 2 * i + p + 1)
                    if c.selfattn:
                        pe.wait_ge(S("logits"), B + 2 * loop + p + 1)
                    feat(p, 2, W[f"{wn}_wq"], bufs[p].xinT, (P, P), L).then_inc(S(f"{n}_q"), 1)

                def project_v(p):
                    b, w = bufs[p], 2 * i + p + 1
                    if c.selfattn:
                        pe.wait_ge(S(f"{n}_qh"), 2 * w)
                    for t in range(c.key_tiles):
                        for k in range(KC):
                            if c.selfattn:
                                ins = mm(bank(p, 2)[:, t * D:(t + 1) * D], b.xinT[:, k, t * P:(t + 1) * P], W[f"{wn}_wv"][:, k, :],
                                         start=(k == 0), stop=(k == KC - 1))
                            else:
                                rows = (P, DC - P)[k]
                                ins = mm(bank(p, 1)[0:M, 0:D], b.ctxT[0:rows, k, 0:M], W[f"{wn}_wv"][0:rows, k, :],
                                         start=(k == 0), stop=(k == KC - 1))
                    ins.then_inc(S(f"{n}_kv"), 1)

                def scores(p):
                    b, w = bufs[p], 2 * i + p + 1
                    kb = b.KB if c.selfattn else b.KBm
                    pe.wait_ge(S(f"{n}_qh"), 2 * w)
                    pe.wait_ge(S(f"{n}_va"), w)
                    per = c.rounds // NT
                    for r in range(c.rounds):
                        t, g = r // per, r % per
                        if t == 0:
                            last = ((2 * g + 2) * c.bank_heads - 1) // HC
                            pe.wait_ge(S(f"{n}_KB"), QC * (w - 1) + last + 1)
                        if r >= 2:
                            pe.wait_ge(S(f"{n}_Smax"), c.rounds * (2 * i + p) + r - 1)
                        for j in range(2):
                            h = (2 * g + j) * c.bank_heads
                            k, hh = h // HC, h % HC
                            dst = bank(p, 2 * (r % 2) + j)
                            ins = mm(dst[:, 0:c.bank_heads * c.nk], b.qh[:, k, t * P:(t + 1) * P],
                                     kb[:, k, hh:hh + c.bank_heads, :].rearrange("p h k -> p (h k)"),
                                     start=True, stop=not c.selfattn)
                            if c.selfattn:
                                for a in range(c.bank_heads):
                                    ins = mm(dst[:, a * L + (1 - t) * P:a * L + (2 - t) * P], identb[:, :], winmask[:, t, :],
                                             start=False, stop=(a == c.bank_heads - 1))
                        ins.then_inc(S(f"{n}_S"), 1)

                def shift(p):
                    b = bufs[p]
                    pe.wait_ge(S(f"{n}_nmb"), 2 * i + p + 1)
                    for t in range(NT):
                        ins = mm(bank(p, 3)[0:3 * H, t * P:(t + 1) * P], b.nmb[:, t].rearrange("p a h -> p (a h)"), identb[:, :],
                                 start=True, stop=True)
                    ins.then_inc(S(f"{n}_nmT_done"), 1)

                def attend():
                    def products(p, u):
                        b = bufs[p]
                        kb = b.KB if c.selfattn else b.KBm
                        if u < 2:
                            pe.wait_ge(S(f"{n}_Smax"), c.rounds * (2 * i + p + 1))
                            pe.wait_ge(S(f"{n}_qs"), 2 * i + p + 1)
                        else:
                            pe.wait_ge(S(f"{n}_PT"), 2 * c.units * i + 2 * (u - 2) + p + 1)
                        for a in range(2):
                            h = u if c.selfattn else 2 * u + a
                            kt = a if c.selfattn else 0
                            k, hh = h // HC, h % HC
                            cols = bank(p, u % 2)[0:c.keys, a * L:(a + 1) * L]
                            key = kb[:, k, hh, kt * P:kt * P + c.keys]
                            mm(cols, key, b.qh[:, k, :], start=(a == 0), stop=False, skip_group_check=True)
                            ins = mm(cols, key, b.ql[:, k, :], start=False, stop=c.clip, skip_group_check=True)
                            if c.selfattn:
                                ins = mm(cols[:, (1 - kt) * P:(2 - kt) * P], identb[:, :], winmask[:, kt, :], start=False, stop=False,
                                         skip_group_check=True)
                        if c.clip:
                            ins.then_inc(S(f"{n}_ST0"), 1)

                    def shifted(p, u):
                        if c.clip:
                            pe.wait_ge(S(f"{n}_clip"), 2 * c.units * loop + 2 * u + p + 1)
                        for a in range(2):
                            h = u if c.selfattn else 2 * u + a
                            ins = mm(bank(p, u % 2)[0:c.keys, a * L:(a + 1) * L], headrow[:, h, 0:c.keys], bufs[p].nmT,
                                     start=False, stop=True, skip_group_check=True)
                        ins.then_inc(S(f"{n}_ST"), 1)

                    def values(p, u0):
                        b = bufs[p]
                        pe.wait_ge(S(f"{n}_PT"), 2 * c.units * i + 2 * (u0 + c.units_at_once - 1) + p + 1)
                        for kt in range(c.key_tiles):
                            for j in range(4):
                                h = u0 * c.unit_heads + j
                                u, gg = h // c.unit_heads, h // 4
                                half = kt if c.selfattn else h % 2
                                ins = mm(bank(p, 2 + gg // 2)[32 * j:32 * j + 32, (gg % 2) * L:(gg % 2 + 1) * L],
                                         b.va[0:c.keys, kt, h, :], b.PT[0:c.keys, u % c.PT_units, half * L:(half + 1) * L],
                                         start=(kt == 0), stop=(kt == c.key_tiles - 1))
                        return ins

                    for p, u in ((0, 0), (1, 0), (0, 1), (1, 1)) if c.clip else ((0, 0), (0, 1), (1, 0), (1, 1)):
                        products(p, u)
                    for p in range(2):
                        shift(p)
                    for p in range(2):
                        pe.wait_ge(S(f"{n}_nmT"), 2 * i + p + 1)
                        shifted(p, 0)
                    for u in range(c.units):
                        for p in range(2):
                            if u + 1 < c.units:
                                shifted(p, u + 1)
                        for p in range(2):
                            if u + 2 < c.units:
                                products(p, u + 2)
                        if (u + 1) % c.units_at_once == 0:
                            for p in range(2):
                                ins = values(p, u + 1 - c.units_at_once)
                                if u + 1 == c.units:
                                    ins.then_inc(S(f"{n}_OT_done"), 1)

                def untranspose(p):
                    b, w = bufs[p], 2 * i + p + 1
                    pe.wait_ge(S(f"{n}_OT"), w)
                    for t in range(NT):
                        for gg in range(4):
                            ins = tr(bank(p, t)[:, gg * P:(gg + 1) * P], b.OT[:, gg, t * P:(t + 1) * P], ident[:, :])
                    ins.then_inc(S(f"{n}_O"), 1)

                def turn_out(p):
                    b, w = bufs[p], 2 * i + p + 1
                    pe.wait_ge(S(f"{n}_on"), w)
                    for k in range(KC):
                        for t in range(NT):
                            ins = tr(bank(p, 2)[:, k * L + t * P:k * L + (t + 1) * P], b.on[:, t, k * P:(k + 1) * P], ident[:, :])
                    ins.then_inc(S(f"{n}_onT_done"), 1)

                def project_out(p):
                    b, w = bufs[p], 2 * i + p + 1
                    pe.wait_ge(S(f"{n}_onT"), w)
                    for t in range(NT):
                        for k in range(KC):
                            ins = mm(bank(p, 3)[:, t * D:(t + 1) * D], b.onT[:, k, t * P:(t + 1) * P], W[f"{wn}_wo"][:, k, :],
                                     start=(k == 0), stop=(k == KC - 1))
                    ins.then_inc(S(f"{n}_wo"), 1)

                if c.selfattn:
                    first = [turn, project_k, project_q, project_v]
                else:
                    first = [project_k, project_v, turn, project_q]
                return first + [scores, Both(attend), untranspose, turn_out, project_out]

            def out_stages(first, r, i):
                def turn(p):
                    b, w = bufs[p], 2 * i + p + 1
                    pe.wait_ge(S("x_out"), first + w)
                    for k in range(KC):
                        for t in range(NT):
                            ins = tr(bank(p, 2)[:, k * L + t * P:k * L + (t + 1) * P], b.xo[:, t, k * P:(k + 1) * P], ident[:, :])
                    ins.then_inc(S("xoT_done"), 1)

                def route(p):
                    b, w = bufs[p], 2 * i + p + 1
                    pe.wait_ge(S("xoT"), first + w)
                    for t in range(NT):
                        for k in range(KC):
                            ins = mm(bank(p, 3)[:, t * E:(t + 1) * E], b.xoT[:, k, t * P:(t + 1) * P], r[:, k, :],
                                     start=(k == 0), stop=(k == KC - 1))
                    ins.then_inc(S("logits_done"), 1)

                return [turn, route]

            def gla_stages(i):
                def keys(p):
                    b, w = bufs[p], 2 * i + p + 1
                    pe.wait_ge(S(f"a_in{p}"), 64 * (i + 1))
                    pe.wait_ge(S("logits"), w)
                    for k in range(KC):
                        ins = mm(bank(p, 2)[0:LOWRANK, 0:L], W["a_w1"][:, k, :], b.xT[:, k, :], start=(k == 0), stop=(k == KC - 1))
                    ins.then_inc(S("a_g1_done"), 1)
                    for n, wt in enumerate(("a_wq", "a_wk")):
                        for m in range(KC):
                            for k in range(KC):
                                ins = mm(bank(p, n)[:, m * L:(m + 1) * L], W[wt][:, k, m * P:(m + 1) * P], b.xT[:, k, :],
                                         start=(k == 0), stop=(k == KC - 1))
                    ins.then_inc(S("a_qk"), 1)

                def decay(p):
                    b, w = bufs[p], 2 * i + p + 1
                    pe.wait_ge(S("a_g1"), w)
                    for m in range(KC):
                        ins = mm(bank(p, 3)[:, m * L:(m + 1) * L], W["a_w2"][:, m * P:(m + 1) * P], b.g1, start=True, stop=True)
                    ins.then_inc(S("a_z"), 1)

                def tokens(wt, signal):
                    def stage(p):
                        b, w = bufs[p], 2 * i + p + 1
                        pe.wait_ge(S("a_zb" if wt == "a_wv" else "a_vs"), w)
                        for t in range(NT):
                            for k in range(KC):
                                ins = mm(bank(p, 2 + t), b.xT[:, k, t * P:(t + 1) * P], W[wt][:, k, :],
                                         start=(k == 0), stop=(k == KC - 1))
                        ins.then_inc(S(signal), 1)
                    return stage

                def scores(p):
                    b, w = bufs[p], 2 * i + p + 1
                    pe.wait_ge(S("a_scaled"), w)
                    pe.wait_ge(S("a_gate"), w)
                    for h in range(GH):
                        k, r = h // 2, slice(GDK * (h % 2), GDK * (h % 2) + GDK)
                        for a, (key, qry) in enumerate(((b.kd[r, k, 0:P], b.qd[r, k, 0:P]), (b.kd[r, k, P:L], b.qd[r, k, P:L]),
                                                        (b.kd[r, k, 0:P], b.qx[r, k, :]))):
                            ins = mm(bank(p, h)[:, a * P:(a + 1) * P], key, qry, start=True, stop=True)
                    ins.then_inc(S("a_A"), 1)

                def mix(p):
                    b, w = bufs[p], 2 * i + p + 1
                    pe.wait_ge(S("a_AT"), w)
                    for h in range(GH):
                        c = slice(h * GDV, (h + 1) * GDV)
                        mm(bank(p, 0)[:, c], b.AT[:, 3 * h, :], b.v[:, 0, c], start=True, stop=True)
                        mm(bank(p, 1)[:, c], b.AT[:, 3 * h + 2, :], b.v[:, 0, c], start=True, stop=False)
                        ins = mm(bank(p, 1)[:, c], b.AT[:, 3 * h + 1, :], b.v[:, 1, c], start=False, stop=True)
                    ins.then_inc(S("a_o"), 1)

                def turn(p):
                    b, w = bufs[p], 2 * i + p + 1
                    pe.wait_ge(S("a_yn"), w)
                    for t in range(NT):
                        for k in range(VC):
                            ins = tr(bank(p, 2 + t)[:, k * P:(k + 1) * P], b.y[:, t, k * P:(k + 1) * P], ident[:, :])
                    ins.then_inc(S("a_yT_done"), 1)

                def project_out(p):
                    b, w = bufs[p], 2 * i + p + 1
                    pe.wait_ge(S("a_yT"), w)
                    for t in range(NT):
                        for k in range(VC):
                            ins = mm(bank(p, 3)[:, t * D:(t + 1) * D], b.yT[:, t, k * P:(k + 1) * P], W["a_wo"][:, k, :],
                                     start=(k == 0), stop=(k == VC - 1))
                    ins.then_inc(S("a_wo"), 1)

                return [keys, decay, tokens("a_wv", "a_v"), tokens("a_wg", "a_g"), scores, mix, turn, project_out]

            pe.wait_ge(S("a_weights"), a_loads)
            with pe.Fori(0, PAIRS) as i:
                in_turn(gla_stages(i) + attn_stages(X0, i, ("a", 0), lambda b: b.xA, "a_in") + out_stages(0, r0, i))

            def count(nth):
                pe.wait_ge(S("chosen"), nth)
                chosen = masked[:, :, :].rearrange("p t e -> p (t e)")
                mm(ps[:, 4, 0:P], causal[:, 0, :], chosen, start=True, stop=True)
                mm(ps[:, 4, P:2 * P], onemat[:, :], chosen, start=True, stop=True).then_inc(S("counted"), 1)

            def turn0(p, h):
                pe.wait_ge(S(f"t_in{p}"), 16 * (h + 1))
                for k in range(KC):
                    ins = tr(bank(p, 2)[:, k * P:(k + 1) * P], slots0[p].x[:, k * P:(k + 1) * P], ident[:, :])
                ins.then_inc(S("t_X"), 1)

            def expert_of(j):
                return pe.value_load(owner_i[0:1, bass.ds(j, 1)], min_val=0, max_val=E - 1)

            def weights0(e, off, n):
                return ew[:, bass.ds(e, 1), off:off + n].rearrange("p a n -> p (a n)")

            def hidden0(p, e, a, signal):
                for k in range(KC):
                    ins = mm(bank(p, a), slots0[p].xT[:, k, :], weights0(e, a * KC * FH + k * FH, FH), start=(k == 0), stop=(k == KC - 1))
                ins.then_inc(S(signal), 1)

            def turn_hidden0(j, p):
                pe.wait_ge(S("t_h"), j + 1)
                for m in range(MC):
                    ins = tr(bank(p, 2)[:, m * P:(m + 1) * P], slots0[p].h[:, m * P:(m + 1) * P], ident[:, :])
                ins.then_inc(S("t_H"), 1)

            def outputs0(j, p, e, first=False):
                pe.wait_ge(S("t_hT"), j + 1)
                if not first:
                    pe.wait_ge(S("t_ys"), j - 1)
                for m in range(MC):
                    ins = mm(bank(p, 3)[:, 0:D], slots0[p].hT[:, m, :], weights0(e, 2 * KC * FH + m * D, D), start=(m == 0), stop=(m == MC - 1))
                ins.then_inc(S("t_y"), 1)

            def tile0(j, p, h, before=None, first=False, last=False):
                e = expert_of(j)
                before = expert_of(j - 1) if before is None else before
                pe.wait_ge(S("t_xT"), j + 1)
                hidden0(p, e, 0, "t_u")
                turn_hidden0(j - 1, 1 - p)
                hidden0(p, e, 1, "t_v")
                if not last:
                    pe.wait_ge(S("t_hT"), j)
                    turn0(1 - p, h)
                outputs0(j - 1, 1 - p, before, first)
                return e

            count(1)
            pe.wait_ge(S("t_w"), 16 * 3 * E)
            pe.wait_ge(S("dispatched"), 2)
            turn0(0, 0)
            turn0(1, 0)
            e = expert_of(0)
            pe.wait_ge(S("t_xT"), 1)
            hidden0(0, e, 0, "t_u")
            hidden0(0, e, 1, "t_v")
            e = tile0(1, 1, 1, e, True)
            tile0(2, 0, 1, e, True)
            with pe.Fori(1, TILES0 // 2 - 1) as i:
                e = tile0(2 * i + 1, 1, i + 1)
                tile0(2 * i + 2, 0, i + 1, e)
            e = tile0(TILES0 - 1, 1, 0, last=True)
            turn_hidden0(TILES0 - 1, 1)
            outputs0(TILES0 - 1, 1, e)

            pe.wait_ge(S("c_weights"), c_loads)
            with pe.Fori(0, PAIRS) as i:
                in_turn(attn_stages(S1, i, ("a", B), lambda b: b.xA, "") + attn_stages(X1, i, ("s", 0), lambda b: b.xB, "c_in") \
                        + out_stages(B, r1, i))

            def turn1(p, h):
                pe.wait_ge(S(f"e_in{p}"), 16 * (h + 1))
                for k in range(KC):
                    for t in range(ST1):
                        ins = tr(ps[:, k, t * P:(t + 1) * P], experts1[p].x[:, t, k * P:(k + 1) * P], ident[:, :])
                ins.then_inc(S("e_X"), 1)

            def expert1(e, p, h, first=False, last=False):
                b = experts1[p]
                pe.wait_ge(S(f"e_w{p}"), 64 * (h + 1))
                pe.wait_ge(S("e_xT"), e + 1)
                for m in range(KC):
                    for k in range(KC):
                        ins = mm(ps[:, 2 + m, 0:SLOTS1], b.w1[:, k, m * P:(m + 1) * P], b.xT[:, k, :], start=(k == 0), stop=(k == KC - 1))
                    ins.then_inc(S("e_u"), 1)
                if not last:
                    turn1(1 - p, h + p)
                pe.wait_ge(S("e_h"), KC * (e + 1))
                if not first:
                    pe.wait_ge(S("e_ys"), e - 1)
                for t in range(ST1):
                    for m in range(KC):
                        ins = mm(ps[:, 4 + 2 * p + t // 2, (t % 2) * D:(t % 2 + 1) * D], b.hid[:, m, t * P:(t + 1) * P], b.w2[:, m, :],
                                 start=(m == 0), stop=(m == KC - 1))
                ins.then_inc(S("e_y"), 1)

            count(2)
            turn1(0, 0)
            for p in range(2):
                expert1(p, p, 0, True)
            with pe.Fori(1, E // 2 - 1) as i:
                for p in range(2):
                    expert1(2 * i + p, p, i)
            expert1(E - 2, 0, E // 2 - 1)
            expert1(E - 1, 1, E // 2 - 1, last=True)


def kernel(**inputs):
    import concourse.bacc as bacc
    from concourse.bass_utils import run_bass_kernel_spmd
    import ml_dtypes

    a = {k: np.asarray(v) for k, v in inputs.items()}
    bf = ml_dtypes.bfloat16

    def chunk(w):
        return w.reshape(-1, P, w.shape[-1]).transpose(1, 0, 2)

    def cols(v):
        return v.reshape(-1, P).T

    d = {"x": a["x"].reshape(B, NT, P, D), "xT": a["x"].transpose(0, 2, 1).reshape(B, KC, P, L),
         "ctxT": a["ctx_768"].transpose(0, 2, 1)}
    for n, k in (("wq", "Wq"), ("wk", "Wk"), ("wv", "Wv"), ("wg", "Wg"), ("w1", "gk_w1"), ("wo", "Wo")):
        d["a_" + n] = chunk(a["L0_attn_" + k])
    d["a_w2"] = a["L0_attn_gk_w2"]
    d["a_b2"] = cols(a["L0_attn_gk_b2"])
    d["a_gn"] = a["L0_attn_g_norm_w"][None]
    wkv = a["L0_xattn_Wkv"].reshape(H, 2, DH, DC)
    bkv = a["L0_xattn_bkv"].reshape(H, 2, DH)
    layers = {
        "x0": {"wq": a["L0_xattn_Wq"].T, "wk": wkv[:, 0].reshape(D, DC).T, "wv": wkv[:, 1].reshape(D, DC).T,
               "wo": a["L0_xattn_Wo"].T, "bq": a["L0_xattn_bq"], "bk": bkv[:, 0].reshape(D), "bv": bkv[:, 1].reshape(D),
               "bo": a["L0_xattn_bo"]},
        "s1": {n.lower(): a["L1_attn_" + n] for n in ("Wq", "Wk", "Wv", "Wo", "bq", "bk", "bv", "bo")},
        "x1": {n.lower(): a["L1_xattn_" + n] for n in ("Wq", "Wk", "Wv", "Wo", "bq", "bk", "bv", "bo")},
    }
    twice = np.broadcast_to(np.arange(D).reshape(H, 1, DH), (H, 2, DH)).reshape(2 * D)
    for x, w in layers.items():
        for n, t in w.items():
            if n[1] in "qk":
                t = t[..., twice]
            if n[0] == "w":
                d[f"{x}_{n}"] = chunk(t) if t.shape[0] % P == 0 else t
            else:
                d[f"{x}_{n}"] = cols(t) if n in ("bq", "bk") else t[None]
    d["r0"] = chunk(a["L0_ffn_Wg"])
    d["r1"] = chunk(a["L1_ffn_gate_w"].T)
    d["m1_b1"] = a["L1_ffn_b1"].reshape(E, KC, P).transpose(0, 2, 1)
    d["m1_b2"] = a["L1_ffn_b2"].reshape(E, 1, D)
    d["m0_w1"] = a["L0_ffn_W1"].reshape(E, KC, P, FH)
    d["m0_w2"] = a["L0_ffn_W2"].reshape(E, KC, P, FH)
    d["m0_w3"] = a["L0_ffn_W3"].reshape(E, MC, P, D)
    d["m1_w1"] = a["L1_ffn_w1"].transpose(0, 2, 1).reshape(E, KC, P, D)
    d["m1_w2"] = a["L1_ffn_w2"].transpose(0, 2, 1).reshape(E, KC, P, D)
    r = np.arange(P)
    upper = (r[None, :] >= r[:, None]).astype(np.float32)
    d["ident"] = np.eye(P, dtype=np.float32)
    d["identb"] = np.eye(P, dtype=bf)
    d["causal"] = np.stack([upper, upper, np.ones((P, P), np.float32)], 1)
    d["rowmask"] = (r[:, None] // (2 * DH) == np.arange(HC)[None]).astype(np.float32)
    low = (r // DH % 2).astype(np.float32)
    d["lowrow"] = np.stack([low, 1 - 2 * low], 1)
    d["headrow"] = np.broadcast_to((np.arange(3 * H)[:, None] % H == np.arange(H)[None])[:, :, None], (3 * H, H, P)).astype(bf)
    d["winmask"] = np.stack([np.where(r[None, :] > r[:, None], -BIG, 0), np.where(r[None, :] < r[:, None], -BIG, 0)], 1).astype(bf)
    d["tiebreak"] = np.broadcast_to(E - np.arange(E, dtype=np.float32), (P, TILES, E))

    tiles = np.arange(TILES)
    d["scan_reset"] = np.broadcast_to(np.tile(tiles > 0, E).astype(np.float32), (P, E * TILES))
    d["tile_start"] = np.broadcast_to((tiles * P).astype(np.float32), (P, TILES))
    d["tile_no"] = np.broadcast_to(np.arange(TILES0, dtype=np.float32), (P, TILES0))
    d["base1"] = np.broadcast_to(SLOTS1 * np.arange(E, dtype=np.float32), (P, E))
    d["trash"] = (TRASH + 2 * (tiles[None, None] * P + r[:, None, None]) + np.arange(2)[None, :, None]).astype(np.float32)

    nc = bacc.Bacc("TRN2", target_bir_lowering=False, num_devices=1)
    arrays, dram = {}, {}
    for n, t in d.items():
        t = np.ascontiguousarray(t)
        arrays["in_" + n] = t
        dram[n] = nc.dram_tensor("in_" + n, t.shape, mybir.dt.from_np(t.dtype), kind="ExternalInput").ap()
    out = nc.dram_tensor("out_x", (B, NT, P, D), F32, kind="ExternalOutput").ap()
    rows_in = nc.dram_tensor("rows_in", (ROWS, D), F32, kind="Internal").ap()
    rows_out = nc.dram_tensor("rows_out", (TILES0 * P, D), F32, kind="Internal").ap()
    build_program(nc, dram, out, rows_in, rows_out)
    r = run_bass_kernel_spmd(nc, [arrays], core_ids=[0])
    return r.results[0]["out_x"].reshape(B, L, D)
```

```python
from contextlib import ExitStack

import numpy as np

import concourse.bass as bass
from concourse import mybir

F32 = mybir.dt.float32
F32R = mybir.dt.float32r
I32 = mybir.dt.int32
BF16 = mybir.dt.bfloat16
ALU = mybir.AluOpType
ACT = mybir.ActivationFunctionType
AX = mybir.AxisListType

P = 128
B, L, D = 8, 256, 256
NT = L // P
KC = D // P
TILES = B * NT
PAIRS = B // 2
M, DC = 77, 192
GH, GDK, GDV = 4, 64, 128
VD = GH * GDV
VC = VD // P
LOWRANK = 16
GATE_NORM = 16.0
H, DH = 16, 16
HC = P // (2 * DH)
QC = H // HC
QSCALE = DH ** -0.5
E, FH = 8, 512
MC = FH // P
TILES0 = (2 * TILES * P + E * (P - 1)) // P
assert TILES0 % 4 == 3
SLOTS1 = 384
ST1 = SLOTS1 // P
CAP = int(1.25 * B * L / E)
assert CAP <= SLOTS1
EARLY = TILES - 2 * NT
TRASH = E * SLOTS1
ROWS = max(TILES0 * P, TRASH + 2 * B * L)
assert TRASH <= TILES0 * P
CLAMP = 10000.0
EPS = 1e-5
BIG = 1e30


class Attn:

    def __init__(self, name, prefix, before, selfattn, clip):
        self.name, self.selfattn, self.clip = name, selfattn, clip
        self.prefix, self.pairs_before = prefix, before
        self.keys = P if selfattn else M
        self.key_tiles = NT if selfattn else 1
        self.nk = self.keys * self.key_tiles
        self.bank_heads = 2 if selfattn else 4
        self.turn_bank = 1 if selfattn else 2
        self.rounds = NT * H // (2 * self.bank_heads)
        self.unit_heads = 1 if selfattn else 2
        self.units = H // self.unit_heads
        self.units_at_once = 4 // self.unit_heads
        self.PT_units = 2 * self.units_at_once


class Both:

    def __init__(self, steps):
        self.steps = steps


def in_turn(stages):
    for stage in stages:
        if isinstance(stage, Both):
            stage.steps()
        else:
            for p in range(2):
                stage(p)


X0 = Attn("x0", "x", 0, False, False)
S1 = Attn("s1", "s", 0, True, False)
X1 = Attn("x1", "x", PAIRS, False, True)


def build_program(nc, dram, out, rows_in, rows_out):
    with ExitStack() as ctx:
        def sb(name, shape, dt=F32):
            return ctx.enter_context(nc.sbuf_tensor("sb_" + name, shape, dt))

        sems = {}

        def S(name):
            if name not in sems:
                sems[name] = ctx.enter_context(nc.semaphore(name))
            return sems[name]

        ident = sb("ident", [P, P])
        causal = sb("causal", [P, 3, P])
        rowmask = sb("rowmask", [P, HC])
        lowrow = sb("lowrow", [P, 2])
        headrow = sb("headrow", [3 * H, H, P], BF16)
        identb = sb("identb", [P, P], BF16)
        winmask = sb("winmask", [P, 2, P], BF16)
        tiebreak = sb("tiebreak", [P, TILES, E])
        onemat = sb("onemat", [P, P])
        ones = sb("ones", [P, L])
        neghalf = sb("neghalf", [P, 8])
        eps = sb("eps", [P, 8])
        ptick = sb("ptick", [P, 1])
        tick = sb("tick", [P, 1])
        r0, r1 = sb("r0", [P, KC, E]), sb("r1", [P, KC, E])
        zeros = sb("zeros", [P, D])
        scan_reset = sb("scan_reset", [P, E * TILES])
        tile_start = sb("tile_start", [P, TILES])
        tile_no = sb("tile_no", [P, TILES0])
        base1 = sb("base1", [P, E])
        trash = sb("trash", [P, 2, TILES])
        always = {"ident": ident, "causal": causal, "rowmask": rowmask, "lowrow": lowrow, "headrow": headrow, "identb": identb,
                  "winmask": winmask, "tiebreak": tiebreak, "r0": r0, "r1": r1, "scan_reset": scan_reset, "tile_start": tile_start, "tile_no": tile_no, "base1": base1, "trash": trash}
        always = {n: t[:] for n, t in always.items()}

        xres = sb("xres", [P, TILES, D])
        logits = sb("logits", [P, TILES, E])
        wts = sb("wts", [P, 2, TILES])
        hot = sb("hot", [P, 2, TILES, E])
        rt = sb("rt", [P, TILES, E])
        masked = sb("masked", [P, TILES, E])
        rank = sb("rank", [P, E, TILES])
        part = sb("part", [P, E, TILES])
        top = sb("top", [P, 8, TILES])
        cnt = sb("cnt", [P, 4, E])
        counts = sb("counts", [P, 2 * P])
        slot = sb("slot", [P, 2, TILES])
        keep = sb("keep", [P, 2, TILES])
        scat = sb("scat", [P, 2, TILES], I32)
        gath = sb("gath", [P, 2, TILES], I32)
        gidx = sb("gidx", [P, 2, 2, NT], I32)
        owner = sb("owner", [1, TILES0])
        owner_i = sb("owner_i", [1, TILES0], I32)
        owned = sb("owned", [1, TILES0, E])

        WREG = 8192
        wreg = sb("wreg", [P, WREG])

        def view(t, off, dims, rows=P):
            v = t[0:rows, off:off + int(np.prod(dims))]
            if len(dims) == 2:
                v = v.rearrange("p (a b) -> p a b", a=dims[0])
            if len(dims) == 3:
                v = v.rearrange("p (a b c) -> p a b c", a=dims[0], b=dims[1])
            return v

        def place(t, off, end, items):
            got = {}
            for name, dims in items:
                got[name] = view(t, off, dims)
                off += int(np.prod(dims))
            assert off <= end, (off, end)
            return got

        def attn_items(n):
            return [(f"{n}_{w}", (KC, 2 * D)) for w in ("wq", "wk")] + [(f"{n}_{w}", (KC, D)) for w in ("wv", "wo")] + \
                   [(f"{n}_{w}", (QC,)) for w in ("bq", "bk")] + [(f"{n}_{w}", (D,)) for w in ("bv", "bo")]

        w0 = place(wreg, 0, WREG, [("a_wq", (KC, D)), ("a_wk", (KC, D)), ("a_wv", (KC, VD)), ("a_wg", (KC, VD)),
                                   ("a_w1", (KC, LOWRANK)), ("a_w2", (D,)), ("a_b2", (KC,)), ("a_gn", (GDV,)),
                                   ("a_wo", (VC, D))] + attn_items("x0"))
        w1 = place(wreg, 0, WREG, attn_items("s1") + attn_items("x1"))
        W = w0 | w1
        W["a_w2"] = W["a_w2"][0:LOWRANK, :]

        COMMON, REGION = 5248, 12288
        arena = sb("arena", [P, 2 * (COMMON + REGION)])
        arena_at = nc.sbuf_base - 4 * 2 * (COMMON + REGION)
        bufs = []
        for p in range(2):
            o = p * (COMMON + REGION)
            b = place(arena, o, o + COMMON, [
                ("xT", (KC, L)), ("xtok", (NT, D)), ("ctxT", (2, M + 1)), ("xA", (NT, D)), ("xB", (NT, D)),
                ("xinT", (KC, L)), ("xb", (NT, D)), ("res", (NT, D)), ("xo", (NT, D)), ("xoT", (KC, L)),
                ("f", (KC,)), ("fx", (KC,)), ("ms", (8,)), ("rms", (8,)), ("st0", (6,)), ("st1", (6,)),
                ("mv", (NT, 2)), ("var", (NT,)), ("rstd", (NT,)), ("nm", (NT, H)), ("rec", (NT, H)),
                ("nmb", (NT * 3 * H // 2,)), ("nmr", (2 * NT * H,)), ("nmTf", (L // 2,))])
            o += COMMON
            b |= place(arena, o, o + REGION, [
                ("v", (NT, VD)), ("gw", (NT, VD)), ("th", (NT, VD)), ("zb", (KC, L)), ("la", (KC, L)),
                ("gl", (KC, L)), ("G", (KC, L)), ("qd", (KC, L)), ("kd", (KC, L)), ("qx", (KC, P)), ("g1", (L,)),
                ("AT", (GH * 3, P))])
            b |= place(arena, o + 3072, o + REGION, [("Eq", (KC, L)), ("Ek", (KC, L)), ("Dd", (KC, L))])
            b |= place(arena, o + 2048, o + REGION, [("sq", (NT, VD)), ("y", (NT, VD)), ("yT", (NT, VD))])
            b |= place(arena, o, o + REGION, [
                ("parts", (3 * QC * 2 * L,)), ("va", (NT, H, 2 * DH)), ("PT", (8, 2 * L)), ("OT", (4, L))])
            parts = nc.alloc_sbuf_tensor_at(f"sb_parts{p}", [P, 3 * QC * 2 * L], F32R, offset=arena_at + 4 * o)
            b |= place(parts, 0, 3 * QC * 2 * L, [("qh", (QC, L)), ("ql", (QC, L)), ("KB", (QC, HC, L))])
            b["KBm"] = view(parts, 2 * QC * L, (QC, HC, M))
            b |= place(arena, o + 3 * QC * 2 * L + 1024, o + REGION, [("qf", (QC, L)), ("kl", (QC, L)), ("kh", (QC, L)), ("kp", (QC, L))])
            b |= place(arena, o, o + 1024, [("onT", (KC, L)), ("on", (NT, D))])
            b["g1"] = b["g1"][0:LOWRANK, :]
            b["yg"] = view(arena, p * (COMMON + REGION), (2 * NT * D,))
            b["nmb"] = b["nmb"].bitcast(BF16).rearrange("p (t a h) -> p t a h", t=NT, a=3)
            b["nmr"] = b["nmr"].rearrange("p (a t h) -> p a t h", a=2, t=NT)
            b["nmT"] = b["nmTf"].bitcast(BF16)[0:3 * H, :]
            bufs.append(type("Bufs", (), b))
        ew = arena[:, 0:E * 3072].rearrange("p (e a) -> p e a", e=E)
        slots0, experts1 = [], []
        for p in range(2):
            o = E * 3072 + 2304 * p
            slots0.append(type("Slots", (), place(arena, o, o + 2304, [
                ("x", (D,)), ("xT", (KC, P)), ("sil", (FH,)), ("h", (FH,)), ("hT", (MC, P)), ("y", (D,))])))
            o = 4608 * p
            experts1.append(type("Expert", (), place(arena, o, o + 4608, [
                ("w1", (KC, D)), ("w2", (KC, D)), ("b1", (KC,)), ("b2", (D,)), ("x", (ST1, D)), ("xT", (KC, SLOTS1)),
                ("hid", (KC, SLOTS1)), ("y", (ST1, D))])))

        yg_all = view(arena, 2 * 4608, (B, 2 * NT * D))

        ps = ctx.enter_context(nc.psum_tensor("ps", [P, 8, 512], F32))

        def bank(p, n, k=1):
            return ps[:, 4 * p + n, :] if k == 1 else ps[:, 4 * p + n:4 * p + n + k, :]

        def halves(ap):
            return ap.rearrange("p (a b) -> p a b", a=2)

        def chunks128(ap):
            return ap.rearrange("p (a b) -> p a b", b=P)

        block = ctx.enter_context(nc.Block())

        def load_weight(eng, n, signal):
            src = dram[n]
            dst = W.get(n, always.get(n))
            if n[-2:] in ("bv", "bo") or n == "a_gn":
                src = src.broadcast_to([P, src.shape[1]])
            if n in ("x0_wk", "x0_wv", "x1_wk", "x1_wv"):
                eng.dma_start(dst[:, 0, :], src[0:P, :]).then_inc(S(signal), 16)
                eng.dma_start(dst[0:DC - P, 1, :], src[P:DC, :]).then_inc(S(signal), 16)
            else:
                eng.dma_start(dst, src).then_inc(S(signal), 16)

        x0_names = [n for n, _ in attn_items("x0")]
        first_loads = 16 * 7
        a_loads = 16 * (3 + len(always))
        x0_loads = 16 * (len(x0_names) - 1 + 2)
        c_loads = 16 * (2 * len(x0_names) + 2)

        @block.sync
        def _(sp):
            def loads(b1, p, first):
                bf = bufs[p]
                if first:
                    sp.dma_start(bf.xT, dram["xT"][b1, :, :, :].rearrange("a k p t -> (a p) k t")).then_inc(S(f"a_in{p}"), 16)
                    sp.dma_start(bf.xtok, dram["x"][b1, :, :, :].rearrange("a t p d -> (a p) t d")).then_inc(S(f"a_in{p}"), 16)
                sp.dma_start(bf.ctxT[:, 0, 0:M], dram["ctxT"][b1, 0:P, :].rearrange("a c m -> (a c) m")).then_inc(S(f"a_in{p}"), 16)
                sp.dma_start(bf.ctxT[0:DC - P, 1, 0:M], dram["ctxT"][b1, P:DC, :].rearrange("a c m -> (a c) m")).then_inc(S(f"a_in{p}"), 16)

            for n in ("a_w1", "a_wq", "a_wk"):
                load_weight(sp, n, "a_first")
            for p in range(2):
                loads(bass.ds(p, 1), p, True)
            for n in ("a_wv", "a_wg"):
                load_weight(sp, n, "a_weights")
            with sp.Fori(1, PAIRS) as i:
                for p in range(2):
                    sp.wait_ge(S("x_kv"), 4 * i + p - 1)
                    sp.wait_ge(S("a_res"), 2 * i + p - 1)
                    loads(bass.ds(2 * i + p, 1), p, True)
            sp.wait_ge(S("memsets"), 5)
            sp.dma_start(rows_in[0:TILES0 * P, :].rearrange("(t p) d -> p t d", p=P),
                         zeros[:, :].unsqueeze(1).broadcast_to([P, TILES0, D])).then_inc(S("cleared"), 16)
            sp.wait_ge(S("logits"), 2 + B)
            sp.wait_ge(S("store"), B)

            for e in range(E):
                for n, o, k in (("w1", 0, KC), ("w2", 1024, KC), ("w3", 2048, MC)):
                    sp.dma_start(ew[:, e, o:o + 1024].rearrange("p (k h) -> p k h", k=k),
                                 dram["m0_" + n][e:e + 1, :, :, :].rearrange("a k p h -> (a p) k h")).then_inc(S("t_w"), 16)

            def load_tile(j, p):
                sp.dma_start(slots0[p].x, rows_in[bass.ds(j * P, P), :]).then_inc(S(f"t_in{p}"), 16)

            def store_tile(j, p):
                sp.wait_ge(S("t_ys"), j + 1)
                sp.dma_start(rows_out[bass.ds(j * P, P), :], slots0[p].y).then_inc(S(f"t_out{p}"), 16)

            sp.wait_ge(S("scattered"), 16 * 2 * TILES)
            for p in range(2):
                load_tile(p, p)
            for n in [n for n, _ in attn_items("s1") + attn_items("x1")]:
                load_weight(sp, n, "c_weights")
            with sp.Fori(0, TILES0 // 2 - 1) as i:
                for p in range(2):
                    sp.wait_ge(S("t_X"), 2 * i + p + 1)
                    load_tile(2 * i + p + 2, p)
                    store_tile(2 * i + p, p)
            sp.wait_ge(S("t_X"), TILES0 - 2)
            load_tile(TILES0 - 1, 0)
            for j in range(TILES0 - 3, TILES0):
                store_tile(j, j % 2)
            for p in range(2):
                sp.wait_ge(S(f"t_out{p}"), 16 * (TILES0 // 2 + 1 - p))
            for p in range(2):
                loads(bass.ds(p, 1), p, False)
            with sp.Fori(1, PAIRS) as i:
                for p in range(2):
                    sp.wait_ge(S("x_out"), B + 2 * i + p - 1)
                    loads(bass.ds(2 * i + p, 1), p, False)
            sp.wait_ge(S("logits"), 2 + 2 * B)
            sp.wait_ge(S("store"), 2 * B)

            def load_expert(e, p):
                b = experts1[p]
                for n in ("w1", "w2"):
                    sp.dma_start(b.w1 if n == "w1" else b.w2,
                                 dram["m1_" + n][e, :, :, :].rearrange("a k p h -> (a p) k h")).then_inc(S(f"e_w{p}"), 16)
                sp.dma_start(b.b1, dram["m1_b1"][e, :, :].rearrange("a p k -> (a p) k")).then_inc(S(f"e_w{p}"), 16)

            def load_bias(e, p):
                b = experts1[p]
                sp.dma_start(b.b2, dram["m1_b2"][e, :, :].rearrange("a b d -> (a b) d").broadcast_to([P, D])).then_inc(S(f"e_w{p}"), 16)

            def load_rows(e, p):
                sp.dma_start(experts1[p].x, rows_in[bass.ds(e * SLOTS1, SLOTS1), :].rearrange("(t p) d -> p t d", p=P)
                             ).then_inc(S(f"e_in{p}"), 16)

            def store_rows(e, p):
                sp.wait_ge(S("e_ys"), e + 1)
                sp.dma_start(rows_out[bass.ds(e * SLOTS1, SLOTS1), :].rearrange("(t p) d -> p t d", p=P),
                             experts1[p].y).then_inc(S(f"e_out{p}"), 16)

            for p in range(2):
                load_expert(bass.ds(p, 1), p)
                load_bias(bass.ds(p, 1), p)
            sp.wait_ge(S("scattered"), 2 * 16 * 2 * TILES)
            for p in range(2):
                load_rows(p, p)
            with sp.Fori(0, E // 2 - 1) as i:
                for p in range(2):
                    sp.wait_ge(S("e_X"), 2 * i + p + 1)
                    load_rows(2 * i + p + 2, p)
                    sp.wait_ge(S("e_y"), 2 * i + p + 1)
                    load_expert(bass.ds(2 * i + p + 2, 1), p)
                    store_rows(2 * i + p, p)
                    load_bias(bass.ds(2 * i + p + 2, 1), p)
            for p in range(2):
                store_rows(E - 2 + p, p)
            for p in range(2):
                sp.wait_ge(S(f"e_out{p}"), 16 * E // 2)
            with sp.Fori(0, PAIRS) as i:
                for p in range(2):
                    sp.wait_ge(S("a_out"), 2 * B + 2 * i + p + 1)
                    sp.dma_start(out[bass.ds(2 * i + p, 1), :, :, :].rearrange("a t p d -> (a p) t d"),
                                 bufs[p].xo).then_inc(S(f"stored{p}"), 16)
            for p in range(2):
                sp.wait_ge(S(f"stored{p}"), 16 * PAIRS)

        @block.scalar
        def _(act):
            for n in ("a_w2", "a_b2", "a_gn", "x0_bq"):
                load_weight(act, n, "a_first")
            for n in always:
                load_weight(act, n, "a_weights")
            load_weight(act, "a_wo", "a_weights")
            for n in x0_names:
                if n != "x0_bq":
                    load_weight(act, n, "x0_weights")
            nc.scalar.preload_act_table_set("natural_log_exp_and_others")

            def attn_stages(c, i):
                n, wn, i = c.prefix, c.name, i + c.pairs_before

                def xinT(p):
                    act.wait_ge(S(f"{n}_xT_done"), 2 * i + p + 1)
                    nc.scalar.activation(bufs[p].xinT, halves(bank(p, c.turn_bank)), ACT.Copy).then_inc(S(f"{n}_xinT"), 1)

                def q(p):
                    act.wait_ge(S(f"{n}_q"), 2 * i + p + 1)
                    for k0 in range(0, QC, 2):
                        for dst, k in ((dst, k) for dst in (bufs[p].qh, bufs[p].qf) for k in (k0, k0 + 1)):
                            ins = nc.scalar.activation(dst[:, k, :], bank(p, 2 + k // 2)[:, k % 2 * L:(k % 2 + 1) * L], ACT.Identity,
                                                       bias=W[f"{wn}_bq"][:, k:k + 1], scale=QSCALE)
                        ins.then_inc(S(f"{n}_qh"), 1)

                def shift(p):
                    act.wait_ge(S(f"{n}_nmT_done"), 2 * i + p + 1)
                    nc.scalar.activation(bufs[p].nmT, bank(p, 3)[0:3 * H, 0:L], ACT.Copy).then_inc(S(f"{n}_nmT"), 1)

                def probs():
                    for u in range(c.units):
                        for p in range(2):
                            act.wait_ge(S(f"{n}_ST"), 2 * c.units * i + 2 * u + p + 1)
                            nc.scalar.activation(bufs[p].PT[0:c.keys, u % c.PT_units, :], bank(p, u % 2)[0:c.keys, :],
                                                 ACT.Exp).then_inc(S(f"{n}_PT"), 1)

                def heads(p):
                    act.wait_ge(S(f"{n}_OT_done"), 2 * i + p + 1)
                    nc.scalar.activation(bufs[p].OT, bank(p, 2, 2), ACT.Copy).then_inc(S(f"{n}_OT"), 1)

                def onT(p):
                    act.wait_ge(S(f"{n}_onT_done"), 2 * i + p + 1)
                    nc.scalar.activation(bufs[p].onT, halves(bank(p, 2)), ACT.Copy).then_inc(S(f"{n}_onT"), 1)

                return [xinT, q, shift, Both(probs), heads, onT]

            def out_stages(i, tile):
                def outT(p):
                    act.wait_ge(S("xoT_done"), 2 * i + p + 1)
                    nc.scalar.activation(bufs[p].xoT, halves(bank(p, 2)), ACT.Copy).then_inc(S("xoT"), 1)

                def route(p):
                    act.wait_ge(S("logits_done"), 2 * i + p + 1)
                    nc.scalar.activation(logits[:, bass.ds(tile + 2 * p, NT), :].rearrange("p t e -> p (t e)"),
                                         bank(p, 2)[:, 0:NT * E], ACT.Copy).then_inc(S("logits"), 1)

                return [outT, route]

            def gla_stages(i):
                def v(p):
                    act.wait_ge(S("a_v"), 2 * i + p + 1)
                    nc.scalar.activation(bufs[p].v, bank(p, 2, 2), ACT.Copy).then_inc(S("a_vs"), 1)

                def gate(p):
                    act.wait_ge(S("a_g"), 2 * i + p + 1)
                    nc.scalar.activation(bufs[p].th, bank(p, 2, 2), ACT.Tanh, scale=0.5).then_inc(S("a_th"), 1)

                def lowrank(p):
                    act.wait_ge(S("a_g1_done"), 2 * i + p + 1)
                    nc.scalar.activation(bufs[p].g1, bank(p, 2)[0:LOWRANK, 0:L], ACT.Copy).then_inc(S("a_g1"), 1)

                def softplus(p):
                    b = bufs[p]
                    if p == 0:
                        nc.scalar.preload_act_table_set("natural_log_exp_and_others")
                    act.wait_ge(S("a_zb"), 2 * i + p + 1)
                    nc.scalar.activation(b.la, b.zb, ACT.Abs).then_inc(S("a_log"), 1)
                    act.wait_ge(S("a_log"), 3 * (2 * i + p) + 1)
                    nc.scalar.activation(b.la, b.la, ACT.Exp, scale=-1.0).then_inc(S("a_log"), 1)
                    act.wait_ge(S("a_log"), 3 * (2 * i + p) + 2)
                    nc.scalar.activation(b.la, b.la, ACT.Ln, bias=ones[:, 0:1]).then_inc(S("a_log"), 1)

                def decay(p):
                    b = bufs[p]
                    act.wait_ge(S("a_Dd"), 2 * i + p + 1)
                    nc.scalar.activation(b.Eq, b.Dd, ACT.Exp, scale=1.0 / GATE_NORM)
                    nc.scalar.activation(b.Ek, b.Dd, ACT.Exp, scale=-1.0 / GATE_NORM)
                    nc.scalar.activation(b.fx, b.f, ACT.Exp, scale=1.0 / GATE_NORM).then_inc(S("a_decay"), 1)

                def square(p):
                    act.wait_ge(S("a_o"), 2 * i + p + 1)
                    nc.scalar.activation(bufs[p].sq, bank(p, 0, 2), ACT.Square, scale=GDV ** -0.5).then_inc(S("a_sq_yn"), 1)

                def normed(p):
                    b, w = bufs[p], 2 * i + p + 1
                    act.wait_ge(S("a_rms"), w)
                    act.wait_ge(S("a_y"), w)
                    for h in range(GH):
                        y = b.y[:, 1, h * GDV:(h + 1) * GDV]
                        ins = nc.scalar.activation(y, y, ACT.Copy, scale=b.rms[:, GH + h:GH + h + 1])
                    ins.then_inc(S("a_sq_yn"), 1)

                def yT(p):
                    act.wait_ge(S("a_yT_done"), 2 * i + p + 1)
                    nc.scalar.activation(bufs[p].yT, bank(p, 2, 2), ACT.Copy).then_inc(S("a_yT"), 1)

                return [lowrank, softplus, v, decay, gate, square, normed, yT]

            act.wait_ge(S("memsets"), 5)
            act.wait_ge(S("rescaled"), 1)
            def first_layer(i, last=False):
                in_turn(gla_stages(i)[1:] + attn_stages(X0, i) + ([] if last else gla_stages(i + 1)[:1]) + out_stages(i, 4 * i))

            in_turn(gla_stages(0)[:1])
            with act.Fori(0, PAIRS - 1) as i:
                first_layer(i)
            first_layer(PAIRS - 1, True)

            def router(nth):
                act.wait_ge(S("top2"), nth)
                nc.scalar.activation(top[:, 5, :], top[:, 4, :], ACT.Exp)
                nc.scalar.activation(rt[:, :, :], rt[:, :, :], ACT.Exp).then_inc(S("exp2"), 1)

            router(1)

            def tile0(j, p):
                b = slots0[p]
                act.wait_ge(S("t_u"), j + 1)
                nc.scalar.activation(b.sil, bank(p, 0), ACT.Silu).then_inc(S("t_sil"), 1)
                act.wait_ge(S("t_H"), j + 1)
                nc.scalar.activation(b.hT, chunks128(bank(p, 2)), ACT.Copy).then_inc(S("t_hT"), 1)

            with act.Fori(0, TILES0 // 4) as i:
                for j in range(4):
                    tile0(4 * i + j, j % 2)
            for j in range(TILES0 - TILES0 % 4, TILES0):
                tile0(j, j % 2)
            act.wait_ge(S("rescaled"), 3)

            def second_layer(i, last=False):
                in_turn(attn_stages(S1, i)[1:] + attn_stages(X1, i) + ([] if last else attn_stages(S1, i + 1)[:1]) + out_stages(i + PAIRS, 4 * i))

            in_turn(attn_stages(S1, 0)[:1])
            with act.Fori(0, PAIRS - 1) as i:
                second_layer(i)
            second_layer(PAIRS - 1, True)
            router(2)
            with act.Fori(0, E // 4) as i:
                for j in range(4):
                    p = j % 2
                    for m in range(KC):
                        if m == 0:
                            act.wait_ge(S(f"e_w{p}"), 64 * (2 * i + j // 2 + 1))
                        act.wait_ge(S("e_u"), KC * (4 * i + j) + m + 1)
                        nc.scalar.activation(experts1[p].hid[:, m, :], ps[:, 2 + m, 0:SLOTS1], ACT.Silu,
                                             bias=experts1[p].b1[:, m:m + 1]).then_inc(S("e_h"), 1)

        @block.vector
        def _(dve):
            v = nc.vector
            v.memset(onemat[:, :], 1.0).then_inc(S("memsets"), 1)
            v.memset(neghalf[:, :], -0.5).then_inc(S("memsets"), 1)
            v.memset(eps[:, :], EPS).then_inc(S("memsets"), 1)
            v.memset(ones[:, :], 1.0).then_inc(S("memsets"), 1)
            v.memset(zeros[:, :], 0.0).then_inc(S("memsets"), 1)
            v.memset(cnt[:, 0, 3:4], 0.0).then_inc(S("logits"), 2)

            def scale_bias(names, signal):
                for k, n in enumerate(names):
                    ins = v.tensor_scalar(W[n], W[n], QSCALE, None, ALU.mult)
                ins.then_inc(S(signal), 1)

            dve.wait_ge(S("a_first"), first_loads)
            scale_bias(["x0_bq"], "rescaled")
            v.tensor_scalar(W["a_gn"], W["a_gn"], 0.5, None, ALU.mult).then_inc(S("rescaled"), 1)

            def layernorm(n, p, i, src, dst):
                b = bufs[p]
                w = 2 * i + p + 1
                dve.wait_ge(S(f"{n}_res"), w)
                v.bn_stats(b.st0, src[:, 0, :])
                v.bn_stats(b.st1, src[:, 1, :]).then_inc(S(f"{n}_stats"), 1)
                dve.wait_ge(S(f"{n}_stats"), w)
                v.memset(tick[:, :], 0.0)
                v.bn_aggr(b.mv[:, 0, :], b.st0)
                v.bn_aggr(b.mv[:, 1, :], b.st1).then_inc(S(f"{n}_mv"), 1)

            def normalise(n, p, i, src, dst):
                b = bufs[p]
                dve.wait_ge(S(f"{n}_rstd"), 2 * i + p + 1)
                for t in range(NT):
                    ins = v.tensor_scalar(dst[:, t, :], src[:, t, :], b.mv[:, t, 0:1], b.rstd[:, t:t + 1],
                                          ALU.subtract, ALU.mult)
                ins.then_inc(S(f"{n}_out"), 1)

            def attn_stages(c, loop, xout, between=(), behind_values=()):
                n, wn, i = c.prefix, c.name, loop + c.pairs_before

                def keys(p):
                    b, w = bufs[p], 2 * i + p + 1
                    dve.wait_ge(S(f"{n}_kv"), 4 * i + p + 1)
                    kp = bank(p, 0, 2).rearrange("p a b -> p (a b)")[:, 0:QC * c.nk].rearrange("p (a b) -> p a b", a=QC)
                    kl, kh, parts = b.kl[:, :, 0:c.nk], b.kh[:, :, 0:c.nk], b.kp[:, :, 0:c.nk]
                    v.tensor_tensor(kh.bitcast(F32R), kp, W[f"{wn}_bk"].unsqueeze(2).broadcast_to([P, QC, c.nk]), ALU.add)
                    for k in range(QC):
                        ins = v.tensor_scalar(kl[:, k, :], kp[:, k, :], W[f"{wn}_bk"][:, k:k + 1], lowrow[:, 0:1], ALU.add, ALU.mult)
                    ins.then_inc(S(f"{n}_kT"), 1)
                    dve.wait_ge(S(f"{n}_kT"), 2 * w - 1)
                    v.scalar_tensor_tensor(out=parts.bitcast(F32R), in0=kh, scalar=lowrow[:, 1:2], in1=kl,
                                           op0=ALU.mult, op1=ALU.add).then_inc(S(f"{n}_kT"), 1)
                    for t in range(c.key_tiles):
                        v.memset(b.va[0:c.keys, t, :, DH:DH + 1], 1.0)
                        v.memset(b.va[0:c.keys, t, :, DH + 1:2 * DH], 0.0)

                def values(p):
                    b, w = bufs[p], 2 * i + p + 1
                    dve.wait_ge(S(f"{n}_kv"), 4 * i + 2 + p + 1)
                    bv = W[f"{wn}_bv"].rearrange("p (h d) -> p h d", h=H)
                    for t in range(c.key_tiles):
                        vp = halves(bank(p, 2))[:, t, :] if c.selfattn else bank(p, 1)[:, 0:D]
                        ins = v.tensor_tensor(b.va[0:c.keys, t, :, 0:DH], vp.rearrange("p (h d) -> p h d", h=H)[0:c.keys],
                                        bv[0:c.keys], ALU.add)
                    ins.then_inc(S(f"{n}_va"), 1)

                def maxima(p):
                    b, w = bufs[p], 2 * i + p + 1
                    per = c.rounds // NT
                    hr = 2 * c.bank_heads
                    for r in range(c.rounds):
                        t, g = r // per, r % per
                        dve.wait_ge(S(f"{n}_S"), c.rounds * (2 * i + p) + r + 1)
                        src = bank(p, 2 * (r % 2), 2)[:, :, 0:c.bank_heads * c.nk].rearrange("p a (h k) -> p a h k", k=c.nk)
                        v.tensor_reduce(b.nm[:, t, g * hr:(g + 1) * hr].rearrange("p (a h) -> p a h", a=2), src,
                                        axis=AX.X, op=ALU.max, negate=True).then_inc(S(f"{n}_Smax"), 1)

                def split():
                    def step(k, p):
                        return S(f"{n}_nm"), 8 * i + 2 * k + p + 1

                    for p in range(2):
                        b = bufs[p]
                        dve.wait_ge(S(f"{n}_Smax"), c.rounds * (2 * i + p + 1))
                        if c.clip:
                            ins = v.tensor_scalar(b.nmr[:, 0], b.nm, CLAMP, -CLAMP, ALU.min, ALU.max)
                        else:
                            ins = v.tensor_copy(b.nmr[:, 0], b.nm)
                        ins.then_inc(S(f"{n}_nm"), 1)
                    for p in range(2):
                        b = bufs[p]
                        dve.wait_ge(*step(0, p))
                        v.tensor_copy(b.nmb[:, :, 0, :], b.nmr[:, 0]).then_inc(S(f"{n}_nm"), 1)
                    for p in range(2):
                        b = bufs[p]
                        dve.wait_ge(*step(1, p))
                        v.tensor_tensor(b.nmr[:, 1], b.nmr[:, 0], b.nmb[:, :, 0, :], ALU.subtract).then_inc(S(f"{n}_nm"), 1)
                    for p in range(2):
                        b = bufs[p]
                        dve.wait_ge(*step(2, p))
                        v.tensor_copy(b.nmb[:, :, 1, :], b.nmr[:, 1]).then_inc(S(f"{n}_nm"), 1)
                    for p in range(2):
                        b = bufs[p]
                        dve.wait_ge(*step(3, p))
                        v.tensor_tensor(b.nmb[:, :, 2, :], b.nmr[:, 1], b.nmb[:, :, 1, :], ALU.subtract).then_inc(S(f"{n}_nmb"), 1)

                def clip():
                    for u in range(c.units):
                        for p in range(2):
                            dve.wait_ge(S(f"{n}_ST0"), 2 * c.units * loop + 2 * u + p + 1)
                            sc = bank(p, u % 2)[0:c.keys, :]
                            v.tensor_scalar(sc, sc, CLAMP, -CLAMP, ALU.min, ALU.max).then_inc(S(f"{n}_clip"), 1)

                def norm(p):
                    b, w = bufs[p], 2 * i + p + 1
                    dve.wait_ge(S(f"{n}_O"), w)
                    o = bank(p, 0, 2).rearrange("p t (h x) -> p t h x", x=2 * DH)
                    v.reciprocal(b.rec, o[:, :, :, DH]).then_inc(S(f"{n}_rec"), 1)
                    dve.wait_ge(S(f"{n}_rec"), w)
                    v.tensor_tensor(b.on.rearrange("p t (h x) -> p t h x", h=H), o[:, :, :, 0:DH],
                                    b.rec.unsqueeze(3).broadcast_to([P, NT, H, DH]), ALU.mult).then_inc(S(f"{n}_on"), 1)

                def residual(p):
                    b, w = bufs[p], 2 * i + p + 1
                    dve.wait_ge(S(f"{n}_wo"), w)
                    dve.wait_ge(S(f"{n}_xb"), w)
                    v.tensor_tensor(b.res, halves(bank(p, 3)), b.xb, ALU.add).then_inc(S(f"{n}_res"), 1)
                    layernorm(n, p, i, b.res, None)

                def final(p):
                    normalise(n, p, i, bufs[p].res, xout(bufs[p]))

                return [keys, values, *behind_values, maxima, Both(split), *between] + [Both(clip)] * c.clip + [norm, residual, final]

            def gla_stages(i):
                def gate(p):
                    b, w = bufs[p], 2 * i + p + 1
                    dve.wait_ge(S("a_th"), w)
                    v.scalar_tensor_tensor(out=b.gw, in0=b.th, scalar=1.0, in1=bank(p, 2, 2), op0=ALU.add,
                                           op1=ALU.mult).then_inc(S("a_gate"), 1)

                def zbias(p):
                    b, w = bufs[p], 2 * i + p + 1
                    dve.wait_ge(S("a_z"), w)
                    for k in range(KC):
                        ins = v.tensor_scalar(b.zb[:, k, :], bank(p, 3)[:, k * L:(k + 1) * L], W["a_b2"][:, k:k + 1], None, ALU.add)
                    ins.then_inc(S("a_zb"), 1)

                def sums(p):
                    b, w = bufs[p], 2 * i + p + 1
                    dve.wait_ge(S("a_log"), 3 * w)
                    v.scalar_tensor_tensor(out=b.gl, in0=b.zb, scalar=0.0, in1=b.la, op0=ALU.min,
                                           op1=ALU.subtract).then_inc(S("a_gl"), 1)
                    dve.wait_ge(S("a_gl"), w)
                    for k in range(KC):
                        ins = v.tensor_tensor_scan(b.G[:, k, :], ones[:, :], b.gl[:, k, :], 0.0, ALU.mult, ALU.add)
                    ins.then_inc(S("a_G"), 1)
                    dve.wait_ge(S("a_G"), w)
                    g4 = b.G.rearrange("p k (t s) -> p (k t) s", t=NT)
                    mid = P // 2 - 1
                    v.tensor_tensor(b.f, b.G[:, :, P + mid], b.G[:, :, mid], ALU.subtract)
                    v.tensor_tensor(b.Dd.rearrange("p k (t s) -> p (k t) s", t=NT), g4,
                                    g4[:, :, mid:mid + 1].broadcast_to([P, KC * NT, P]), ALU.subtract).then_inc(S("a_Dd"), 1)

                def scaled(p):
                    b, w = bufs[p], 2 * i + p + 1
                    dve.wait_ge(S("a_decay"), w)
                    dve.wait_ge(S("a_qk"), w)
                    v.scalar_tensor_tensor(out=b.qd, in0=halves(bank(p, 0)), scalar=GDK ** -0.5, in1=b.Eq,
                                           op0=ALU.mult, op1=ALU.mult).then_inc(S("a_qd"), 1)
                    v.tensor_tensor(b.kd, halves(bank(p, 1)), b.Ek, ALU.mult)
                    dve.wait_ge(S("a_qd"), w)
                    for k in range(KC):
                        ins = v.tensor_scalar(b.qx[:, k, :], b.qd[:, k, P:L], b.fx[:, k:k + 1], None, ALU.mult)
                    ins.then_inc(S("a_scaled"), 1)

                def mask(p):
                    b, w = bufs[p], 2 * i + p + 1
                    dve.wait_ge(S("a_A"), w)
                    v.tensor_tensor(b.AT.rearrange("p (h a) s -> p h (a s)", h=GH), bank(p, 0, 4)[:, :, 0:3 * P],
                                    causal[:, :, :].rearrange("p a s -> p (a s)").unsqueeze(1).broadcast_to([P, GH, 3 * P]),
                                    ALU.mult).then_inc(S("a_AT"), 1)

                def gated(p):
                    b, w = bufs[p], 2 * i + p + 1
                    dve.wait_ge(S("a_sq_yn"), 4 * i + p + 1)
                    v.tensor_reduce(b.ms, b.sq.rearrange("p t (h d) -> p (t h) d", h=GH), axis=AX.X, op=ALU.add).then_inc(S("a_ms"), 1)
                    dve.wait_ge(S("a_gatew"), w)
                    v.tensor_tensor(b.y, bank(p, 0, 2), b.gw, ALU.mult).then_inc(S("a_y"), 1)

                def residual(p):
                    b, w = bufs[p], 2 * i + p + 1
                    dve.wait_ge(S("a_wo"), w)
                    v.tensor_tensor(b.res, halves(bank(p, 3)), b.xtok, ALU.add).then_inc(S("a_res"), 1)
                    layernorm("a", p, i, b.res, None)

                def final(p):
                    normalise("a", p, i, bufs[p].res, bufs[p].xA)

                return [zbias, sums, scaled, gate, mask, gated, residual, final]

            def first_layer(i, last=False):
                in_turn(gla_stages(i)[1:] + attn_stages(X0, i, lambda b: b.xo) + ([] if last else gla_stages(i + 1)[:1]))

            in_turn(gla_stages(0)[:1])
            with dve.Fori(0, PAIRS - 1) as i:
                first_layer(i)
            first_layer(PAIRS - 1, True)

            chain = [0]

            def link(ins):
                chain[0] += 1
                ins.then_inc(S("router_chain"), 1)
                dve.wait_ge(S("router_chain"), chain[0])

            def wide(col):
                return top[:, col, :].unsqueeze(2).broadcast_to([P, TILES, E])

            def choices(batches):
                dve.wait_ge(S("logits"), 2 + batches)
                src = logits[:, :, :]
                for k in range(2):
                    link(v.tensor_reduce(top[:, 2 * k, :], src, axis=AX.X, op=ALU.max))
                    link(v.tensor_tensor(rt[:, :, :], src, wide(2 * k), ALU.is_equal))
                    link(v.tensor_tensor(rt[:, :, :], rt[:, :, :], tiebreak[:, :, :], ALU.mult))
                    link(v.tensor_reduce(top[:, 1, :], rt[:, :, :], axis=AX.X, op=ALU.max))
                    link(v.tensor_tensor(hot[:, k], rt[:, :, :], wide(1), ALU.is_equal))
                    if k == 0:
                        link(v.scalar_tensor_tensor(out=masked[:, :, :], in0=hot[:, 0], scalar=-BIG, in1=logits[:, :, :],
                                                    op0=ALU.mult, op1=ALU.add))
                        src = masked[:, :, :]
                link(v.tensor_tensor(masked[:, :, :], hot[:, 0], hot[:, 1], ALU.add))
                v.memset(tick[:, :], 0.0).then_inc(S("chosen"), 1)

            def weigh(nth, over_all):
                v.tensor_tensor(top[:, 4, :], top[:, 2, :], top[:, 0, :], ALU.subtract)
                v.tensor_tensor(rt[:, :, :], logits[:, :, :], wide(0), ALU.subtract).then_inc(S("top2"), 1)
                dve.wait_ge(S("exp2"), nth)
                if over_all:
                    link(v.tensor_reduce(top[:, 6, :], rt[:, :, :], axis=AX.X, op=ALU.add))
                else:
                    link(v.tensor_scalar(top[:, 6, :], top[:, 5, :], 1.0, None, ALU.add))
                link(v.reciprocal(wts[:, 0, :], top[:, 6, :]))
                link(v.tensor_tensor(wts[:, 1, :], top[:, 5, :], wts[:, 0, :], ALU.mult))

            def by_expert(ap):
                return ap.rearrange("p t e -> p e t")

            def over_tiles(ap):
                return ap.unsqueeze(2).broadcast_to([P, E, TILES])

            def choose(dst, values):
                for k in range(2):
                    link(v.tensor_tensor(part[:, :, :], by_expert(hot[:, k]), values, ALU.mult))
                    link(v.tensor_reduce(dst[:, k, :], part[:, :, :].rearrange("p e t -> p t e"), axis=AX.X, op=ALU.add))

            def ranks(before, total):
                link(v.tensor_copy(rank[:, :, :], by_expert(total.rearrange("p (t e) -> p t e", e=E))))
                link(v.tensor_tensor_scan(part[:, :, :].rearrange("p e t -> p (e t)"), scan_reset[:, :],
                                          rank[:, :, :].rearrange("p e t -> p (e t)"), 0.0, ALU.mult, ALU.add))
                v.tensor_copy(cnt[:, 0, :], part[:, :, TILES - 1])
                link(v.tensor_tensor(rank[:, :, :], part[:, :, :], rank[:, :, :], ALU.subtract))
                link(v.tensor_tensor(rank[:, :, :], rank[:, :, :], by_expert(before.rearrange("p (t e) -> p t e", e=E)), ALU.add))
                link(v.tensor_tensor(rank[:, :, :], rank[:, :, :], by_expert(masked[:, :, :]), ALU.subtract))

            def dispatch0():
                link(v.tensor_tensor(part[:, :, :], over_tiles(cnt[:, 0, :]),
                                     tile_start[:, :].unsqueeze(1).broadcast_to([P, E, TILES]), ALU.is_gt))
                link(v.tensor_reduce(cnt[:, 1, :], part[:, :, :], axis=AX.X, op=ALU.add))
                link(v.tensor_tensor_scan(cnt[:, 2, :], ones[:, 0:E], cnt[:, 1, :], 0.0, ALU.mult, ALU.add))
                link(v.tensor_tensor(cnt[:, 3, :], cnt[:, 2, :], cnt[:, 1, :], ALU.subtract))
                link(v.tensor_scalar(cnt[:, 3, :], cnt[:, 3, :], float(P), None, ALU.mult))
                link(v.tensor_tensor(rank[:, :, :], rank[:, :, :], over_tiles(cnt[:, 3, :]), ALU.add))
                choose(slot, rank[:, :, :])
                v.tensor_copy(scat[:, :, :], slot[:, :, :]).then_inc(S("dispatched"), 1)
                link(v.tensor_tensor(owned[:, :, :], cnt[0:1, 2, :].unsqueeze(1).broadcast_to([1, TILES0, E]),
                                     tile_no[0:1, :].unsqueeze(2).broadcast_to([1, TILES0, E]), ALU.is_le))
                link(v.tensor_reduce(owner[:, :], owned[:, :, :], axis=AX.X, op=ALU.add))
                link(v.tensor_scalar(owner[:, :], owner[:, :], float(E - 1), None, ALU.min))
                v.tensor_copy(owner_i[:, :], owner[:, :]).then_inc(S("dispatched"), 1)

            def dispatch1(first, last):
                choose(slot, rank[:, :, :])
                link(v.tensor_scalar(keep[:, :, :], slot[:, :, :], float(SLOTS1), None, ALU.is_lt))
                link(v.tensor_tensor(rank[:, :, :], rank[:, :, :], over_tiles(base1[:, :]), ALU.add))
                choose(slot, rank[:, :, :])
                two = part[:, 0:2, :]
                link(v.tensor_tensor(two, slot[:, :, :], trash[:, :, :], ALU.subtract))
                link(v.tensor_tensor(two, two, keep[:, :, :], ALU.mult))
                link(v.tensor_tensor(two, two, trash[:, :, :], ALU.add))
                v.tensor_copy(scat[:, :, first:last], two[:, :, first:last]).then_inc(S("dispatched"), 1)

            def by_row():
                link(v.tensor_tensor(top[:, 0, :], slot[:, 0, :], slot[:, 1, :], ALU.min))
                link(v.tensor_tensor(top[:, 1, :], slot[:, 0, :], slot[:, 1, :], ALU.max))
                link(v.tensor_copy(gath[:, :, :], top[:, 0:2, :]))
                link(v.tensor_tensor(keep[:, 0, :], slot[:, 0, :], slot[:, 1, :], ALU.is_le))
                link(v.tensor_tensor(keep[:, 1, :], slot[:, 0, :], slot[:, 1, :], ALU.is_gt))
                for k in range(2):
                    link(v.tensor_tensor(part[:, 2 * k:2 * k + 2, :], wts[:, :, :], keep[:, k:k + 1, :].broadcast_to([P, 2, TILES]), ALU.mult))
                link(v.tensor_tensor(wts[:, 0, :], part[:, 0, :], part[:, 3, :], ALU.add))
                link(v.tensor_tensor(wts[:, 1, :], part[:, 1, :], part[:, 2, :], ALU.add))

            def drop():
                link(v.tensor_scalar(cnt[:, 1, :], cnt[:, 0, :], float(CAP), None, ALU.is_le))
                choose(keep, over_tiles(cnt[:, 1, :]))
                link(v.tensor_tensor(wts[:, :, :], wts[:, :, :], keep[:, :, :], ALU.mult))
                link(v.tensor_tensor(slot[:, :, :], slot[:, :, :], keep[:, :, :], ALU.mult))
                by_row()
                v.memset(tick[:, :], 0.0).then_inc(S("dispatched"), 1)

            choices(B)
            dve.wait_ge(S("counted"), 1)
            ranks(ps[:, 4, 0:P], ps[:, 4, P:2 * P])
            dispatch0()
            weigh(1, False)
            by_row()
            v.memset(tick[:, :], 0.0).then_inc(S("dispatched"), 1)

            def rows0(j, p):
                dve.wait_ge(S("t_X"), j + 1)
                v.tensor_copy(slots0[p].xT, bank(p, 2)[:, 0:D].rearrange("p (k t) -> p k t", k=KC)).then_inc(S("t_xT"), 1)

            def hidden0(j, p):
                b = slots0[p]
                dve.wait_ge(S("t_v"), j + 1)
                dve.wait_ge(S("t_sil"), j + 1)
                v.tensor_tensor(b.h, bank(p, 1), b.sil, ALU.mult).then_inc(S("t_h"), 1)

            def outputs0(j, p, h, first=False):
                dve.wait_ge(S("t_y"), j + 1)
                if not first:
                    dve.wait_ge(S(f"t_out{p}"), 16 * h)
                v.tensor_copy(slots0[p].y, bank(p, 3)[:, 0:D]).then_inc(S("t_ys"), 1)

            rows0(0, 0)
            rows0(1, 1)
            hidden0(0, 0)
            for j in (1, 2):
                hidden0(j, j % 2)
                rows0(j + 1, (j + 1) % 2)
                outputs0(j - 1, (j - 1) % 2, 0, True)
            with dve.Fori(1, TILES0 // 2 - 1) as i:
                for p in range(2):
                    j = 2 * i + 1 + p
                    hidden0(j, 1 - p)
                    rows0(j + 1, p)
                    outputs0(j - 1, p, i)
            hidden0(TILES0 - 2, 1)
            rows0(TILES0 - 1, 0)
            outputs0(TILES0 - 3, 0, TILES0 // 2 - 1)
            hidden0(TILES0 - 1, 0)
            outputs0(TILES0 - 2, 1, TILES0 // 2 - 1)
            outputs0(TILES0 - 1, 0, TILES0 // 2)

            dve.wait_ge(S("c_weights"), c_loads)
            scale_bias(["s1_bq", "x1_bq"], "rescaled")
            def mixed(i, ph, xout, first=False):
                def stats(p):
                    b = bufs[p]
                    if ph == 1:
                        dve.wait_ge(S(f"gathered{p}"), 64 * (i + 1))
                        outputs = b.yg
                    else:
                        dve.wait_ge(S("a_out"), 2 * B + 2 * i + p - 1)
                        dve.wait_ge(S(f"gathered{p}"), 96 * PAIRS + 32 * (i + 1))
                        dve.wait_ge(S("mixed"), 2 * B)
                        outputs = yg_all[:, bass.ds(2 * i + p, 1), :].rearrange("p b a -> p (b a)")
                    for k in range(ph - 1, 2):
                        for t in range(NT):
                            tile = 4 * i + 2 * p + t
                            before = b.res[:, t, :] if k > ph - 1 else xres[:, bass.ds(tile, 1), :].rearrange("p a d -> p (a d)")
                            ins = v.scalar_tensor_tensor(out=b.res[:, t, :], in0=outputs[:, (k * NT + t) * D:(k * NT + t + 1) * D],
                                                         scalar=wts[:, k, bass.ds(tile, 1)], in1=before,
                                                         op0=ALU.mult, op1=ALU.add)
                        ins.then_inc(S("mixed" if k == 0 else "a_res"), 1)
                        if k == 0:
                            dve.wait_ge(S("mixed"), 2 * i + p + 1)
                    layernorm("a", p, i + ph * PAIRS, b.res, None)

                def final(p):
                    if ph == 2 and not first:
                        dve.wait_ge(S(f"stored{p}"), 16 * i)
                    normalise("a", p, i + ph * PAIRS, bufs[p].res, xout(bufs[p]))
                return [stats, final]

            def second_layer(i, last=False):
                if not last:
                    ahead, counted = mixed(i + 1, 1, lambda b: b.xA), []
                else:
                    def copy():
                        dve.wait_ge(S("counted"), 2)
                        v.tensor_copy(counts[:, :], ps[:, 3, 0:2 * P]).then_inc(S("counts"), 1)

                    def send():
                        dve.wait_ge(S("counts"), 1)
                        ranks(counts[:, 0:P], counts[:, P:2 * P])
                        dispatch1(0, EARLY)

                    choices(2 * B - 2)
                    ahead, counted = [Both(send)], [Both(copy)]
                in_turn(attn_stages(S1, i, lambda b: b.xB, ahead, counted)[1:] + attn_stages(X1, i, lambda b: b.xo)
                        + ([] if last else attn_stages(S1, i + 1, lambda b: b.xB)[:1]))

            in_turn(mixed(0, 1, lambda b: b.xA) + attn_stages(S1, 0, lambda b: b.xB)[:1])
            with dve.Fori(0, PAIRS - 1) as i:
                second_layer(i)
            second_layer(PAIRS - 1, True)
            choices(2 * B)
            dve.wait_ge(S("counted"), 3)
            ranks(ps[:, 4, 0:P], ps[:, 4, P:2 * P])
            dispatch1(EARLY, TILES)
            weigh(2, True)
            drop()

            def rows1(e, p):
                dve.wait_ge(S("e_X"), e + 1)
                v.tensor_copy(experts1[p].xT, ps[:, 0:2, 0:SLOTS1]).then_inc(S("e_xT"), 1)

            def outputs1(e, p, h, first=False):
                dve.wait_ge(S("e_y"), e + 1)
                if not first:
                    dve.wait_ge(S(f"e_out{p}"), 16 * h)
                b = experts1[p]
                v.tensor_tensor(b.y, ps[:, 4 + 2 * p:6 + 2 * p, :].rearrange("p a (t d) -> p (a t) d", d=D)[:, 0:ST1, :],
                                b.b2.unsqueeze(1).broadcast_to([P, ST1, D]), ALU.add).then_inc(S("e_ys"), 1)

            rows1(0, 0)
            for p in range(2):
                rows1(p + 1, 1 - p)
                outputs1(p, p, 0, True)
            with dve.Fori(1, E // 2 - 1) as i:
                for p in range(2):
                    rows1(2 * i + p + 1, 1 - p)
                    outputs1(2 * i + p, p, i)
            rows1(E - 1, 1)
            for p in range(2):
                outputs1(E - 2 + p, p, E // 2 - 1)
            for p in range(2):
                dve.wait_ge(S(f"gathered{p}"), 96 * PAIRS)
                for i in range(PAIRS):
                    for t in range(NT):
                        tile = 4 * i + 2 * p + t
                        ins = v.scalar_tensor_tensor(out=xres[:, tile, :], in0=yg_all[:, 2 * i + p, t * D:(t + 1) * D],
                                                     scalar=wts[:, 0, tile:tile + 1], in1=xres[:, tile, :],
                                                     op0=ALU.mult, op1=ALU.add)
                    ins.then_inc(S("mixed"), 1)
            in_turn(mixed(0, 2, lambda b: b.xo, True))
            with dve.Fori(1, PAIRS) as i:
                in_turn(mixed(i, 2, lambda b: b.xo))

        @block.gpsimd
        def _(pool):
            g = nc.gpsimd
            pool.wait_ge(S("memsets"), 5)
            pool.wait_ge(S("rescaled"), 2)
            pool.wait_ge(S("a_weights"), a_loads)
            pool.wait_ge(S("x0_weights"), x0_loads)

            def rstd(n, p, i):
                b, w = bufs[p], 2 * i + p + 1
                pool.wait_ge(S(f"{n}_mv"), w)
                g.tensor_tensor(b.var, b.mv[:, :, 1], eps[:, 0:NT], ALU.add).then_inc(S(f"{n}_var"), 1)
                pool.wait_ge(S(f"{n}_var"), w)
                g.tensor_tensor(b.rstd, b.var, neghalf[:, 0:NT], ALU.pow).then_inc(S(f"{n}_rstd"), 1)

            def attn_stages(c, loop, before, xin, between=()):
                n, wn, i = c.prefix, c.name, loop + c.pairs_before

                def xb(p):
                    b = bufs[p]
                    pool.wait_ge(S(f"{before[0]}_out"), before[1] + 2 * loop + p + 1)
                    g.tensor_tensor(b.xb, xin(b), W[f"{wn}_bo"].unsqueeze(1).broadcast_to([P, NT, D]), ALU.add).then_inc(S(f"{n}_xb"), 1)

                def headkeys(p):
                    b, w = bufs[p], 2 * i + p + 1
                    pool.wait_ge(S(f"{n}_kT"), 2 * w)
                    kb = b.KB if c.selfattn else b.KBm
                    for k in range(QC):
                        ins = g.tensor_tensor(kb[:, k], b.kp[:, k, 0:c.nk].unsqueeze(1).broadcast_to([P, HC, c.nk]),
                                              rowmask[:, :].unsqueeze(2).broadcast_to([P, HC, c.nk]), ALU.mult)
                        ins.then_inc(S(f"{n}_KB"), 1)

                def low(p):
                    b = bufs[p]
                    pool.wait_ge(S(f"{n}_qh"), 2 * (2 * i + p + 1))
                    g.tensor_tensor(b.ql, b.qf, b.qh, ALU.subtract).then_inc(S(f"{n}_qs"), 1)

                return [xb, headkeys, low, *between, lambda p: rstd(n, p, i)]

            def store(first, i):
                def stage(p):
                    pool.wait_ge(S("x_out"), first + 2 * i + p + 1)
                    g.tensor_copy(xres[:, bass.ds(4 * i + 2 * p, NT), :], bufs[p].xo).then_inc(S("store"), 1)
                return [stage]

            def scatter(dispatched, batches, first, last):
                pool.wait_ge(S("dispatched"), dispatched)
                pool.wait_ge(S("cleared"), 16)
                pool.wait_ge(S("store"), batches)
                for t in range(first, last):
                    for k in range(2):
                        g.indirect_dma_start(rows_in[:, :], bass.IndirectOffsetOnAxis(ap=scat[:, k, t:t + 1], axis=0),
                                             xres[:, t, :], None).then_inc(S("scattered"), 16)

            def rows_of(p, i):
                g.tensor_copy(gidx[:, p, :, :], gath[:, :, bass.ds(4 * i + 2 * p, NT)]).then_inc(S("gidx"), 1)
                pool.wait_ge(S("gidx"), 2 * i + p + 1)
                g.tensor_tensor(ptick[:, :], eps[:, 0:1], eps[:, 0:1], ALU.add)

            def gather_choice(p, k, rows):
                for t in range(NT):
                    g.indirect_dma_start(bufs[p].yg[:, (k * NT + t) * D:(k * NT + t + 1) * D], None, rows_out[0:rows, :],
                                         bass.IndirectOffsetOnAxis(ap=gidx[:, p, k, t:t + 1], axis=0)
                                         ).then_inc(S(f"gathered{p}"), 16)

            def gather(i):
                def stage(p):
                    pool.wait_ge(S("a_res"), B + 2 * i + p - 1)
                    rows_of(p, i)
                    for k in range(2):
                        gather_choice(p, k, TILES0 * P)
                return [stage]

            def gla_stages(i):
                def gate(p):
                    b, w = bufs[p], 2 * i + p + 1
                    pool.wait_ge(S("a_gate"), w)
                    gw = b.gw.rearrange("p t (h d) -> p (t h) d", h=GH)
                    g.tensor_tensor(gw, gw, W["a_gn"].unsqueeze(1).broadcast_to([P, NT * GH, GDV]), ALU.mult).then_inc(S("a_gatew"), 1)

                def rms(p):
                    b, w = bufs[p], 2 * i + p + 1
                    pool.wait_ge(S("a_ms"), w)
                    g.tensor_tensor(b.ms, b.ms, eps[:, :], ALU.add).then_inc(S("a_msv"), 1)
                    pool.wait_ge(S("a_msv"), w)
                    g.tensor_tensor(b.rms, b.ms, neghalf[:, :], ALU.pow).then_inc(S("a_rms"), 1)
                    pool.wait_ge(S("a_rms"), w)
                    pool.wait_ge(S("a_y"), w)
                    y = b.y[:, 0, :].rearrange("p (h d) -> p h d", h=GH)
                    g.tensor_tensor(y, y, b.rms[:, 0:GH].unsqueeze(2).broadcast_to([P, GH, GDV]), ALU.mult).then_inc(S("a_yn"), 1)

                return [gate, rms, lambda p: rstd("a", p, i)]

            with pool.Fori(0, PAIRS) as i:
                in_turn(gla_stages(i) + attn_stages(X0, i, ("a", 0), lambda b: b.xA) + store(0, i))
            scatter(1, B, 0, TILES)
            pool.wait_ge(S("c_weights"), c_loads)
            pool.wait_ge(S("dispatched"), 3)
            for p in range(2):
                rows_of(p, 0)
            for p in range(2):
                pool.wait_ge(S(f"t_out{p}"), 16 * (TILES0 // 2))
            for p in range(2):
                gather_choice(p, 0, (TILES0 - 1) * P)
            pool.wait_ge(S("t_out0"), 16 * (TILES0 // 2 + 1))
            for p in range(2):
                gather_choice(p, 1, TILES0 * P)

            def second_head(i):
                return attn_stages(S1, i, ("a", B), lambda b: b.xA)[:2]

            def second_layer(i, last=False):
                if last:
                    ahead = [Both(lambda: scatter(4, 2 * B - 2, 0, EARLY))]
                else:
                    ahead = gather(i + 1) + [lambda p: rstd("a", p, i + 1 + PAIRS)]
                in_turn(attn_stages(S1, i, ("a", B), lambda b: b.xA, ahead)[2:]
                        + attn_stages(X1, i, ("s", 0), lambda b: b.xB) + ([] if last else second_head(i + 1)) + store(B, i))

            for p in range(2):
                rstd("a", p, PAIRS)
            in_turn(second_head(0))
            with pool.Fori(0, PAIRS - 1) as i:
                second_layer(i)
            second_layer(PAIRS - 1, True)
            scatter(5, 2 * B, EARLY, TILES)
            pool.wait_ge(S("dispatched"), 6)

            def gather_all(b, k):
                for t in range(NT):
                    g.indirect_dma_start(yg_all[:, b, (k * NT + t) * D:(k * NT + t + 1) * D], None, rows_out[0:TRASH, :],
                                         bass.IndirectOffsetOnAxis(ap=gath[:, k, NT * b + t:NT * b + t + 1], axis=0)
                                         ).then_inc(S(f"gathered{b % 2}"), 16)

            pool.wait_ge(S("e_out0"), 16 * E // 2)
            pool.wait_ge(S("e_out1"), 16 * (E // 2 - 1))
            for p in range(2):
                for i in range(PAIRS):
                    gather_all(2 * i + p, 0)
            pool.wait_ge(S("e_out1"), 16 * E // 2)
            for b in range(B):
                p, i = b % 2, b // 2
                pool.wait_ge(S(f"gathered{p}"), 96 * PAIRS + 32 * i)
                gather_all(b, 1)
                if i and p == 1:
                    for q in range(2):
                        rstd("a", q, i - 1 + 2 * PAIRS)
            for p in range(2):
                rstd("a", p, 3 * PAIRS - 1)

        @block.tensor
        def _(pe):
            mm, tr = nc.tensor.matmul, nc.tensor.transpose

            def attn_stages(c, loop, before, xin, behind_values=()):
                n, wn, i = c.prefix, c.name, loop + c.pairs_before

                def turn(p):
                    b = bufs[p]
                    pe.wait_ge(S(f"{before[0]}_out"), before[1] + 2 * loop + p + 1)
                    for k in range(KC):
                        for t in range(NT):
                            ins = tr(bank(p, c.turn_bank)[:, k * L + t * P:k * L + (t + 1) * P], xin(b)[:, t, k * P:(k + 1) * P], ident[:, :])
                    ins.then_inc(S(f"{n}_xT_done"), 1)

                def feat(p, first, wt, src, rows, cols):
                    dst = bank(p, first, 2).rearrange("p a b -> p (a b)")
                    for m in range(QC):
                        for k in range(KC):
                            ins = mm(dst[:, m * cols:(m + 1) * cols], wt[0:rows[k], k, m * P:(m + 1) * P],
                                     src[0:rows[k], k, 0:cols], start=(k == 0), stop=(k == KC - 1))
                    return ins

                def project_k(p):
                    b = bufs[p]
                    if c is X0:
                        pe.wait_ge(S("x0_weights"), x0_loads)
                    if c.selfattn:
                        pe.wait_ge(S(f"{n}_xinT"), 2 * i + p + 1)
                        ins = feat(p, 0, W[f"{wn}_wk"], b.xinT, (P, P), L)
                    else:
                        if c is X0:
                            pe.wait_ge(S("a_y"), 2 * loop + p + 1)
                        pe.wait_ge(S(f"a_in{p}"), 64 * (loop + 1) if c is X0 else 64 * PAIRS + 32 * (loop + 1))
                        ins = feat(p, 0, W[f"{wn}_wk"], b.ctxT, (P, DC - P), M)
                    ins.then_inc(S(f"{n}_kv"), 1)

                def project_q(p):
                    pe.wait_ge(S(f"{n}_xinT"), 2 * i + p + 1)
                    if c.selfattn:
                        pe.wait_ge(S("logits"), B + 2 * loop + p + 1)
                    feat(p, 2, W[f"{wn}_wq"], bufs[p].xinT, (P, P), L).then_inc(S(f"{n}_q"), 1)

                def project_v(p):
                    b, w = bufs[p], 2 * i + p + 1
                    if c.selfattn:
                        pe.wait_ge(S(f"{n}_qh"), 2 * w - 1)
                    for t in range(c.key_tiles):
                        for k in range(KC):
                            if c.selfattn:
                                ins = mm(bank(p, 2)[:, t * D:(t + 1) * D], b.xinT[:, k, t * P:(t + 1) * P], W[f"{wn}_wv"][:, k, :],
                                         start=(k == 0), stop=(k == KC - 1))
                            else:
                                rows = (P, DC - P)[k]
                                ins = mm(bank(p, 1)[0:M, 0:D], b.ctxT[0:rows, k, 0:M], W[f"{wn}_wv"][0:rows, k, :],
                                         start=(k == 0), stop=(k == KC - 1))
                    ins.then_inc(S(f"{n}_kv"), 1)

                def scores(p):
                    b, w = bufs[p], 2 * i + p + 1
                    kb = b.KB if c.selfattn else b.KBm
                    pe.wait_ge(S(f"{n}_qh"), 2 * w)
                    pe.wait_ge(S(f"{n}_va"), w)
                    per = c.rounds // NT
                    for r in range(c.rounds):
                        t, g = r // per, r % per
                        if t == 0:
                            last = ((2 * g + 2) * c.bank_heads - 1) // HC
                            pe.wait_ge(S(f"{n}_KB"), QC * (w - 1) + last + 1)
                        if r >= 2:
                            pe.wait_ge(S(f"{n}_Smax"), c.rounds * (2 * i + p) + r - 1)
                        for j in range(2):
                            h = (2 * g + j) * c.bank_heads
                            k, hh = h // HC, h % HC
                            dst = bank(p, 2 * (r % 2) + j)
                            ins = mm(dst[:, 0:c.bank_heads * c.nk], b.qh[:, k, t * P:(t + 1) * P],
                                     kb[:, k, hh:hh + c.bank_heads, :].rearrange("p h k -> p (h k)"),
                                     start=True, stop=not c.selfattn)
                            if c.selfattn:
                                for a in range(c.bank_heads):
                                    ins = mm(dst[:, a * L + (1 - t) * P:a * L + (2 - t) * P], identb[:, :], winmask[:, t, :],
                                             start=False, stop=(a == c.bank_heads - 1))
                        ins.then_inc(S(f"{n}_S"), 1)

                def shift(p):
                    b = bufs[p]
                    pe.wait_ge(S(f"{n}_nmb"), 2 * i + p + 1)
                    for t in range(NT):
                        ins = mm(bank(p, 3)[0:3 * H, t * P:(t + 1) * P], b.nmb[:, t].rearrange("p a h -> p (a h)"), identb[:, :],
                                 start=True, stop=True)
                    ins.then_inc(S(f"{n}_nmT_done"), 1)

                def attend():
                    def products(p, u):
                        b = bufs[p]
                        kb = b.KB if c.selfattn else b.KBm
                        if u < 2:
                            pe.wait_ge(S(f"{n}_Smax"), c.rounds * (2 * i + p + 1))
                            pe.wait_ge(S(f"{n}_qs"), 2 * i + p + 1)
                        else:
                            pe.wait_ge(S(f"{n}_PT"), 2 * c.units * i + 2 * (u - 2) + p + 1)
                        for a in range(2):
                            h = u if c.selfattn else 2 * u + a
                            kt = a if c.selfattn else 0
                            k, hh = h // HC, h % HC
                            cols = bank(p, u % 2)[0:c.keys, a * L:(a + 1) * L]
                            key = kb[:, k, hh, kt * P:kt * P + c.keys]
                            mm(cols, key, b.qh[:, k, :], start=(a == 0), stop=False, skip_group_check=True)
                            ins = mm(cols, key, b.ql[:, k, :], start=False, stop=c.clip, skip_group_check=True)
                            if c.selfattn:
                                ins = mm(cols[:, (1 - kt) * P:(2 - kt) * P], identb[:, :], winmask[:, kt, :], start=False, stop=False,
                                         skip_group_check=True)
                        if c.clip:
                            ins.then_inc(S(f"{n}_ST0"), 1)

                    def shifted(p, u):
                        if c.clip:
                            pe.wait_ge(S(f"{n}_clip"), 2 * c.units * loop + 2 * u + p + 1)
                        for a in range(2):
                            h = u if c.selfattn else 2 * u + a
                            ins = mm(bank(p, u % 2)[0:c.keys, a * L:(a + 1) * L], headrow[:, h, 0:c.keys], bufs[p].nmT,
                                     start=False, stop=True, skip_group_check=True)
                        ins.then_inc(S(f"{n}_ST"), 1)

                    def values(p, u0):
                        b = bufs[p]
                        pe.wait_ge(S(f"{n}_PT"), 2 * c.units * i + 2 * (u0 + c.units_at_once - 1) + p + 1)
                        for kt in range(c.key_tiles):
                            for j in range(4):
                                h = u0 * c.unit_heads + j
                                u, gg = h // c.unit_heads, h // 4
                                half = kt if c.selfattn else h % 2
                                ins = mm(bank(p, 2 + gg // 2)[32 * j:32 * j + 32, (gg % 2) * L:(gg % 2 + 1) * L],
                                         b.va[0:c.keys, kt, h, :], b.PT[0:c.keys, u % c.PT_units, half * L:(half + 1) * L],
                                         start=(kt == 0), stop=(kt == c.key_tiles - 1))
                        return ins

                    for p, u in ((0, 0), (1, 0), (0, 1), (1, 1)) if c.clip else ((0, 0), (0, 1), (1, 0), (1, 1)):
                        products(p, u)
                    for p in range(2):
                        shift(p)
                    for p in range(2):
                        pe.wait_ge(S(f"{n}_nmT"), 2 * i + p + 1)
                        shifted(p, 0)
                    for u in range(c.units):
                        for p in range(2):
                            if u + 1 < c.units:
                                shifted(p, u + 1)
                        for p in range(2):
                            if u + 2 < c.units:
                                products(p, u + 2)
                        if (u + 1) % c.units_at_once == 0:
                            for p in range(2):
                                ins = values(p, u + 1 - c.units_at_once)
                                if u + 1 == c.units:
                                    ins.then_inc(S(f"{n}_OT_done"), 1)

                def untranspose(p):
                    b, w = bufs[p], 2 * i + p + 1
                    pe.wait_ge(S(f"{n}_OT"), w)
                    for t in range(NT):
                        for gg in range(4):
                            ins = tr(bank(p, t)[:, gg * P:(gg + 1) * P], b.OT[:, gg, t * P:(t + 1) * P], ident[:, :])
                    ins.then_inc(S(f"{n}_O"), 1)

                def turn_out(p):
                    b, w = bufs[p], 2 * i + p + 1
                    pe.wait_ge(S(f"{n}_on"), w)
                    for k in range(KC):
                        for t in range(NT):
                            ins = tr(bank(p, 2)[:, k * L + t * P:k * L + (t + 1) * P], b.on[:, t, k * P:(k + 1) * P], ident[:, :])
                    ins.then_inc(S(f"{n}_onT_done"), 1)

                def project_out(p):
                    b, w = bufs[p], 2 * i + p + 1
                    pe.wait_ge(S(f"{n}_onT"), w)
                    for t in range(NT):
                        for k in range(KC):
                            ins = mm(bank(p, 3)[:, t * D:(t + 1) * D], b.onT[:, k, t * P:(t + 1) * P], W[f"{wn}_wo"][:, k, :],
                                     start=(k == 0), stop=(k == KC - 1))
                    ins.then_inc(S(f"{n}_wo"), 1)

                if c.selfattn:
                    first = [turn, project_k, project_q, project_v]
                else:
                    first = [project_k, project_v, turn, project_q]
                return first + [*behind_values, scores, Both(attend), untranspose, turn_out, project_out]

            def out_stages(first, r, i, gates_ahead=False):
                def turn(p):
                    b, w = bufs[p], 2 * i + p + 1
                    pe.wait_ge(S("x_out"), first + w)
                    if gates_ahead:
                        pe.wait_ge(S("a_g1"), w + 2)
                    for k in range(KC):
                        for t in range(NT):
                            ins = tr(bank(p, 2)[:, k * L + t * P:k * L + (t + 1) * P], b.xo[:, t, k * P:(k + 1) * P], ident[:, :])
                    ins.then_inc(S("xoT_done"), 1)

                def route(p):
                    b, w = bufs[p], 2 * i + p + 1
                    pe.wait_ge(S("xoT"), first + w)
                    for t in range(NT):
                        for k in range(KC):
                            ins = mm(bank(p, 2)[:, t * E:(t + 1) * E], b.xoT[:, k, t * P:(t + 1) * P], r[:, k, :],
                                     start=(k == 0), stop=(k == KC - 1))
                    ins.then_inc(S("logits_done"), 1)

                return [turn, route]

            def gla_stages(i, first=False):
                def keys(p):
                    b, w = bufs[p], 2 * i + p + 1
                    pe.wait_ge(S(f"a_in{p}"), 64 * (i + 1))
                    for k in range(KC):
                        ins = mm(bank(p, 2)[0:LOWRANK, 0:L], W["a_w1"][:, k, :], b.xT[:, k, :], start=(k == 0), stop=(k == KC - 1))
                    ins.then_inc(S("a_g1_done"), 1)
                    for n, wt in enumerate(("a_wq", "a_wk")):
                        for m in range(KC):
                            for k in range(KC):
                                ins = mm(bank(p, n)[:, m * L:(m + 1) * L], W[wt][:, k, m * P:(m + 1) * P], b.xT[:, k, :],
                                         start=(k == 0), stop=(k == KC - 1))
                    ins.then_inc(S("a_qk"), 1)

                def decay(p):
                    b, w = bufs[p], 2 * i + p + 1
                    pe.wait_ge(S("a_g1"), w)
                    if not first:
                        pe.wait_ge(S("x_res"), w - 2)
                    for m in range(KC):
                        ins = mm(bank(p, 3)[:, m * L:(m + 1) * L], W["a_w2"][:, m * P:(m + 1) * P], b.g1, start=True, stop=True)
                    ins.then_inc(S("a_z"), 1)

                def tokens(wt, signal):
                    def stage(p):
                        b, w = bufs[p], 2 * i + p + 1
                        pe.wait_ge(S("a_weights"), a_loads)
                        pe.wait_ge(S("a_zb" if wt == "a_wv" else "a_vs"), w)
                        if wt == "a_wv":
                            pe.wait_ge(S("logits"), w)
                        for t in range(NT):
                            for k in range(KC):
                                ins = mm(bank(p, 2 + t), b.xT[:, k, t * P:(t + 1) * P], W[wt][:, k, :],
                                         start=(k == 0), stop=(k == KC - 1))
                        ins.then_inc(S(signal), 1)
                    return stage

                def scores(p):
                    b, w = bufs[p], 2 * i + p + 1
                    pe.wait_ge(S("a_scaled"), w)
                    pe.wait_ge(S("a_gate"), w)
                    for h in range(GH):
                        k, r = h // 2, slice(GDK * (h % 2), GDK * (h % 2) + GDK)
                        for a, (key, qry) in enumerate(((b.kd[r, k, 0:P], b.qd[r, k, 0:P]), (b.kd[r, k, P:L], b.qd[r, k, P:L]),
                                                        (b.kd[r, k, 0:P], b.qx[r, k, :]))):
                            ins = mm(bank(p, h)[:, a * P:(a + 1) * P], key, qry, start=True, stop=True)
                    ins.then_inc(S("a_A"), 1)

                def mix(p):
                    b, w = bufs[p], 2 * i + p + 1
                    pe.wait_ge(S("a_AT"), w)
                    for h in range(GH):
                        c = slice(h * GDV, (h + 1) * GDV)
                        mm(bank(p, 0)[:, c], b.AT[:, 3 * h, :], b.v[:, 0, c], start=True, stop=True)
                        mm(bank(p, 1)[:, c], b.AT[:, 3 * h + 2, :], b.v[:, 0, c], start=True, stop=False)
                        ins = mm(bank(p, 1)[:, c], b.AT[:, 3 * h + 1, :], b.v[:, 1, c], start=False, stop=True)
                    ins.then_inc(S("a_o"), 1)

                def turn(p):
                    b, w = bufs[p], 2 * i + p + 1
                    for t in range(NT):
                        if t == 0:
                            pe.wait_ge(S("a_yn"), w)
                        else:
                            pe.wait_ge(S("a_sq_yn"), 4 * i + 2 + p + 1)
                        for k in range(VC):
                            ins = tr(bank(p, 2 + t)[:, k * P:(k + 1) * P], b.y[:, t, k * P:(k + 1) * P], ident[:, :])
                    ins.then_inc(S("a_yT_done"), 1)

                def project_out(p):
                    b, w = bufs[p], 2 * i + p + 1
                    pe.wait_ge(S("a_yT"), w)
                    for t in range(NT):
                        for k in range(VC):
                            ins = mm(bank(p, 3)[:, t * D:(t + 1) * D], b.yT[:, t, k * P:(k + 1) * P], W["a_wo"][:, k, :],
                                     start=(k == 0), stop=(k == VC - 1))
                    ins.then_inc(S("a_wo"), 1)

                return [keys, decay, tokens("a_wv", "a_v"), tokens("a_wg", "a_g"), scores, mix, turn, project_out]

            pe.wait_ge(S("a_first"), first_loads)

            def first_layer(i, last=False):
                turn, route = out_stages(0, r0, i, not last)
                if last:
                    ahead = [turn, route]
                else:
                    keys, decay = gla_stages(i + 1)[:2]
                    ahead = [keys, turn, decay, route]
                *gla, turn_gla, project_gla = gla_stages(i)[2:]
                project_k, *attn = attn_stages(X0, i, ("a", 0), lambda b: b.xA)

                def keys_and_turn():
                    project_k(0)
                    turn_gla(0)
                    turn_gla(1)

                def second_keys():
                    project_k(1)

                in_turn(gla + [Both(keys_and_turn), project_gla, Both(second_keys)] + attn + ahead)

            in_turn(gla_stages(0, True)[:2])
            with pe.Fori(0, PAIRS - 1) as i:
                first_layer(i)
            first_layer(PAIRS - 1, True)

            def count(nth, bank):
                pe.wait_ge(S("chosen"), nth)
                chosen = masked[:, :, :].rearrange("p t e -> p (t e)")
                mm(ps[:, bank, 0:P], causal[:, 0, :], chosen, start=True, stop=True)
                mm(ps[:, bank, P:2 * P], onemat[:, :], chosen, start=True, stop=True).then_inc(S("counted"), 1)

            def turn0(p, h):
                pe.wait_ge(S(f"t_in{p}"), 16 * (h + 1))
                for k in range(KC):
                    ins = tr(bank(p, 2)[:, k * P:(k + 1) * P], slots0[p].x[:, k * P:(k + 1) * P], ident[:, :])
                ins.then_inc(S("t_X"), 1)

            def expert_of(j):
                return pe.value_load(owner_i[0:1, bass.ds(j, 1)], min_val=0, max_val=E - 1)

            def weights0(e, off, n):
                return ew[:, bass.ds(e, 1), off:off + n].rearrange("p a n -> p (a n)")

            def hidden0(p, e, a, signal):
                for k in range(KC):
                    ins = mm(bank(p, a), slots0[p].xT[:, k, :], weights0(e, a * KC * FH + k * FH, FH), start=(k == 0), stop=(k == KC - 1))
                ins.then_inc(S(signal), 1)

            def turn_hidden0(j, p):
                pe.wait_ge(S("t_h"), j + 1)
                for m in range(MC):
                    ins = tr(bank(p, 2)[:, m * P:(m + 1) * P], slots0[p].h[:, m * P:(m + 1) * P], ident[:, :])
                ins.then_inc(S("t_H"), 1)

            def outputs0(j, p, e, first=False):
                pe.wait_ge(S("t_hT"), j + 1)
                if not first:
                    pe.wait_ge(S("t_ys"), j - 1)
                for m in range(MC):
                    ins = mm(bank(p, 3)[:, 0:D], slots0[p].hT[:, m, :], weights0(e, 2 * KC * FH + m * D, D), start=(m == 0), stop=(m == MC - 1))
                ins.then_inc(S("t_y"), 1)

            def tile0(j, p, h, before=None, first=False, last=False):
                e = expert_of(j)
                pe.wait_ge(S("t_xT"), j + 1)
                hidden0(p, e, 0, "t_u")
                before = expert_of(j - 1) if before is None else before
                turn_hidden0(j - 1, 1 - p)
                hidden0(p, e, 1, "t_v")
                if not last:
                    pe.wait_ge(S("t_hT"), j)
                    turn0(1 - p, h)
                outputs0(j - 1, 1 - p, before, first)
                return e

            count(1, 4)
            pe.wait_ge(S("t_w"), 16 * 3 * E)
            pe.wait_ge(S("dispatched"), 2)
            turn0(0, 0)
            turn0(1, 0)
            e = expert_of(0)
            pe.wait_ge(S("t_xT"), 1)
            hidden0(0, e, 0, "t_u")
            hidden0(0, e, 1, "t_v")
            e = tile0(1, 1, 1, e, True)
            tile0(2, 0, 1, e, True)
            with pe.Fori(1, TILES0 // 2 - 1) as i:
                e = tile0(2 * i + 1, 1, i + 1)
                tile0(2 * i + 2, 0, i + 1, e)
            e = tile0(TILES0 - 2, 1, TILES0 // 2)
            e = tile0(TILES0 - 1, 0, 0, e, last=True)
            turn_hidden0(TILES0 - 1, 0)
            outputs0(TILES0 - 1, 0, e)

            pe.wait_ge(S("c_weights"), c_loads)

            def second_head(i):
                return attn_stages(S1, i, ("a", B), lambda b: b.xA)[:2]

            def second_layer(i, last=False, behind_values=()):
                turn_output, route = out_stages(B, r1, i)
                if last:
                    ahead = [turn_output, route]
                else:
                    turn, project_k = second_head(i + 1)

                    def keys_and_output():
                        project_k(0)
                        for p in range(2):
                            turn_output(p)
                        project_k(1)

                    ahead = [turn, Both(keys_and_output), route]
                in_turn(attn_stages(S1, i, ("a", B), lambda b: b.xA, behind_values)[2:] + attn_stages(X1, i, ("s", 0), lambda b: b.xB)
                        + ahead)

            in_turn(second_head(0))
            with pe.Fori(0, PAIRS - 1) as i:
                second_layer(i)

            def early():
                count(2, 3)
                pe.wait_ge(S("counts"), 1)

            second_layer(PAIRS - 1, True, [Both(early)])

            def turn1(p, h):
                pe.wait_ge(S(f"e_in{p}"), 16 * (h + 1))
                for k in range(KC):
                    for t in range(ST1):
                        ins = tr(ps[:, k, t * P:(t + 1) * P], experts1[p].x[:, t, k * P:(k + 1) * P], ident[:, :])
                ins.then_inc(S("e_X"), 1)

            def expert1(e, p, h, first=False, last=False):
                b = experts1[p]
                pe.wait_ge(S(f"e_w{p}"), 64 * (h + 1))
                pe.wait_ge(S("e_xT"), e + 1)
                for m in range(KC):
                    for k in range(KC):
                        ins = mm(ps[:, 2 + m, 0:SLOTS1], b.w1[:, k, m * P:(m + 1) * P], b.xT[:, k, :], start=(k == 0), stop=(k == KC - 1))
                    ins.then_inc(S("e_u"), 1)
                if not last:
                    turn1(1 - p, h + p)
                pe.wait_ge(S("e_h"), KC * (e + 1))
                if not first:
                    pe.wait_ge(S("e_ys"), e - 1)
                for t in range(ST1):
                    for m in range(KC):
                        ins = mm(ps[:, 4 + 2 * p + t // 2, (t % 2) * D:(t % 2 + 1) * D], b.hid[:, m, t * P:(t + 1) * P], b.w2[:, m, :],
                                 start=(m == 0), stop=(m == KC - 1))
                ins.then_inc(S("e_y"), 1)

            count(3, 4)
            turn1(0, 0)
            for p in range(2):
                expert1(p, p, 0, True)
            with pe.Fori(1, E // 2 - 1) as i:
                for p in range(2):
                    expert1(2 * i + p, p, i)
            expert1(E - 2, 0, E // 2 - 1)
            expert1(E - 1, 1, E // 2 - 1, last=True)


def kernel(**inputs):
    import concourse.bacc as bacc
    from concourse.bass_utils import run_bass_kernel_spmd
    import ml_dtypes

    a = {k: np.asarray(v) for k, v in inputs.items()}
    bf = ml_dtypes.bfloat16

    def chunk(w):
        return w.reshape(-1, P, w.shape[-1]).transpose(1, 0, 2)

    def cols(v):
        return v.reshape(-1, P).T

    d = {"x": a["x"].reshape(B, NT, P, D), "xT": a["x"].transpose(0, 2, 1).reshape(B, KC, P, L),
         "ctxT": a["ctx_768"].transpose(0, 2, 1)}
    for n, k in (("wq", "Wq"), ("wk", "Wk"), ("wv", "Wv"), ("wg", "Wg"), ("w1", "gk_w1"), ("wo", "Wo")):
        d["a_" + n] = chunk(a["L0_attn_" + k])
    d["a_w2"] = a["L0_attn_gk_w2"]
    d["a_b2"] = cols(a["L0_attn_gk_b2"])
    d["a_gn"] = a["L0_attn_g_norm_w"][None]
    wkv = a["L0_xattn_Wkv"].reshape(H, 2, DH, DC)
    bkv = a["L0_xattn_bkv"].reshape(H, 2, DH)
    layers = {
        "x0": {"wq": a["L0_xattn_Wq"].T, "wk": wkv[:, 0].reshape(D, DC).T, "wv": wkv[:, 1].reshape(D, DC).T,
               "wo": a["L0_xattn_Wo"].T, "bq": a["L0_xattn_bq"], "bk": bkv[:, 0].reshape(D), "bv": bkv[:, 1].reshape(D),
               "bo": a["L0_xattn_bo"]},
        "s1": {n.lower(): a["L1_attn_" + n] for n in ("Wq", "Wk", "Wv", "Wo", "bq", "bk", "bv", "bo")},
        "x1": {n.lower(): a["L1_xattn_" + n] for n in ("Wq", "Wk", "Wv", "Wo", "bq", "bk", "bv", "bo")},
    }
    twice = np.broadcast_to(np.arange(D).reshape(H, 1, DH), (H, 2, DH)).reshape(2 * D)
    for x, w in layers.items():
        for n, t in w.items():
            if n[1] in "qk":
                t = t[..., twice]
            if n[0] == "w":
                d[f"{x}_{n}"] = chunk(t) if t.shape[0] % P == 0 else t
            else:
                d[f"{x}_{n}"] = cols(t) if n in ("bq", "bk") else t[None]
    d["r0"] = chunk(a["L0_ffn_Wg"])
    d["r1"] = chunk(a["L1_ffn_gate_w"].T)
    d["m1_b1"] = a["L1_ffn_b1"].reshape(E, KC, P).transpose(0, 2, 1)
    d["m1_b2"] = a["L1_ffn_b2"].reshape(E, 1, D)
    d["m0_w1"] = a["L0_ffn_W1"].reshape(E, KC, P, FH)
    d["m0_w2"] = a["L0_ffn_W2"].reshape(E, KC, P, FH)
    d["m0_w3"] = a["L0_ffn_W3"].reshape(E, MC, P, D)
    d["m1_w1"] = a["L1_ffn_w1"].transpose(0, 2, 1).reshape(E, KC, P, D)
    d["m1_w2"] = a["L1_ffn_w2"].transpose(0, 2, 1).reshape(E, KC, P, D)
    r = np.arange(P)
    upper = (r[None, :] >= r[:, None]).astype(np.float32)
    d["ident"] = np.eye(P, dtype=np.float32)
    d["identb"] = np.eye(P, dtype=bf)
    d["causal"] = np.stack([upper, upper, np.ones((P, P), np.float32)], 1)
    d["rowmask"] = (r[:, None] // (2 * DH) == np.arange(HC)[None]).astype(np.float32)
    low = (r // DH % 2).astype(np.float32)
    d["lowrow"] = np.stack([low, 1 - 2 * low], 1)
    d["headrow"] = np.broadcast_to((np.arange(3 * H)[:, None] % H == np.arange(H)[None])[:, :, None], (3 * H, H, P)).astype(bf)
    d["winmask"] = np.stack([np.where(r[None, :] > r[:, None], -BIG, 0), np.where(r[None, :] < r[:, None], -BIG, 0)], 1).astype(bf)
    d["tiebreak"] = np.broadcast_to(E - np.arange(E, dtype=np.float32), (P, TILES, E))

    tiles = np.arange(TILES)
    d["scan_reset"] = np.broadcast_to(np.tile(tiles > 0, E).astype(np.float32), (P, E * TILES))
    d["tile_start"] = np.broadcast_to((tiles * P).astype(np.float32), (P, TILES))
    d["tile_no"] = np.broadcast_to(np.arange(TILES0, dtype=np.float32), (P, TILES0))
    d["base1"] = np.broadcast_to(SLOTS1 * np.arange(E, dtype=np.float32), (P, E))
    d["trash"] = (TRASH + 2 * (tiles[None, None] * P + r[:, None, None]) + np.arange(2)[None, :, None]).astype(np.float32)

    nc = bacc.Bacc("TRN2", target_bir_lowering=False, num_devices=1)
    arrays, dram = {}, {}
    for n, t in d.items():
        t = np.ascontiguousarray(t)
        arrays["in_" + n] = t
        dram[n] = nc.dram_tensor("in_" + n, t.shape, mybir.dt.from_np(t.dtype), kind="ExternalInput").ap()
    out = nc.dram_tensor("out_x", (B, NT, P, D), F32, kind="ExternalOutput").ap()
    rows_in = nc.dram_tensor("rows_in", (ROWS, D), F32, kind="Internal").ap()
    rows_out = nc.dram_tensor("rows_out", (TILES0 * P, D), F32, kind="Internal").ap()
    build_program(nc, dram, out, rows_in, rows_out)
    r = run_bass_kernel_spmd(nc, [arrays], core_ids=[0])
    return r.results[0]["out_x"].reshape(B, L, D)
```
